# Optimizing a Trainium2 kernel written in Bass

```python
import numpy as np
import jax
import jax.numpy as jnp

def _softmax(x, axis=-1):
    return jax.nn.softmax(x, axis=axis)

def _gelu(x):
    return jax.nn.gelu(x, approximate=True)

def _silu(x):
    return jax.nn.silu(x)

def _sigmoid(x):
    return jax.nn.sigmoid(x)

def _layernorm(x, axis=-1, eps=1e-05):
    m = jnp.mean(x, axis=axis, keepdims=True)
    v = jnp.var(x, axis=axis, keepdims=True)
    return (x - m) / jnp.sqrt(v + eps)

def _scatter_add(tgt, idx, src, axis=0):
    return tgt.at[idx].add(src)

def _segment_sum(src, seg, n):
    return jax.ops.segment_sum(src, seg, n)
kernel_name = 'mk_xattn_ffn_d4_seqx_r8_5fff9a'

def setup_inputs(seed: int=0):
    np.random.seed(seed)
    _w = jnp.asarray

    def _rec_inputs():
        import jax
        import jax.numpy as jnp
        _rk = jax.random.key(seed)
        x = -0.0002928 + 1 * jax.random.normal(jax.random.fold_in(_rk, 1), (128, 64, 128), jnp.float32)
        _lenS = 64 - jax.random.randint(jax.random.fold_in(_rk, 7), (128,), 0, max(1, 64 // 4) + 1, jnp.int32)
        _lenS2 = 64 - jax.random.randint(jax.random.fold_in(_rk, 8), (128,), 0, max(1, 64 // 4) + 1, jnp.int32)
        _ctx_1024P = jax.random.normal(jax.random.fold_in(_rk, 11), (128, 16, 128), jnp.float32)
        _ctx_1024c = jax.random.dirichlet(jax.random.fold_in(_rk, 511), 0.3 * jnp.ones((16,), jnp.float32), (128, 64))
        _ctx_1024t = jnp.einsum('bsk,bkd->bsd', _ctx_1024c, _ctx_1024P)
        _ctx_1024t = _ctx_1024t * jax.lax.rsqrt(jnp.mean(jnp.square(_ctx_1024t)) + 1e-12) * 0.953939
        ctx_1024 = -1.39393e-06 + 0.999914 * (_ctx_1024t + 0.3 * jax.random.normal(jax.random.fold_in(_rk, 611), (128, 64, 128), jnp.float32))
        _validS = jnp.arange(64)[None, :] < _lenS[:, None]
        _validS2 = jnp.arange(64)[None, :] < _lenS2[:, None]
        _causal = jnp.tril(jnp.ones((64, 64), dtype=bool))
        mask_Bx1xSxS2_ik1 = jnp.where(jnp.broadcast_to(_validS2[:, None, None, :], (128, 1, 64, 64)), 1, 0).astype(jnp.int32)
        mask_1x1xSxS2_if1 = jnp.where(jnp.ones((1, 1, 64, 64), dtype=bool), 1, 0).astype(jnp.int32)
        return (x, ctx_1024, mask_Bx1xSxS2_ik1, mask_1x1xSxS2_if1)
    x, ctx_1024, mask_Bx1xSxS2_ik1, mask_1x1xSxS2_if1 = _rec_inputs()

    def _L0_xattn_setup():
        import jax, jax.numpy as jnp
        import numpy as np
        HEADS = 16
        key = jax.random.key(seed)
        k1, k2, k3, k4 = jax.random.split(key, 4)
        B, T, S, W = (2, 256, 256, 128)
        x = jax.random.normal(k1, (B, T, W), dtype=jnp.float32)
        cond_k = jax.random.normal(k2, (B, S, W), dtype=jnp.float32)
        cond_v = jax.random.normal(k3, (B, S, W), dtype=jnp.float32)
        w_proj = jax.random.normal(k4, (W, W), dtype=jnp.float32) * 0.02
        b_proj = jnp.zeros((W,), dtype=jnp.float32)
        return {'x': x, 'cond_k': cond_k, 'cond_v': cond_v, 'w_proj': w_proj, 'b_proj': b_proj}
    _L0_xattn_all = _L0_xattn_setup()
    _L0_xattn_in = {k: v for k, v in _L0_xattn_all.items() if k in ('w_proj', 'b_proj')}
    del _L0_xattn_all

    def _L0_ffn_setup():
        import jax, jax.numpy as jnp
        import numpy as np
        INT8_MAX = 127.0

        def _absmax_scale(x, axes):
            amax = jnp.max(jnp.abs(x), axis=axes, keepdims=True)
            return jnp.maximum(amax, 1e-12) / INT8_MAX
        key = jax.random.key(seed)
        k1, k2 = jax.random.split(key)
        lhs = jax.random.normal(k1, (4, 1024, 128), dtype=jnp.float32)
        rhs = jax.random.normal(k2, (128, 128), dtype=jnp.float32)
        return {'lhs': lhs, 'rhs': rhs}
    _L0_ffn_all = _L0_ffn_setup()
    _L0_ffn_in = {k: v for k, v in _L0_ffn_all.items() if k in ('rhs',)}
    del _L0_ffn_all

    def _L1_xattn_setup():
        import jax, jax.numpy as jnp
        import numpy as np
        EMBED = 128
        HEADS = 16
        HEAD_DIM = EMBED // HEADS
        B, S = (4, 256)
        key = jax.random.key(seed)
        ks = jax.random.split(key, 9)
        inp = {'values': jax.random.normal(ks[0], (B, S, EMBED), jnp.float32), 'keys': jax.random.normal(ks[1], (B, S, EMBED), jnp.float32), 'queries': jax.random.normal(ks[2], (B, S, EMBED), jnp.float32), 'mask': jax.random.randint(ks[3], (B, 1, S, S), 0, 2, jnp.int32), 'Wv': jax.random.normal(ks[4], (HEAD_DIM, HEAD_DIM), jnp.float32) / np.sqrt(HEAD_DIM), 'Wk': jax.random.normal(ks[5], (HEAD_DIM, HEAD_DIM), jnp.float32) / np.sqrt(HEAD_DIM), 'Wq': jax.random.normal(ks[6], (HEAD_DIM, HEAD_DIM), jnp.float32) / np.sqrt(HEAD_DIM), 'Wo': jax.random.normal(ks[7], (EMBED, EMBED), jnp.float32) / np.sqrt(EMBED), 'bo': jax.random.normal(ks[8], (EMBED,), jnp.float32) * 0.01}
        return inp
    _L1_xattn_all = _L1_xattn_setup()
    _L1_xattn_in = {k: v for k, v in _L1_xattn_all.items() if k in ('Wv', 'Wk', 'Wq', 'Wo', 'bo')}
    del _L1_xattn_all

    def _L1_ffn_setup():
        import jax, jax.numpy as jnp
        import numpy as np
        B, S, D = (4, 256, 128)
        E = 8
        CF = 1
        key = jax.random.key(seed)
        k_x, k_g, k_w, k_b = jax.random.split(key, 4)
        x = jax.random.normal(k_x, (B, S, D), dtype=jnp.float32)
        Wg = jax.random.normal(k_g, (D, E), dtype=jnp.float32) * (1.0 / np.sqrt(D))
        We = jax.random.normal(k_w, (D, D), dtype=jnp.float32) * (1.0 / np.sqrt(D))
        be = jax.random.normal(k_b, (D,), dtype=jnp.float32) * 0.01
        return {'x': x, 'Wg': Wg, 'We': We, 'be': be}
    _L1_ffn_all = _L1_ffn_setup()
    _L1_ffn_in = {k: v for k, v in _L1_ffn_all.items() if k in ('Wg', 'We', 'be')}
    del _L1_ffn_all

    def _L2_xattn_setup():
        import math
        import jax, jax.numpy as jnp
        import numpy as np
        EMBED_DIM = 128
        N_HEADS = 16
        B = 4
        L = 256
        key = jax.random.key(seed)
        ks = jax.random.split(key, 12)
        s = 1.0 / math.sqrt(EMBED_DIM)
        inp = {'q': jax.random.normal(ks[0], (B, L, EMBED_DIM), jnp.float32), 'k': jax.random.normal(ks[1], (B, L, EMBED_DIM), jnp.float32), 'v': jax.random.normal(ks[2], (B, L, EMBED_DIM), jnp.float32), 'mask': jnp.ones((1, 1, L, L), jnp.int32), 'Wq': jax.random.normal(ks[3], (EMBED_DIM, EMBED_DIM), jnp.float32) * s, 'bq': jnp.zeros((EMBED_DIM,), jnp.float32), 'Wk': jax.random.normal(ks[4], (EMBED_DIM, EMBED_DIM), jnp.float32) * s, 'bk': jnp.zeros((EMBED_DIM,), jnp.float32), 'Wv': jax.random.normal(ks[5], (EMBED_DIM, EMBED_DIM), jnp.float32) * s, 'bv': jnp.zeros((EMBED_DIM,), jnp.float32), 'Wo': jax.random.normal(ks[6], (EMBED_DIM, EMBED_DIM), jnp.float32) * s, 'bo': jnp.zeros((EMBED_DIM,), jnp.float32)}
        return inp
    _L2_xattn_all = _L2_xattn_setup()
    _L2_xattn_in = {k: v for k, v in _L2_xattn_all.items() if k in ('Wq', 'bq', 'Wk', 'bk', 'Wv', 'bv', 'Wo', 'bo')}
    del _L2_xattn_all

    def _L2_ffn_setup():
        import jax, jax.numpy as jnp
        import numpy as np
        B, N, D = (4, 256, 128)
        SPARSITY = 0.01
        key = jax.random.key(seed)
        k1, k2, k3 = jax.random.split(key, 3)
        x = jax.random.normal(k1, (B, N, D), dtype=jnp.float32)
        spatial = jax.random.normal(k2, (D, D), dtype=jnp.float32) * 0.02
        freq = jnp.fft.fft(spatial, axis=-1)
        k = int(D * SPARSITY)
        mag = jnp.abs(freq)
        kth = jax.lax.top_k(mag, k)[0][:, -1:]
        w_sparse = jnp.where(mag >= kth, freq, 0.0 + 0j)
        bias = jax.random.normal(k3, (D,), dtype=jnp.float32) * 0.01
        return {'x': x, 'w_freq_real': jnp.real(w_sparse).astype(jnp.float32), 'w_freq_imag': jnp.imag(w_sparse).astype(jnp.float32), 'bias': bias}
    _L2_ffn_all = _L2_ffn_setup()
    _L2_ffn_in = {k: v for k, v in _L2_ffn_all.items() if k in ('w_freq_real', 'w_freq_imag', 'bias')}
    del _L2_ffn_all

    def _L3_xattn_setup():
        import jax, jax.numpy as jnp
        import numpy as np
        EPS = 0.001
        LEAKY_ALPHA = 0.2

        def layer_norm(x, gamma, beta):
            mu = jnp.mean(x, axis=-1, keepdims=True)
            var = jnp.mean(jnp.square(x - mu), axis=-1, keepdims=True)
            return (x - mu) * jax.lax.rsqrt(var + EPS) * gamma + beta

        def attention_head(x_k, x_v, x_q, Wk, Wq, Wv, use_mask):
            K = x_k @ Wk
            V = x_v @ Wv
            Q = x_q @ Wq
            Lq, Lk = (Q.shape[1], K.shape[1])
            score = jnp.einsum('bqd,bkd->bqk', Q, K) / jnp.sqrt(jnp.float32(Lk))
            if use_mask:
                mask = jnp.triu(jnp.full((Lq, Lk), -jnp.inf, dtype=score.dtype), k=1)
                score = score + mask
            return jax.nn.softmax(score, axis=-1) @ V
        key = jax.random.key(seed)
        ks = jax.random.split(key, 12)
        B, S, D = (8, 256, 128)
        inp = {'inputs': jax.random.normal(ks[0], (B, S, D), jnp.float32), 'context_sequence': jax.random.normal(ks[1], (B, S, D), jnp.float32), 'Wk1': jax.random.normal(ks[2], (D, D), jnp.float32) * 0.01, 'Wq1': jax.random.normal(ks[3], (D, D), jnp.float32) * 0.01, 'Wv1': jax.random.normal(ks[4], (D, D), jnp.float32) * 0.01, 'Wk2': jax.random.normal(ks[5], (D, D), jnp.float32) * 0.01, 'Wq2': jax.random.normal(ks[6], (D, D), jnp.float32) * 0.01, 'Wv2': jax.random.normal(ks[7], (D, D), jnp.float32) * 0.01, 'W1': jax.random.normal(ks[8], (D, D), jnp.float32) * (1.0 / np.sqrt(D)), 'b1': jnp.zeros((D,), jnp.float32), 'W2': jax.random.normal(ks[9], (D, D), jnp.float32) * (1.0 / np.sqrt(D)), 'b2': jnp.zeros((D,), jnp.float32), 'gamma': jnp.ones((D,), jnp.float32), 'beta': jnp.zeros((D,), jnp.float32)}
        return inp
    _L3_xattn_all = _L3_xattn_setup()
    _L3_xattn_in = {k: v for k, v in _L3_xattn_all.items() if k in ('Wk1', 'Wq1', 'Wv1', 'Wk2', 'Wq2', 'Wv2', 'W1', 'b1', 'W2', 'b2', 'gamma', 'beta')}
    del _L3_xattn_all

    def _L3_ffn_setup():
        import jax, jax.numpy as jnp
        import numpy as np
        DIM = 128
        DEPTH = 2
        HEADS = 8
        DIM_HEAD = 64
        WINDOW = 64
        INNER = HEADS * DIM_HEAD
        HID = int(DIM * 4 * 2 / 3)
        B, N = (2, 1024)
        QK_SCALE = 8.0

        def shift_token(t):
            t1, t2 = jnp.split(t, 2, axis=-1)
            t2 = jnp.pad(t2, ((0, 0), (1, 0), (0, 0)))[:, :-1]
            return jnp.concatenate([t1, t2], axis=-1)

        def l2norm(t):
            return t / jnp.clip(jnp.linalg.norm(t, axis=-1, keepdims=True), 1e-12)

        def rotate_half(x):
            x1, x2 = jnp.split(x, 2, axis=-1)
            return jnp.concatenate([-x2, x1], axis=-1)

        def rotary_xpos(q, k):
            n = q.shape[-2]
            half_idx = jnp.arange(0, DIM_HEAD, 2, dtype=jnp.float32)
            inv_freq = 1.0 / 10000.0 ** (half_idx / DIM_HEAD)
            t = jnp.arange(n, dtype=jnp.float32)
            freqs = t[:, None] * inv_freq[None, :]
            freqs = jnp.concatenate([freqs, freqs], axis=-1)
            base = (half_idx + 0.4 * DIM_HEAD) / (1.4 * DIM_HEAD)
            power = (t - n // 2) / float(WINDOW // 2)
            scale = base[None, :] ** power[:, None]
            scale = jnp.concatenate([scale, scale], axis=-1)
            cos, sin = (jnp.cos(freqs), jnp.sin(freqs))
            q = q * cos * scale + rotate_half(q) * sin * scale
            k = k * cos / scale + rotate_half(k) * sin / scale
            return (q, k)

        def local_attention(q, k, v):
            b, h, n, d = q.shape
            w = n // WINDOW
            bq = q.reshape(b, h, w, WINDOW, d) * QK_SCALE
            bk = k.reshape(b, h, w, WINDOW, d)
            bv = v.reshape(b, h, w, WINDOW, d)

            def look_around(t):
                p = jnp.pad(t, ((0, 0), (0, 0), (1, 0), (0, 0), (0, 0)))
                return jnp.concatenate([p[:, :, :w], p[:, :, 1:]], axis=3)
            bk, bv = (look_around(bk), look_around(bv))
            bt = jnp.arange(n).reshape(w, WINDOW)
            btp = jnp.pad(bt, ((1, 0), (0, 0)), constant_values=-1)
            btk = jnp.concatenate([btp[:w], btp[1:]], axis=1)
            sim = jnp.einsum('bhwid,bhwjd->bhwij', bq, bk)
            i = bt[:, :, None]
            j = btk[:, None, :]
            mask = (i < j) | (i > j + WINDOW) | (j == -1)
            sim = jnp.where(mask, -jnp.finfo(sim.dtype).max, sim)
            attn = jax.nn.softmax(sim, axis=-1)
            out = jnp.einsum('bhwij,bhwjd->bhwid', attn, bv)
            return out.reshape(b, h, n, d)

        def _layer(x, wqkv, qs, ksc, wo, lg, lb, w1, b1, w2, b2):
            b, n, _ = x.shape
            h = shift_token(x)
            qkv = h @ wqkv
            q, k, v = jnp.split(qkv, 3, axis=-1)
            to_heads = lambda t: t.reshape(b, n, HEADS, DIM_HEAD).transpose(0, 2, 1, 3)
            q, k, v = (to_heads(q), to_heads(k), to_heads(v))
            q = l2norm(q) * qs
            k = l2norm(k) * ksc
            q, k = rotary_xpos(q, k)
            o = local_attention(q, k, v)
            o = o.transpose(0, 2, 1, 3).reshape(b, n, INNER)
            x = x + o @ wo
            h = shift_token(x)
            mu = h.mean(-1, keepdims=True)
            var = h.var(-1, keepdims=True)
            h = (h - mu) / jnp.sqrt(var + 1e-05) * lg + lb
            h = h @ w1 + b1
            a, g = jnp.split(h, 2, axis=-1)
            h = a * jax.nn.gelu(g, approximate=False)
            x = x + h @ w2 + b2
            return x
        key = jax.random.key(seed)
        ks = jax.random.split(key, 6)
        return {'x': jax.random.normal(ks[0], (B, N, DIM), jnp.float32), 'wqkv': jax.random.normal(ks[1], (DEPTH, DIM, 3 * INNER), jnp.float32) * 0.02, 'q_scale': jnp.ones((DEPTH, DIM_HEAD), jnp.float32), 'k_scale': jnp.ones((DEPTH, DIM_HEAD), jnp.float32), 'wo': jax.random.normal(ks[2], (DEPTH, INNER, DIM), jnp.float32) * 0.02, 'ln_g': jnp.ones((DEPTH, DIM), jnp.float32), 'ln_b': jnp.zeros((DEPTH, DIM), jnp.float32), 'w1': jax.random.normal(ks[3], (DEPTH, DIM, 2 * HID), jnp.float32) * 0.02, 'b1': jnp.zeros((DEPTH, 2 * HID), jnp.float32), 'w2': jax.random.normal(ks[4], (DEPTH, HID, DIM), jnp.float32) * 0.02, 'b2': jnp.zeros((DEPTH, DIM), jnp.float32)}
    _L3_ffn_all = _L3_ffn_setup()
    _L3_ffn_in = {k: v for k, v in _L3_ffn_all.items() if k in ('wqkv', 'q_scale', 'k_scale', 'wo', 'ln_g', 'ln_b', 'w1', 'b1', 'w2', 'b2')}
    del _L3_ffn_all
    return {'x': x, 'ctx_1024': ctx_1024, 'mask_Bx1xSxS2_ik1': mask_Bx1xSxS2_ik1, 'mask_1x1xSxS2_if1': mask_1x1xSxS2_if1, 'L0_xattn_w_proj': _L0_xattn_in['w_proj'], 'L0_xattn_b_proj': _L0_xattn_in['b_proj'], 'L0_ffn_rhs': _L0_ffn_in['rhs'], 'L1_xattn_Wv': _L1_xattn_in['Wv'], 'L1_xattn_Wk': _L1_xattn_in['Wk'], 'L1_xattn_Wq': _L1_xattn_in['Wq'], 'L1_xattn_Wo': _L1_xattn_in['Wo'], 'L1_xattn_bo': _L1_xattn_in['bo'], 'L1_ffn_Wg': _L1_ffn_in['Wg'], 'L1_ffn_We': _L1_ffn_in['We'], 'L1_ffn_be': _L1_ffn_in['be'], 'L2_xattn_Wq': _L2_xattn_in['Wq'], 'L2_xattn_bq': _L2_xattn_in['bq'], 'L2_xattn_Wk': _L2_xattn_in['Wk'], 'L2_xattn_bk': _L2_xattn_in['bk'], 'L2_xattn_Wv': _L2_xattn_in['Wv'], 'L2_xattn_bv': _L2_xattn_in['bv'], 'L2_xattn_Wo': _L2_xattn_in['Wo'], 'L2_xattn_bo': _L2_xattn_in['bo'], 'L2_ffn_w_freq_real': _L2_ffn_in['w_freq_real'], 'L2_ffn_w_freq_imag': _L2_ffn_in['w_freq_imag'], 'L2_ffn_bias': _L2_ffn_in['bias'], 'L3_xattn_Wk1': _L3_xattn_in['Wk1'], 'L3_xattn_Wq1': _L3_xattn_in['Wq1'], 'L3_xattn_Wv1': _L3_xattn_in['Wv1'], 'L3_xattn_Wk2': _L3_xattn_in['Wk2'], 'L3_xattn_Wq2': _L3_xattn_in['Wq2'], 'L3_xattn_Wv2': _L3_xattn_in['Wv2'], 'L3_xattn_W1': _L3_xattn_in['W1'], 'L3_xattn_b1': _L3_xattn_in['b1'], 'L3_xattn_W2': _L3_xattn_in['W2'], 'L3_xattn_b2': _L3_xattn_in['b2'], 'L3_xattn_gamma': _L3_xattn_in['gamma'], 'L3_xattn_beta': _L3_xattn_in['beta'], 'L3_ffn_wqkv': _L3_ffn_in['wqkv'], 'L3_ffn_q_scale': _L3_ffn_in['q_scale'], 'L3_ffn_k_scale': _L3_ffn_in['k_scale'], 'L3_ffn_wo': _L3_ffn_in['wo'], 'L3_ffn_ln_g': _L3_ffn_in['ln_g'], 'L3_ffn_ln_b': _L3_ffn_in['ln_b'], 'L3_ffn_w1': _L3_ffn_in['w1'], 'L3_ffn_b1': _L3_ffn_in['b1'], 'L3_ffn_w2': _L3_ffn_in['w2'], 'L3_ffn_b2': _L3_ffn_in['b2']}

def reference(x, ctx_1024, mask_Bx1xSxS2_ik1, mask_1x1xSxS2_if1, L0_xattn_w_proj, L0_xattn_b_proj, L0_ffn_rhs, L1_xattn_Wv, L1_xattn_Wk, L1_xattn_Wq, L1_xattn_Wo, L1_xattn_bo, L1_ffn_Wg, L1_ffn_We, L1_ffn_be, L2_xattn_Wq, L2_xattn_bq, L2_xattn_Wk, L2_xattn_bk, L2_xattn_Wv, L2_xattn_bv, L2_xattn_Wo, L2_xattn_bo, L2_ffn_w_freq_real, L2_ffn_w_freq_imag, L2_ffn_bias, L3_xattn_Wk1, L3_xattn_Wq1, L3_xattn_Wv1, L3_xattn_Wk2, L3_xattn_Wq2, L3_xattn_Wv2, L3_xattn_W1, L3_xattn_b1, L3_xattn_W2, L3_xattn_b2, L3_xattn_gamma, L3_xattn_beta, L3_ffn_wqkv, L3_ffn_q_scale, L3_ffn_k_scale, L3_ffn_wo, L3_ffn_ln_g, L3_ffn_ln_b, L3_ffn_w1, L3_ffn_b1, L3_ffn_w2, L3_ffn_b2):
    import jax
    import jax.numpy as jnp

    def _L0_xattn_ref(x, cond_k, cond_v, w_proj, b_proj):
        import jax, jax.numpy as jnp
        import numpy as np
        HEADS = 16
        B, T, W = x.shape
        S = cond_k.shape[1]
        H = HEADS
        d = W // H
        scale = 1.0 / jnp.sqrt(jnp.sqrt(jnp.float32(d)))
        q = x.reshape(B, T, H, d) * scale
        k = cond_k.reshape(B, S, H, d) * scale
        v = cond_v.reshape(B, S, H, d)
        scores = jnp.einsum('bthd,bshd->bhts', q, k)
        w = jax.nn.softmax(scores.astype(jnp.float32), axis=-1).astype(scores.dtype)
        out = jnp.einsum('bhts,bshd->bthd', w, v).reshape(B, T, W)
        return out @ w_proj.T + b_proj

    def _L0_ffn_ref(lhs, rhs):
        import jax, jax.numpy as jnp
        import numpy as np
        INT8_MAX = 127.0

        def _absmax_scale(x, axes):
            amax = jnp.max(jnp.abs(x), axis=axes, keepdims=True)
            return jnp.maximum(amax, 1e-12) / INT8_MAX
        lhs_scale = _absmax_scale(lhs, (2,))
        rhs_scale = _absmax_scale(rhs, (0,))
        q_lhs = jnp.clip(jnp.round(lhs / lhs_scale), -INT8_MAX, INT8_MAX).astype(jnp.int8)
        q_rhs = jnp.clip(jnp.round(rhs / rhs_scale), -INT8_MAX, INT8_MAX).astype(jnp.int8)
        acc = jax.lax.dot_general(q_lhs, q_rhs, (((2,), (0,)), ((), ())), preferred_element_type=jnp.int32)
        return acc.astype(jnp.float32) * lhs_scale * rhs_scale

    def _L1_xattn_ref(values, keys, queries, mask, Wv, Wk, Wq, Wo, bo):
        import jax, jax.numpy as jnp
        import numpy as np
        EMBED = 128
        HEADS = 16
        HEAD_DIM = EMBED // HEADS
        B, S = (4, 256)
        N, q_len = (queries.shape[0], queries.shape[1])
        v_len, k_len = (values.shape[1], keys.shape[1])
        v = values.reshape(N, v_len, HEADS, HEAD_DIM)
        k = keys.reshape(N, k_len, HEADS, HEAD_DIM)
        q = queries.reshape(N, q_len, HEADS, HEAD_DIM)
        v = jnp.einsum('nlhd,ed->nlhe', v, Wv)
        k = jnp.einsum('nlhd,ed->nlhe', k, Wk)
        q = jnp.einsum('nlhd,ed->nlhe', q, Wq)
        energy = jnp.einsum('nqhd,nkhd->nhqk', q, k)
        energy = jnp.where(mask == 0, jnp.float32(-1e+20), energy)
        attention = jax.nn.softmax(energy / np.sqrt(EMBED).astype(np.float32), axis=3)
        out = jnp.einsum('nhql,nlhd->nqhd', attention, v).reshape(N, q_len, EMBED)
        return out @ Wo.T + bo

    def _L1_ffn_ref(x, Wg, We, be):
        import jax, jax.numpy as jnp
        import numpy as np
        B, S, D = (4, 256, 128)
        E = 8
        CF = 1
        b, s, d = x.shape
        n = b * s
        cap = n // E * CF
        h = x.reshape(n, d)
        router_logits = h @ Wg
        probs = jax.nn.softmax(router_logits, axis=1)
        best = jnp.argmax(probs, axis=1)
        mask = jax.nn.one_hot(best, E, dtype=probs.dtype)
        gate = jnp.sum(probs * mask, axis=1)
        locations = jnp.cumsum(mask, axis=0) - 1.0
        mask = mask * (locations < cap).astype(mask.dtype)
        loc_idx = jnp.sum(locations * mask, axis=1).astype(jnp.int32)
        new_gate = gate[:, None] * mask
        loc_oh = jax.nn.one_hot(loc_idx, cap, dtype=new_gate.dtype)
        combine = new_gate[:, :, None] * loc_oh[:, None, :]
        dispatch = (combine != 0).astype(h.dtype)
        dispatched = jnp.einsum('nec,nd->ecd', dispatch, h).reshape(E * cap, d)
        expert_out = dispatched @ We + be
        out = combine.reshape(n, E * cap) @ expert_out
        return out.reshape(b, s, d)

    def _L2_xattn_ref(q, k, v, mask, Wq, bq, Wk, bk, Wv, bv, Wo, bo):
        import math
        import jax, jax.numpy as jnp
        import numpy as np
        EMBED_DIM = 128
        N_HEADS = 16
        B = 4
        L = 256
        Bq, Lq, C = q.shape
        Bk, Lk, _ = k.shape
        H = N_HEADS
        hd = C // H
        qp = q @ Wq + bq
        kp = k @ Wk + bk
        vp = v @ Wv + bv
        qh = qp.reshape(Bq, Lq, H, hd).transpose(0, 2, 1, 3)
        kh = kp.reshape(Bk, Lk, H, hd).transpose(0, 2, 1, 3)
        vh = vp.reshape(Bk, Lk, H, hd).transpose(0, 2, 1, 3)
        scores = jnp.einsum('bhqd,bhkd->bhqk', qh, kh) / math.sqrt(hd)
        scores = jnp.where(mask == 0, jnp.float32(-10000000000.0), scores)
        attn = jax.nn.softmax(scores, axis=-1)
        x = jnp.einsum('bhqk,bhkd->bhqd', attn, vh)
        x = x.transpose(0, 2, 1, 3).reshape(Bq, Lq, C)
        return x @ Wo + bo

    def _L2_ffn_ref(x, w_freq_real, w_freq_imag, bias):
        import jax, jax.numpy as jnp
        import numpy as np
        B, N, D = (4, 256, 128)
        SPARSITY = 0.01
        w = jax.lax.complex(w_freq_real, w_freq_imag)
        x_freq = jnp.fft.fft(x, axis=-1)
        y_freq = jnp.einsum('bnd,do->bno', x_freq, w)
        y = jnp.real(jnp.fft.ifft(y_freq, axis=-1))
        return y + bias

    def _L3_xattn_ref(inputs, context_sequence, Wk1, Wq1, Wv1, Wk2, Wq2, Wv2, W1, b1, W2, b2, gamma, beta):
        import jax, jax.numpy as jnp
        import numpy as np
        EPS = 0.001
        LEAKY_ALPHA = 0.2

        def layer_norm(x, gamma, beta):
            mu = jnp.mean(x, axis=-1, keepdims=True)
            var = jnp.mean(jnp.square(x - mu), axis=-1, keepdims=True)
            return (x - mu) * jax.lax.rsqrt(var + EPS) * gamma + beta

        def attention_head(x_k, x_v, x_q, Wk, Wq, Wv, use_mask):
            K = x_k @ Wk
            V = x_v @ Wv
            Q = x_q @ Wq
            Lq, Lk = (Q.shape[1], K.shape[1])
            score = jnp.einsum('bqd,bkd->bqk', Q, K) / jnp.sqrt(jnp.float32(Lk))
            if use_mask:
                mask = jnp.triu(jnp.full((Lq, Lk), -jnp.inf, dtype=score.dtype), k=1)
                score = score + mask
            return jax.nn.softmax(score, axis=-1) @ V
        att = attention_head(inputs, inputs, inputs, Wk1, Wq1, Wv1, use_mask=True)
        norm = layer_norm(att + inputs, gamma, beta)
        att2 = attention_head(context_sequence, context_sequence, att, Wk2, Wq2, Wv2, use_mask=False)
        norm2 = layer_norm(att2 + norm, gamma, beta)
        h = jax.nn.leaky_relu(norm2 @ W1 + b1, negative_slope=LEAKY_ALPHA)
        ff = h @ W2 + b2
        norm3 = layer_norm(ff + norm2, gamma, beta)
        return jax.nn.relu(norm3)

    def _L3_ffn_ref(x, wqkv, q_scale, k_scale, wo, ln_g, ln_b, w1, b1, w2, b2):
        import jax, jax.numpy as jnp
        import numpy as np
        DIM = 128
        DEPTH = 2
        HEADS = 8
        DIM_HEAD = 64
        WINDOW = 64
        INNER = HEADS * DIM_HEAD
        HID = int(DIM * 4 * 2 / 3)
        B, N = (2, 1024)
        QK_SCALE = 8.0

        def shift_token(t):
            t1, t2 = jnp.split(t, 2, axis=-1)
            t2 = jnp.pad(t2, ((0, 0), (1, 0), (0, 0)))[:, :-1]
            return jnp.concatenate([t1, t2], axis=-1)

        def l2norm(t):
            return t / jnp.clip(jnp.linalg.norm(t, axis=-1, keepdims=True), 1e-12)

        def rotate_half(x):
            x1, x2 = jnp.split(x, 2, axis=-1)
            return jnp.concatenate([-x2, x1], axis=-1)

        def rotary_xpos(q, k):
            n = q.shape[-2]
            half_idx = jnp.arange(0, DIM_HEAD, 2, dtype=jnp.float32)
            inv_freq = 1.0 / 10000.0 ** (half_idx / DIM_HEAD)
            t = jnp.arange(n, dtype=jnp.float32)
            freqs = t[:, None] * inv_freq[None, :]
            freqs = jnp.concatenate([freqs, freqs], axis=-1)
            base = (half_idx + 0.4 * DIM_HEAD) / (1.4 * DIM_HEAD)
            power = (t - n // 2) / float(WINDOW // 2)
            scale = base[None, :] ** power[:, None]
            scale = jnp.concatenate([scale, scale], axis=-1)
            cos, sin = (jnp.cos(freqs), jnp.sin(freqs))
            q = q * cos * scale + rotate_half(q) * sin * scale
            k = k * cos / scale + rotate_half(k) * sin / scale
            return (q, k)

        def local_attention(q, k, v):
            b, h, n, d = q.shape
            w = n // WINDOW
            bq = q.reshape(b, h, w, WINDOW, d) * QK_SCALE
            bk = k.reshape(b, h, w, WINDOW, d)
            bv = v.reshape(b, h, w, WINDOW, d)

            def look_around(t):
                p = jnp.pad(t, ((0, 0), (0, 0), (1, 0), (0, 0), (0, 0)))
                return jnp.concatenate([p[:, :, :w], p[:, :, 1:]], axis=3)
            bk, bv = (look_around(bk), look_around(bv))
            bt = jnp.arange(n).reshape(w, WINDOW)
            btp = jnp.pad(bt, ((1, 0), (0, 0)), constant_values=-1)
            btk = jnp.concatenate([btp[:w], btp[1:]], axis=1)
            sim = jnp.einsum('bhwid,bhwjd->bhwij', bq, bk)
            i = bt[:, :, None]
            j = btk[:, None, :]
            mask = (i < j) | (i > j + WINDOW) | (j == -1)
            sim = jnp.where(mask, -jnp.finfo(sim.dtype).max, sim)
            attn = jax.nn.softmax(sim, axis=-1)
            out = jnp.einsum('bhwij,bhwjd->bhwid', attn, bv)
            return out.reshape(b, h, n, d)

        def _layer(x, wqkv, qs, ksc, wo, lg, lb, w1, b1, w2, b2):
            b, n, _ = x.shape
            h = shift_token(x)
            qkv = h @ wqkv
            q, k, v = jnp.split(qkv, 3, axis=-1)
            to_heads = lambda t: t.reshape(b, n, HEADS, DIM_HEAD).transpose(0, 2, 1, 3)
            q, k, v = (to_heads(q), to_heads(k), to_heads(v))
            q = l2norm(q) * qs
            k = l2norm(k) * ksc
            q, k = rotary_xpos(q, k)
            o = local_attention(q, k, v)
            o = o.transpose(0, 2, 1, 3).reshape(b, n, INNER)
            x = x + o @ wo
            h = shift_token(x)
            mu = h.mean(-1, keepdims=True)
            var = h.var(-1, keepdims=True)
            h = (h - mu) / jnp.sqrt(var + 1e-05) * lg + lb
            h = h @ w1 + b1
            a, g = jnp.split(h, 2, axis=-1)
            h = a * jax.nn.gelu(g, approximate=False)
            x = x + h @ w2 + b2
            return x
        for l in range(DEPTH):
            x = _layer(x, wqkv[l], q_scale[l], k_scale[l], wo[l], ln_g[l], ln_b[l], w1[l], b1[l], w2[l], b2[l])
        return x
    x = x + _L0_xattn_ref(_layernorm(x, axis=-1), ctx_1024, ctx_1024, L0_xattn_w_proj, L0_xattn_b_proj)
    x = x + _L0_ffn_ref(_layernorm(x, axis=-1), L0_ffn_rhs)
    x = x + _L1_xattn_ref(ctx_1024, ctx_1024, _layernorm(x, axis=-1), mask_Bx1xSxS2_ik1, L1_xattn_Wv, L1_xattn_Wk, L1_xattn_Wq, L1_xattn_Wo, L1_xattn_bo)
    x = x + _L1_ffn_ref(_layernorm(x, axis=-1), L1_ffn_Wg, L1_ffn_We, L1_ffn_be)
    x = x + _L2_xattn_ref(_layernorm(x, axis=-1), ctx_1024, ctx_1024, mask_1x1xSxS2_if1, L2_xattn_Wq, L2_xattn_bq, L2_xattn_Wk, L2_xattn_bk, L2_xattn_Wv, L2_xattn_bv, L2_xattn_Wo, L2_xattn_bo)
    x = x + _L2_ffn_ref(_layernorm(x, axis=-1), L2_ffn_w_freq_real, L2_ffn_w_freq_imag, L2_ffn_bias)
    x = x + _L3_xattn_ref(_layernorm(x, axis=-1), ctx_1024, L3_xattn_Wk1, L3_xattn_Wq1, L3_xattn_Wv1, L3_xattn_Wk2, L3_xattn_Wq2, L3_xattn_Wv2, L3_xattn_W1, L3_xattn_b1, L3_xattn_W2, L3_xattn_b2, L3_xattn_gamma, L3_xattn_beta)
    x = x + _L3_ffn_ref(_layernorm(x, axis=-1), L3_ffn_wqkv, L3_ffn_q_scale, L3_ffn_k_scale, L3_ffn_wo, L3_ffn_ln_g, L3_ffn_ln_b, L3_ffn_w1, L3_ffn_b1, L3_ffn_w2, L3_ffn_b2)
    return x

_drawn_inputs = setup_inputs


def setup_inputs(seed=0):
    import zlib

    import numpy as np

    out = dict(_drawn_inputs(seed))
    spreads = {'L0_xattn_b_proj': (0.0, 0.1),
     'L2_xattn_bq': (0.0, 0.8),
     'L2_xattn_bk': (0.0, 2.0),
     'L2_xattn_bv': (0.0, 0.8),
     'L2_xattn_bo': (0.0, 0.8),
     'L3_xattn_b1': (0.0, 0.8),
     'L3_xattn_b2': (0.0, 0.8),
     'L3_xattn_gamma': (1.0, 0.2),
     'L3_xattn_beta': (0.0, 0.532),
     'L3_ffn_q_scale': (1.0, 0.6),
     'L3_ffn_k_scale': (1.0, 0.6),
     'L3_ffn_ln_g': (1.0, 0.6),
     'L3_ffn_ln_b': (0.0, 0.8),
     'L3_ffn_b1': (0.0, 0.8),
     'L3_ffn_b2': (0.0, 0.68)}
    factors = {'L1_xattn_Wk': 7.935,
     'L1_xattn_Wq': 8.0,
     'L1_xattn_bo': 8.0,
     'L1_ffn_Wg': 4.586,
     'L1_ffn_be': 28.382,
     'L2_xattn_Wq': 2.803,
     'L2_xattn_Wk': 2.764,
     'L2_ffn_bias': 8.0,
     'L3_xattn_Wk1': 8.0,
     'L3_xattn_Wq1': 8.0,
     'L3_xattn_Wv1': 8.0,
     'L3_xattn_Wk2': 45.605,
     'L3_xattn_Wq2': 44.522,
     'L3_xattn_Wv2': 8.0,
     'L3_ffn_wqkv': 8.0,
     'L3_ffn_wo': 8.0,
     'L3_ffn_w1': 8.0,
     'L3_ffn_w2': 8.0}
    for name, (base, spread) in spreads.items():
        noise = np.random.default_rng([zlib.crc32(name.encode()), seed]).standard_normal(out[name].shape)
        drawn = base * np.exp(spread * noise) if base else spread * noise
        out[name] = jnp.asarray(drawn.astype(out[name].dtype))
    for name, factor in factors.items():
        out[name] = (out[name] * factor).astype(out[name].dtype)
    return out
```

```python
import math
from contextlib import ExitStack

import numpy as np
import concourse.bass as bass
from concourse import mybir

F32 = mybir.dt.float32
BF16 = mybir.dt.bfloat16
I32 = mybir.dt.int32
ALU = mybir.AluOpType
ACT = mybir.ActivationFunctionType
AX = mybir.AxisListType.X

BATCH, SEQ, D = 128, 64, 128
P = 128
TILES = BATCH * SEQ // P
T = 4
ROWS = T * P
NB = ROWS // SEQ
GROUPS = TILES // T
LANES = 2
STEPS = GROUPS // LANES
SMALL_HEADS, SMALL_DIM = 16, 8
Q4 = 4
HEADS, HEAD_DIM = 8, 64
INNER = HEADS * HEAD_DIM
DEPTH = 2
HID = int(D * 4 * 2 / 3)
HID_CHUNKS = [(c, min(P, HID - c)) for c in range(0, HID, P)]
NHC = len(HID_CHUNKS)
EXPERTS = 8
CAPACITY = BATCH * SEQ // EXPERTS
MASKED = -1.0e30
ROUND = 12582912.0
INT8_MAX = 127.0
RSQRT_SEED = float(0x5F3759DF)

COLUMNS = ["A2_bq", "A2_bk", "A2_bv", "A3_b1"]
for _l in range(2):
    COLUMNS += [f"F3_{_l}_lg", f"F3_{_l}_lb", f"F3_{_l}_b2"] + [f"F3_{_l}_b1{_k}" for _k in range(2 * NHC)]
LAYOUT = [
    ("columns", len(COLUMNS)),
    ("ident", P), ("ones", P), ("tri", P), ("shift", P), ("causal", SEQ), ("head_cols", Q4),
    ("sum_cols", 2 * 32), ("tie", EXPERTS),
    ("A0_wo", D), ("A0_bo", D),
    ("F0_rhsT", D),
    ("A1_wq", D), ("A1_wk", D), ("A1_wv", D), ("A1_wo", D), ("A1_bo", D),
    ("F1_we", D + EXPERTS), ("F1_be", D),
    ("A2_wq", D), ("A2_wk", D), ("A2_wv", D), ("A2_wo", D), ("A2_bo", D),
    ("F2_wr", D), ("F2_wi", D), ("F2_bias", D), ("dft_cos", D), ("dft_sin", D),
    ("A3_wq1", D), ("A3_wk1", D), ("A3_wv1", D), ("A3_wq2", D), ("A3_wk2", D), ("A3_wv2", D),
    ("A3_w1", D), ("A3_w2", D), ("A3_b2", D), ("A3_gamma", D), ("A3_beta", D),
    ("rope", 4 * HEAD_DIM),
]
for _l in range(2):
    LAYOUT += [(f"F3_{_l}_wqkv", 3 * INNER), (f"F3_{_l}_scales", 4 * HEAD_DIM), (f"F3_{_l}_wo", 4 * D),
               (f"F3_{_l}_w1", 2 * HID), (f"F3_{_l}_w2", NHC * D)]
OFFSET, _at = {}, 0
for _name, _n in LAYOUT:
    OFFSET[_name] = (_at, _n)
    _at += _n
WEIGHT_COLS = _at


def transformer_program(nc, x, ctxT, mask1, mask2, weights, out):
    ctx = ExitStack()
    with ctx:
        def keep(name):
            return ctx.enter_context(nc.semaphore(name))

        stage_sems, stages_run = [], [0]

        def sem(name):
            s = nc.alloc_semaphore(name=f"{name}_{stages_run[0]}")
            stage_sems.append(s)
            return s

        X = ctx.enter_context(nc.sbuf_tensor("X", [P, TILES, D], F32))
        ident = ctx.enter_context(nc.sbuf_tensor("ident", [P, P], F32))
        ident_bf = ctx.enter_context(nc.sbuf_tensor("ident_bf", [P, P], BF16))
        causal_bf = ctx.enter_context(nc.sbuf_tensor("causal_bf", [P, SEQ], BF16))
        columns = ctx.enter_context(nc.sbuf_tensor("columns", [P, len(COLUMNS)], F32))
        mhalf = ctx.enter_context(nc.sbuf_tensor("mhalf", [P, 1], F32))
        st = [ctx.enter_context(nc.sbuf_tensor(f"st{l}", [P, T, 6], F32)) for l in range(LANES)]
        mv = [ctx.enter_context(nc.sbuf_tensor(f"mv{l}", [P, T, 2], F32)) for l in range(LANES)]
        ve = [ctx.enter_context(nc.sbuf_tensor(f"ve{l}", [P, T], F32)) for l in range(LANES)]
        rstd = [ctx.enter_context(nc.sbuf_tensor(f"rstd{l}", [P, T], F32)) for l in range(LANES)]
        h = [ctx.enter_context(nc.sbuf_tensor(f"h{l}", [P, T, D], F32)) for l in range(LANES)]
        hT = [ctx.enter_context(nc.sbuf_tensor(f"hT{l}", [P, ROWS], F32)) for l in range(LANES)]
        PS = ctx.enter_context(nc.psum_tensor("PS", [P, 8, 512], F32))

        def banks(l, k, n=1):
            return PS[:, 4 * l + k:4 * l + k + n, :].rearrange("p b c -> p (b c)")

        loads = [0]
        loaded = keep("loaded")
        ticks = {e: keep(f"tick_{e}") for e in ("pe", "act", "dve", "pool", "sp")}

        def hold(eng, name, s, v):
            eng.wait_ge(s, v)
            eng.sem_inc(ticks[name], 1)

        def load(sp, dst, name, first=0, n=None):
            a, cols = OFFSET[name]
            n = cols if n is None else n
            sp.dma_start(dst, weights[:, a + first:a + first + n]).then_inc(loaded, 16)
            loads[0] += 16

        def column(name, k=None):
            at = COLUMNS.index(name if k is None else f"{name}{k}")
            return columns[:, at:at + 1]

        def rows(t, i, l):
            return t[:, bass.ds(2 * T * i + T * l, T), :]

        def row(t, i, l, k):
            return t[:, bass.ds(2 * T * i + (T * l + k), 1), :].rearrange("p a c -> p (a c)")

        with nc.Block() as block:
            @block.sync
            def _(sp):
                load(sp, ident[:, :], "ident")
                load(sp, columns[:, :], "columns")
                for q in range(4):
                    s = slice(16 * q, 16 * q + 16)
                    sp.dma_start(X[:, s, :], x[128 * 16 * q:128 * 16 * (q + 1), :].rearrange("(t p) c -> p t c", p=P)
                                 ).then_inc(loaded, 16)
                    loads[0] += 16
                load(sp, h[0][:, 0, 0:SEQ], "causal")
                sp.wait_ge(loaded, loads[0])

        base_ready = keep("base_ready")
        with nc.Block() as block:
            @block.vector
            def _(dve):
                nc.vector.memset(mhalf[:, :], -0.5)
                nc.vector.tensor_copy(ident_bf[:, :], ident[:, :])
                nc.vector.tensor_copy(causal_bf[:, :], h[0][:, 0, 0:SEQ]).then_inc(base_ready, 1)
                dve.wait_ge(base_ready, 1)

        ln = {}

        def run_stage(stage):
            ln.update({n: sem("ln_" + n) for n in ("bn", "var", "ve", "rstd", "norm", "hTp", "hT")})
            stage()
            with nc.Block() as block:
                @block.gpsimd
                def _(pool):
                    nc.clear_and_free_semaphores(stage_sems)
            stage_sems.clear()
            stages_run[0] += 1

        def ln_stats(dve, v, l, src):
            for t in range(T):
                op = nc.vector.bn_stats(st[l][:, t, :], src(t))
            op.then_inc(ln["bn"], 1)
            hold(dve, "dve", ln["bn"], v)
            for t in range(T):
                op = nc.vector.bn_aggr(mv[l][:, t, :], st[l][:, t, :])
            op.then_inc(ln["var"], 1)

        def ln_rstd(pool, v, l, eps):
            hold(pool, "pool", ln["var"], v)
            nc.gpsimd.tensor_scalar(ve[l][:, :], mv[l][:, :, 1], 1.0, eps, ALU.mult, ALU.add).then_inc(ln["ve"], 1)
            pool.wait_ge(ln["ve"], v)
            nc.gpsimd.tensor_tensor(rstd[l][:, :], ve[l][:, :], mhalf[:, 0:1].to_broadcast([P, T]), ALU.pow
                                    ).then_inc(ln["rstd"], 1)

        def ln_norm(dve, v, l, src, dst):
            hold(dve, "dve", ln["rstd"], v)
            for t in range(T):
                op = nc.vector.tensor_scalar(dst(t), src(t), mv[l][:, t, 0:1], rstd[l][:, t:t + 1],
                                             ALU.subtract, ALU.mult)
            op.then_inc(ln["norm"], 1)

        def transposes(dst, src):
            for t in range(T):
                op = nc.tensor.transpose(dst[:, t * P:(t + 1) * P], src[:, t, :], ident[:, :])
            return op


        def small_attention(name, project, biased, score_scale, mask_kind):
            sa_mask = sem("sa_mask")
            sa_ready = sem("sa_ready")
            sa_cg = [sem(f"sa_context{l}") for l in range(LANES)]
            sa_lane = [sem(f"sa_lane_done{l}") for l in range(LANES)]
            sa = {n: sem("sa_" + n) for n in (
                "kvp", "kT", "vT", "kb", "vdp", "vb0", "vb1", "qp", "q", "bias", "scores", "max", "sub",
                "exp", "ptp", "pt0", "pt1", "ov", "rec", "o", "out")}
            with ExitStack() as c:
                def sb(n, shape, dt=F32):
                    return c.enter_context(nc.sbuf_tensor(f"{name}_{n}", shape, dt))
                wo = sb("wo", [P, D])
                bo = sb("bo", [P, D])
                head_cols = sb("head_cols", [P, Q4])
                sum_cols = sb("sum_cols", [P, 2, 32])
                if project:
                    wq, wk, wv = sb("wq", [P, D]), sb("wk", [P, D]), sb("wv", [P, D])
                bq, bk, bv = (column(f"{name}_{n}") if biased else 0.0 for n in ("bq", "bk", "bv"))
                lanes = range(LANES)
                xb = [sb(f"xb{l}", [P, T, D]) for l in lanes]
                cg = [sb(f"cg{l}", [P, ROWS]) for l in lanes]
                kT = [sb(f"kT{l}", [P, ROWS]) if project else cg[l] for l in lanes]
                vT = [sb(f"vT{l}", [P, NB, 2, SEQ]) for l in lanes]
                kb = [sb(f"kb{l}", [P, NB, Q4, SEQ]) for l in lanes]
                vb = [sb(f"vb{l}", [P, NB, 8, 32]) for l in lanes]
                qT = [sb(f"qT{l}", [P, ROWS]) if project else hT[l] for l in lanes]
                pr = [sb(f"pr{l}", [P, 2048]) for l in lanes]
                pT = [sb(f"pT{l}", [P, 2, 8, P]) for l in lanes]
                mx = [sb(f"mx{l}", [P, 32]) for l in lanes]
                rec = [sb(f"rec{l}", [P, 256]) for l in lanes]
                oT = [sb(f"oT{l}", [P, ROWS]) for l in lanes]
                if mask_kind == 1:
                    nm = sb("nm", [P, TILES, SEQ], BF16)
                    mraw = sb("mraw", [P, TILES, SEQ], I32)
                elif mask_kind == 2:
                    nm = sb("nm", [P, SEQ], BF16)
                    mraw = sb("mraw", [P, SEQ], I32)

                with nc.Block() as block:
                    @block.sync
                    def _(sp):
                        load(sp, wo[:, :], f"{name}_wo")
                        load(sp, bo[:, :], f"{name}_bo")
                        load(sp, head_cols[:, :], "head_cols")
                        load(sp, sum_cols[:, :, :].rearrange("p a b -> p (a b)"), "sum_cols")
                        if project:
                            for w, n in ((wq, "wq"), (wk, "wk"), (wv, "wv")):
                                load(sp, w[:, :], f"{name}_{n}")
                        if mask_kind == 1:
                            sp.dma_start(mraw[:, :, :], mask1.rearrange("(t p) k -> p t k", p=P)).then_inc(loaded, 16)
                            loads[0] += 16
                        elif mask_kind == 2:
                            for b in range(2):
                                sp.dma_start(mraw[SEQ * b:SEQ * (b + 1), :], mask2).then_inc(loaded, 16)
                                loads[0] += 16
                        sp.wait_ge(loaded, loads[0])

                    @block.gpsimd
                    def _(pool):
                        for l in lanes:
                            op = nc.gpsimd.memset(vb[l][:, :, :, :], 0.0)
                        op.then_inc(sa_ready, 1)
                        pool.wait_ge(sa_ready, 1)

                if mask_kind:
                    with nc.Block() as block:
                        @block.vector
                        def _(dve):
                            m, r = (nm[:, :, :], mraw[:, :, :]) if mask_kind == 1 else (nm[:, :], mraw[:, :])
                            nc.vector.tensor_scalar(m, r, 0.0, MASKED, ALU.is_equal, ALU.mult).then_inc(sa_mask, 1)
                            dve.wait_ge(sa_mask, 1)

                def count_half(i, half, l):
                    return 4 * i + (2 * half + l + 1)

                with nc.Block() as block:
                    @block.sync
                    def _(sp):
                        with sp.Fori(0, STEPS) as i:
                            for l in lanes:
                                hold(sp, "sp", sa_lane[l], i + 1)
                                sp.dma_start(cg[l][:, :], ctxT[:, bass.ds(2 * ROWS * i + ROWS * l, ROWS)]
                                             ).then_inc(sa_cg[l], 16)

                    @block.gpsimd
                    def _(pool):
                        with pool.Fori(0, STEPS) as i:
                            for l in lanes:
                                g = 2 * i + l
                                hold(pool, "pool", sa_lane[l], i + 1)
                                nc.gpsimd.tensor_tensor(xb[l][:, :, :], rows(X, i, l),
                                                        bo[:, :].unsqueeze(1).to_broadcast([P, T, D]), ALU.add
                                                        ).then_inc(sa["bias"], 1)
                            for l in lanes:
                                g = 2 * i + l
                                if project:
                                    hold(pool, "pool", sa["kT"], g + 1)
                                else:
                                    hold(pool, "pool", sa_cg[l], 16 * i + 16)
                                for j in range(Q4):
                                    op = nc.gpsimd.tensor_scalar(
                                        kb[l][:, :, j, :], kT[l][:, :].rearrange("p (b k) -> p b k", b=NB),
                                        bk, head_cols[:, j:j + 1], ALU.add, ALU.mult)
                                op.then_inc(sa["kb"], 1)
                                ln_rstd(pool, 2 * i + l + 1, l, 1e-5)

                    @block.vector
                    def _(dve):
                        for lane in sa_lane:
                            dve.sem_inc(lane, 1)
                        with dve.Fori(0, STEPS) as i:
                            for l in lanes:
                                hold(dve, "dve", sa_lane[l], i + 1)
                                ln_stats(dve, 2 * i + l + 1, l, lambda t: row(X, i, l, t))
                            for l in lanes:
                                ln_norm(dve, 2 * i + l + 1, l, lambda t: row(X, i, l, t), lambda t: h[l][:, t, :])
                            for l in lanes:
                                g = 2 * i + l
                                hold(dve, "dve", sa["vdp"], g + 1)
                                for par in range(2):
                                    src = banks(l, 2, 2)[SEQ:P, :].rearrange("p (n q d) -> p n q d", q=4, d=8)[:, :, 2 * par + 1, :]
                                    dst = vb[l][SEQ:P, :, :, :].rearrange("p b t c -> p (b t c)").rearrange(
                                        "p (n q c) -> p n q c", q=2, c=32)[:, :, par, 8 * (2 * par + 1):8 * (2 * par + 2)]
                                    op = nc.vector.tensor_copy(dst, src)
                                op.then_inc(sa["vb1"], 1)
                            for half in range(2):
                                for l in lanes:
                                    v = count_half(i, half, l)
                                    S = banks(l, 0, 4)
                                    dve.wait_ge(sa["scores"], v)
                                    nc.vector.tensor_reduce(mx[l][:, :], S.rearrange("p (n k) -> p n k", k=SEQ),
                                                            op=ALU.max, axis=AX).then_inc(sa["max"], 1)
                                    dve.wait_ge(sa["max"], v)
                                    nc.vector.tensor_tensor(pr[l][:, :].rearrange("p (n k) -> p n k", k=SEQ),
                                                            S.rearrange("p (n k) -> p n k", k=SEQ),
                                                            mx[l][:, :].unsqueeze(2).to_broadcast([P, 32, SEQ]),
                                                            ALU.subtract).then_inc(sa["sub"], 1)
                                for l in lanes:
                                    v = count_half(i, half, l)
                                    hold(dve, "dve", sa["ptp"], v)
                                    nc.vector.tensor_copy(pT[l][:, 1, :, :].rearrange("p t q -> p (t q)"),
                                                          banks(l, 2, 2)).then_inc(sa["pt1"], 1)
                                for l in lanes:
                                    v = count_half(i, half, l)
                                    dve.wait_ge(sa["ov"], v)
                                    nc.vector.reciprocal(rec[l][:, :], banks(l, 1)[:, 0:256]).then_inc(sa["rec"], 1)
                                    dve.wait_ge(sa["rec"], v)
                                    nc.vector.tensor_tensor(oT[l][:, 256 * half:256 * half + 256], banks(l, 0)[:, 0:256],
                                                            rec[l][:, :], ALU.mult).then_inc(sa["o"], 1)
                            for l in lanes:
                                g = 2 * i + l
                                hold(dve, "dve", sa["out"], g + 1)
                                nc.vector.tensor_tensor(rows(X, i, l), banks(l, 2).rearrange("p (t c) -> p t c", t=T),
                                                        xb[l][:, :, :], ALU.add).then_inc(sa_lane[l], 1)

                    @block.scalar
                    def _(act):
                        with act.Fori(0, STEPS) as i:
                            for l in lanes:
                                g = 2 * i + l
                                if project:
                                    act.wait_ge(sa["kvp"], g + 1)
                                    nc.scalar.activation(kT[l][:, :], banks(l, 1), ACT.Copy).then_inc(sa["kT"], 1)
                                    nc.scalar.activation(vT[l][:, :, :, :],
                                                         banks(l, 2).rearrange("p (b k) -> p b k", b=NB).unsqueeze(2)
                                                         .to_broadcast([P, NB, 2, SEQ]),
                                                         ACT.Identity, bias=bv).then_inc(sa["vT"], 1)
                                else:
                                    act.wait_ge(sa_cg[l], 16 * i + 16)
                                    nc.scalar.activation(vT[l][:, :, :, :],
                                                         cg[l][:, :].rearrange("p (b k) -> p b k", b=NB).unsqueeze(2)
                                                         .to_broadcast([P, NB, 2, SEQ]), ACT.Copy).then_inc(sa["vT"], 1)
                            for l in lanes:
                                g = 2 * i + l
                                act.wait_ge(ln["hTp"], 2 * i + l + 1)
                                nc.scalar.activation(hT[l][:, :], banks(l, 0), ACT.Copy).then_inc(ln["hT"], 1)
                                act.wait_ge(sa["vdp"], g + 1)
                                for par in range(2):
                                    src = banks(l, 2, 2)[0:SEQ, :].rearrange("p (n q d) -> p n q d", q=4, d=8)[:, :, 2 * par, :]
                                    dst = vb[l][0:SEQ, :, :, :].rearrange("p b t c -> p (b t c)").rearrange(
                                        "p (n q c) -> p n q c", q=2, c=32)[:, :, par, 16 * par:16 * par + 8]
                                    op = nc.scalar.activation(dst, src, ACT.Copy)
                                op.then_inc(sa["vb0"], 1)
                            if project:
                                for l in lanes:
                                    g = 2 * i + l
                                    act.wait_ge(sa["qp"], g + 1)
                                    nc.scalar.activation(qT[l][:, :], banks(l, 1), ACT.Identity, bias=bq
                                                         ).then_inc(sa["q"], 1)
                            for half in range(2):
                                for l in lanes:
                                    v = count_half(i, half, l)
                                    act.wait_ge(sa["sub"], v)
                                    nc.scalar.activation(pr[l][:, :], pr[l][:, :], ACT.Exp, scale=score_scale
                                                         ).then_inc(sa["exp"], 1)
                                for l in lanes:
                                    v = count_half(i, half, l)
                                    act.wait_ge(sa["ptp"], v)
                                    nc.scalar.activation(pT[l][:, 0, :, :].rearrange("p t q -> p (t q)"),
                                                         banks(l, 0, 2), ACT.Copy).then_inc(sa["pt0"], 1)

                    @block.tensor
                    def _(pe):
                        with pe.Fori(0, STEPS) as i:
                            for l in lanes:
                                g = 2 * i + l
                                if project:
                                    pe.wait_ge(sa_cg[l], 16 * i + 16)
                                    nc.tensor.matmul(banks(l, 1), wk[:, :], cg[l][:, :], start=True, stop=True)
                                    nc.tensor.matmul(banks(l, 2), wv[:, :], cg[l][:, :], start=True, stop=True
                                                     ).then_inc(sa["kvp"], 1)
                            for l in lanes:
                                g = 2 * i + l
                                hold(pe, "pe", sa["vT"], g + 1)
                                for b in range(NB):
                                    op = nc.tensor.transpose(banks(l, 2, 2)[:, b * P:(b + 1) * P],
                                                             vT[l][:, b, :, :].rearrange("p a k -> p (a k)"), ident[:, :])
                                op.then_inc(sa["vdp"], 1)
                                pe.wait_ge(ln["norm"], 2 * i + l + 1)
                                transposes(banks(l, 0), h[l]).then_inc(ln["hTp"], 1)
                            if project:
                                for l in lanes:
                                    g = 2 * i + l
                                    pe.wait_ge(ln["hT"], 2 * i + l + 1)
                                    nc.tensor.matmul(banks(l, 1), wq[:, :], hT[l][:, :], start=True, stop=True
                                                     ).then_inc(sa["qp"], 1)
                            for half in range(2):
                                for l in lanes:
                                    g = 2 * i + l
                                    if half == 0:
                                        hold(pe, "pe", sa["q"] if project else ln["hT"],
                                             g + 1 if project else 2 * i + l + 1)
                                        hold(pe, "pe", sa["kb"], g + 1)
                                        hold(pe, "pe", sa["vb0"], g + 1)
                                        hold(pe, "pe", sa["vb1"], g + 1)
                                    else:
                                        hold(pe, "pe", sa["o"], count_half(i, 0, l))
                                    for r in range(Q4):
                                        bank = banks(l, r).rearrange("p (t n k) -> p t n k", t=2, n=Q4)
                                        if mask_kind:
                                            if mask_kind == 1:
                                                m = nm[:, bass.ds(2 * T * i + (T * l + 2 * half), 2), :].unsqueeze(2)
                                            else:
                                                m = nm[:, :].unsqueeze(1).unsqueeze(1)
                                            nc.tensor.matmul(bank, ident_bf[:, :], m.to_broadcast([P, 2, Q4, SEQ]),
                                                             start=True, stop=False, skip_group_check=True)
                                    for t in range(2):
                                        for r in range(Q4):
                                            bank = banks(l, r).rearrange("p (t c) -> p t c", t=2)
                                            for b in range(2):
                                                seq = 4 * half + 2 * t + b
                                                op = nc.tensor.matmul(
                                                    bank[SEQ * b:SEQ * (b + 1), t, :],
                                                    qT[l][32 * r:32 * r + 32, SEQ * seq:SEQ * (seq + 1)],
                                                    kb[l][32 * r:32 * r + 32, seq, :, :].rearrange("p n k -> p (n k)"),
                                                    start=(not mask_kind and t == 0), stop=True, skip_group_check=True)
                                    op.then_inc(sa["scores"], 1)
                                for l in lanes:
                                    v = count_half(i, half, l)
                                    pe.wait_ge(sa["exp"], v)
                                    for t in range(2):
                                        for pair in range(8):
                                            op = nc.tensor.transpose(
                                                banks(l, 0, 4)[:, (8 * t + pair) * P:(8 * t + pair + 1) * P],
                                                pr[l][:, :].rearrange("p (r t m c) -> p r t m c", r=Q4, t=2, m=2)[
                                                    :, pair // 2, t, pair % 2, :], ident[:, :])
                                    op.then_inc(sa["ptp"], 1)
                                for l in lanes:
                                    v = count_half(i, half, l)
                                    hold(pe, "pe", sa["pt0"], v)
                                    hold(pe, "pe", sa["pt1"], v)
                                    for t in range(2):
                                        for b in range(2):
                                            seq = 4 * half + 2 * t + b
                                            for m in range(2):
                                                for r in range(Q4):
                                                    nc.tensor.matmul(
                                                        banks(l, 0)[32 * r:32 * r + 32, t * P + b * SEQ:t * P + (b + 1) * SEQ],
                                                        vb[l][:, seq, 2 * r + m, :],
                                                        pT[l][:, t, 2 * r + m, b * SEQ:(b + 1) * SEQ],
                                                        start=(m == 0), stop=(m == 1))
                                        for m in range(2):
                                            for r in range(Q4):
                                                op = nc.tensor.matmul(
                                                    banks(l, 1)[32 * r:32 * r + 32, t * P:(t + 1) * P], sum_cols[:, m, :],
                                                    pT[l][:, t, 2 * r + m, :], start=(m == 0), stop=(m == 1))
                                    op.then_inc(sa["ov"], 1)
                            for l in lanes:
                                g = 2 * i + l
                                pe.wait_ge(sa["o"], count_half(i, 1, l))
                                for t in range(T):
                                    op = nc.tensor.matmul(banks(l, 2)[:, t * P:(t + 1) * P], oT[l][:, t * P:(t + 1) * P],
                                                          wo[:, :], start=True, stop=True)
                                op.then_inc(sa["out"], 1)


        def int8_ffn():
            i8_lane = [sem(f"i8_lane_done{l}") for l in range(LANES)]
            i8 = {n: sem("i8_" + n) for n in ("w", "amax", "scale", "rec", "round", "clip", "q", "qTp", "qT", "acc", "tmp")}
            lanes = range(LANES)
            with ExitStack() as c:
                def sb(n, shape, dt=F32):
                    return c.enter_context(nc.sbuf_tensor(f"i8_{n}", shape, dt))
                rhsT = sb("rhsT", [P, D])
                ones = sb("ones", [P, P])
                ws, wr = sb("ws", [P, 1]), sb("wr", [P, 1])
                wdiag = sb("wdiag", [P, P])
                wqf = sb("wqf", [P, D])
                wqT = sb("wqT", [P, D], BF16)
                wq = sb("wq", [P, D], BF16)
                wscale = sb("wscale", [P, D])
                am = [sb(f"am{l}", [P, T]) for l in lanes]
                sc = [sb(f"sc{l}", [P, T]) for l in lanes]
                rc = [sb(f"rc{l}", [P, T]) for l in lanes]
                qr = [sb(f"qr{l}", [P, T, D]) for l in lanes]
                qb = [sb(f"qb{l}", [P, T, D], BF16) for l in lanes]
                qT = [sb(f"qT{l}", [P, ROWS], BF16) for l in lanes]
                tmp = [sb(f"tmp{l}", [P, T, D]) for l in lanes]
                with nc.Block() as block:
                    @block.sync
                    def _(sp):
                        load(sp, rhsT[:, :], "F0_rhsT")
                        load(sp, ones[:, :], "ones")
                        sp.wait_ge(loaded, loads[0])

                def bf(ap):
                    return ap.bitcast(BF16)

                with nc.Block() as block:
                    @block.vector
                    def _(dve):
                        nc.vector.tensor_reduce(ws[:, :], rhsT[:, :], op=ALU.max, axis=AX, apply_absolute_value=True
                                                ).then_inc(i8["w"], 1)
                        dve.wait_ge(i8["w"], 1)
                        nc.vector.tensor_scalar(ws[:, :], ws[:, :], 1e-12, 1.0 / INT8_MAX, ALU.max, ALU.mult
                                                ).then_inc(i8["w"], 1)
                        dve.wait_ge(i8["w"], 2)
                        nc.vector.reciprocal(wr[:, :], ws[:, :])
                        nc.vector.tensor_scalar(wdiag[:, :], ident[:, :], ws[:, 0:1], None, ALU.mult).then_inc(i8["w"], 1)
                        dve.wait_ge(i8["w"], 3)
                        nc.vector.tensor_scalar(wqf[:, :], rhsT[:, :], wr[:, 0:1], ROUND, ALU.mult, ALU.add
                                                ).then_inc(i8["w"], 1)
                        dve.wait_ge(i8["w"], 4)
                        nc.vector.tensor_scalar(wqf[:, :], wqf[:, :], ROUND + INT8_MAX, ROUND - INT8_MAX, ALU.min, ALU.max
                                                ).then_inc(i8["w"], 1)
                        dve.wait_ge(i8["w"], 5)
                        nc.vector.tensor_scalar(wqT[:, :], wqf[:, :], ROUND, None, ALU.subtract).then_inc(i8["w"], 1)
                        dve.wait_ge(i8["w"], 8)
                        nc.vector.tensor_copy(wq[:, :], bf(PS[:, 0, 0:64]))
                        nc.vector.tensor_copy(wscale[:, :], PS[:, 1, 0:D]).then_inc(i8["w"], 1)
                        dve.wait_ge(i8["w"], 9)

                    @block.tensor
                    def _(pe):
                        pe.wait_ge(i8["w"], 6)
                        nc.tensor.transpose(bf(PS[:, 0, 0:64]), wqT[:, :], ident_bf[:, :]).then_inc(i8["w"], 1)
                        nc.tensor.matmul(PS[:, 1, 0:D], ones[:, :], wdiag[:, :], start=True, stop=True
                                         ).then_inc(i8["w"], 1)

                with nc.Block() as block:
                    @block.gpsimd
                    def _(pool):
                        with pool.Fori(0, STEPS) as i:
                            for l in lanes:
                                ln_rstd(pool, 2 * i + l + 1, l, 1e-5)

                    @block.vector
                    def _(dve):
                        for lane in i8_lane:
                            dve.sem_inc(lane, 1)
                        with dve.Fori(0, STEPS) as i:
                            for l in lanes:
                                hold(dve, "dve", i8_lane[l], i + 1)
                                ln_stats(dve, 2 * i + l + 1, l, lambda t: row(X, i, l, t))
                            for l in lanes:
                                g = 2 * i + l
                                ln_norm(dve, g + 1, l, lambda t: row(X, i, l, t), lambda t: h[l][:, t, :])
                                dve.wait_ge(ln["norm"], g + 1)
                                nc.vector.tensor_reduce(am[l][:, :], h[l][:, :, :], op=ALU.max, axis=AX,
                                                        apply_absolute_value=True).then_inc(i8["amax"], 1)
                                dve.wait_ge(i8["amax"], g + 1)
                                nc.vector.tensor_scalar(sc[l][:, :], am[l][:, :], 1e-12, 1.0 / INT8_MAX, ALU.max, ALU.mult
                                                        ).then_inc(i8["scale"], 1)
                                dve.wait_ge(i8["scale"], g + 1)
                                nc.vector.reciprocal(rc[l][:, :], sc[l][:, :]).then_inc(i8["rec"], 1)
                                dve.wait_ge(i8["rec"], g + 1)
                                for t in range(T):
                                    op = nc.vector.tensor_scalar(qr[l][:, t, :], h[l][:, t, :], rc[l][:, t:t + 1], ROUND,
                                                                 ALU.mult, ALU.add)
                                op.then_inc(i8["round"], 1)
                                dve.wait_ge(i8["round"], g + 1)
                                nc.vector.tensor_scalar(qr[l][:, :, :], qr[l][:, :, :], ROUND + INT8_MAX, ROUND - INT8_MAX,
                                                        ALU.min, ALU.max).then_inc(i8["clip"], 1)
                                dve.wait_ge(i8["clip"], g + 1)
                                nc.vector.tensor_scalar(qb[l][:, :, :], qr[l][:, :, :], ROUND, None, ALU.subtract
                                                        ).then_inc(i8["q"], 1)
                            for l in lanes:
                                g = 2 * i + l
                                dve.wait_ge(i8["acc"], g + 1)
                                for t in range(T):
                                    op = nc.vector.scalar_tensor_tensor(tmp[l][:, t, :], banks(l, 1)[:, t * P:(t + 1) * P],
                                                                        sc[l][:, t:t + 1], wscale[:, :], ALU.mult, ALU.mult)
                                op.then_inc(i8["tmp"], 1)
                                hold(dve, "dve", i8["tmp"], g + 1)
                                nc.vector.tensor_tensor(rows(X, i, l), rows(X, i, l), tmp[l][:, :, :], ALU.add
                                                        ).then_inc(i8_lane[l], 1)

                    @block.scalar
                    def _(act):
                        with act.Fori(0, STEPS) as i:
                            for l in lanes:
                                act.wait_ge(i8["qTp"], 2 * i + l + 1)
                                nc.scalar.activation(qT[l][:, :], bf(banks(l, 0)[:, 0:256]), ACT.Copy
                                                     ).then_inc(i8["qT"], 1)

                    @block.tensor
                    def _(pe):
                        with pe.Fori(0, STEPS) as i:
                            for l in lanes:
                                pe.wait_ge(i8["q"], 2 * i + l + 1)
                                for t in range(T):
                                    op = nc.tensor.transpose(bf(banks(l, 0)[:, 64 * t:64 * t + 64]), qb[l][:, t, :],
                                                             ident_bf[:, :])
                                op.then_inc(i8["qTp"], 1)
                            for l in lanes:
                                pe.wait_ge(i8["qT"], 2 * i + l + 1)
                                for t in range(T):
                                    op = nc.tensor.matmul(banks(l, 1)[:, t * P:(t + 1) * P], qT[l][:, t * P:(t + 1) * P],
                                                          wq[:, :], start=True, stop=True)
                                op.then_inc(i8["acc"], 1)


        def routed_ffn():
            mo_lane = [sem(f"mo_lane_done{l}") for l in range(LANES)]
            mo = {n: sem("mo_" + n) for n in ("lin", "lm", "ls", "ex", "den", "eq", "tie", "tm", "oh", "ohf", "pre", "pos",
                                              "run", "fit", "keep", "kp", "cf", "lt", "zero")}
            lanes = range(LANES)
            E = EXPERTS
            with ExitStack() as c:
                def sb(n, shape, dt=F32):
                    return c.enter_context(nc.sbuf_tensor(f"mo_{n}", shape, dt))
                we = sb("we", [P, D + E])
                be = sb("be", [P, D])
                tie = sb("tie", [P, E])
                trif, onesf = sb("trif", [P, P]), sb("onesf", [P, P])
                tri, ones = sb("tri", [P, P], BF16), sb("ones", [P, P], BF16)
                run = sb("run", [P, LANES, T, E])
                lm = [sb(f"lm{l}", [P, T]) for l in lanes]
                ls = [sb(f"ls{l}", [P, T, E]) for l in lanes]
                ex = [sb(f"ex{l}", [P, T, E]) for l in lanes]
                den = [sb(f"den{l}", [P, T]) for l in lanes]
                gate = [sb(f"gate{l}", [P, T]) for l in lanes]
                eq = [sb(f"eq{l}", [P, T, E]) for l in lanes]
                tm = [sb(f"tm{l}", [P, T]) for l in lanes]
                oh = [sb(f"oh{l}", [P, T, E], BF16) for l in lanes]
                pos = [sb(f"pos{l}", [P, T, E]) for l in lanes]
                kp = [sb(f"kp{l}", [P, T]) for l in lanes]
                cf = [sb(f"cf{l}", [P, T]) for l in lanes]
                lt = [sb(f"lt{l}", [P, T, D]) for l in lanes]
                with nc.Block() as block:
                    @block.sync
                    def _(sp):
                        load(sp, we[:, :], "F1_we")
                        load(sp, be[:, :], "F1_be")
                        load(sp, tie[:, :], "tie")
                        load(sp, trif[:, :], "tri")
                        load(sp, onesf[:, :], "ones")
                        sp.wait_ge(loaded, loads[0])
                with nc.Block() as block:
                    @block.vector
                    def _(dve):
                        nc.vector.tensor_copy(tri[:, :], trif[:, :])
                        nc.vector.tensor_copy(ones[:, :], onesf[:, :])
                        nc.vector.memset(run[:, :, :, :], 0.0).then_inc(mo["zero"], 1)
                        dve.wait_ge(mo["zero"], 1)

                def lin(l):
                    return banks(l, 1, 2).rearrange("p (b c) -> p b c", b=2)[:, :, 0:2 * (D + E)].rearrange(
                        "p b (t c) -> p b t c", t=2)

                def halves(ap):
                    return ap.rearrange("p (b t) c -> p b t c", b=2)

                def over(ap):
                    return ap.unsqueeze(2).to_broadcast([P, T, E])

                with nc.Block() as block:
                    @block.gpsimd
                    def _(pool):
                        with pool.Fori(0, STEPS) as i:
                            for l in lanes:
                                ln_rstd(pool, 2 * i + l + 1, l, 1e-5)

                    @block.vector
                    def _(dve):
                        for lane in mo_lane:
                            dve.sem_inc(lane, 1)
                        with dve.Fori(0, STEPS) as i:
                            for l in lanes:
                                hold(dve, "dve", mo_lane[l], i + 1)
                                ln_stats(dve, 2 * i + l + 1, l, lambda t: row(X, i, l, t))
                            for l in lanes:
                                ln_norm(dve, 2 * i + l + 1, l, lambda t: row(X, i, l, t), lambda t: h[l][:, t, :])
                            for l in lanes:
                                g = 2 * i + l
                                dve.wait_ge(mo["lin"], g + 1)
                                nc.vector.tensor_reduce(lm[l][:, :].rearrange("p (b t) -> p b t", b=2), lin(l)[:, :, :, D:D + E],
                                                        op=ALU.max, axis=AX).then_inc(mo["lm"], 1)
                                nc.vector.tensor_tensor(lt[l][:, :, :].rearrange("p (b t) c -> p b t c", b=2),
                                                        lin(l)[:, :, :, 0:D],
                                                        be[:, :].unsqueeze(1).unsqueeze(1).to_broadcast([P, 2, 2, D]),
                                                        ALU.add).then_inc(mo["lt"], 1)
                                dve.wait_ge(mo["lm"], g + 1)
                                nc.vector.tensor_tensor(halves(ls[l][:, :, :]), lin(l)[:, :, :, D:D + E],
                                                        halves(over(lm[l][:, :])), ALU.subtract).then_inc(mo["ls"], 1)
                                dve.wait_ge(mo["ls"], g + 1)
                                nc.vector.tensor_scalar(eq[l][:, :, :], ls[l][:, :, :], 0.0, None, ALU.is_equal
                                                        ).then_inc(mo["eq"], 1)
                                dve.wait_ge(mo["eq"], g + 1)
                                nc.vector.tensor_tensor(eq[l][:, :, :], eq[l][:, :, :],
                                                        tie[:, :].unsqueeze(1).to_broadcast([P, T, E]), ALU.mult
                                                        ).then_inc(mo["tie"], 1)
                                dve.wait_ge(mo["tie"], g + 1)
                                nc.vector.tensor_reduce(tm[l][:, :], eq[l][:, :, :], op=ALU.max, axis=AX
                                                        ).then_inc(mo["tm"], 1)
                                dve.wait_ge(mo["tm"], g + 1)
                                nc.vector.tensor_tensor(oh[l][:, :, :], eq[l][:, :, :], over(tm[l][:, :]), ALU.is_equal
                                                        ).then_inc(mo["oh"], 1)
                            for l in lanes:
                                g = 2 * i + l
                                dve.wait_ge(mo["ex"], g + 1)
                                nc.vector.tensor_reduce(den[l][:, :], ex[l][:, :, :], op=ALU.add, axis=AX
                                                        ).then_inc(mo["den"], 1)
                                dve.wait_ge(mo["den"], g + 1)
                                nc.vector.reciprocal(gate[l][:, :], den[l][:, :])
                                dve.wait_ge(mo["pre"], g + 1)
                                total = banks(l, 3)[:, T * E:2 * T * E].rearrange("p (t e) -> p t e", t=T)
                                for t in range(T):
                                    nxt = run[:, l, t + 1, :] if t < T - 1 else run[:, 1 - l, 0, :]
                                    nc.vector.tensor_tensor(nxt, run[:, l, t, :], total[:, t, :], ALU.add
                                                            ).then_inc(mo["run"], 1)
                                    dve.wait_ge(mo["run"], T * g + t + 1)
                                nc.vector.tensor_tensor(pos[l][:, :, :], run[:, l, :, :],
                                                        banks(l, 3)[:, 0:T * E].rearrange("p (t e) -> p t e", t=T), ALU.add
                                                        ).then_inc(mo["pos"], 1)
                                dve.wait_ge(mo["pos"], g + 1)
                                nc.vector.tensor_scalar(pos[l][:, :, :], pos[l][:, :, :], float(CAPACITY), None, ALU.is_le
                                                        ).then_inc(mo["fit"], 1)
                                dve.wait_ge(mo["fit"], g + 1)
                                nc.vector.tensor_tensor(pos[l][:, :, :], pos[l][:, :, :], oh[l][:, :, :], ALU.mult
                                                        ).then_inc(mo["keep"], 1)
                                dve.wait_ge(mo["keep"], g + 1)
                                nc.vector.tensor_reduce(kp[l][:, :], pos[l][:, :, :], op=ALU.add, axis=AX
                                                        ).then_inc(mo["kp"], 1)
                                dve.wait_ge(mo["kp"], g + 1)
                                nc.vector.tensor_tensor(cf[l][:, :], kp[l][:, :], gate[l][:, :], ALU.mult
                                                        ).then_inc(mo["cf"], 1)
                                hold(dve, "dve", mo["cf"], g + 1)
                                for t in range(T):
                                    op = nc.vector.scalar_tensor_tensor(row(X, i, l, t), lt[l][:, t, :], cf[l][:, t:t + 1],
                                                                        row(X, i, l, t), ALU.mult, ALU.add)
                                op.then_inc(mo_lane[l], 1)

                    @block.scalar
                    def _(act):
                        with act.Fori(0, STEPS) as i:
                            for l in lanes:
                                act.wait_ge(ln["hTp"], 2 * i + l + 1)
                                nc.scalar.activation(hT[l][:, :], banks(l, 0), ACT.Copy).then_inc(ln["hT"], 1)
                            for l in lanes:
                                act.wait_ge(mo["ls"], 2 * i + l + 1)
                                nc.scalar.activation(ex[l][:, :, :], ls[l][:, :, :], ACT.Exp).then_inc(mo["ex"], 1)

                    @block.tensor
                    def _(pe):
                        with pe.Fori(0, STEPS) as i:
                            for l in lanes:
                                pe.wait_ge(ln["norm"], 2 * i + l + 1)
                                transposes(banks(l, 0), h[l]).then_inc(ln["hTp"], 1)
                            for l in lanes:
                                pe.wait_ge(ln["hT"], 2 * i + l + 1)
                                for t in range(T):
                                    op = nc.tensor.matmul(lin(l)[:, t // 2, t % 2, :], hT[l][:, t * P:(t + 1) * P], we[:, :],
                                                          start=True, stop=True)
                                op.then_inc(mo["lin"], 1)
                            for l in lanes:
                                pe.wait_ge(mo["oh"], 2 * i + l + 1)
                                flat = oh[l][:, :, :].rearrange("p t e -> p (t e)")
                                nc.tensor.matmul(banks(l, 3)[:, 0:T * E], tri[:, :], flat, start=True, stop=True)
                                nc.tensor.matmul(banks(l, 3)[:, T * E:2 * T * E], ones[:, :], flat, start=True, stop=True
                                                 ).then_inc(mo["pre"], 1)


        def spectral_ffn():
            sf_lane = [sem(f"sf_lane_done{l}") for l in range(LANES)]
            sp_s = {n: sem("sf_" + n) for n in ("p1", "a", "p2", "b", "bias", "out")}
            lanes = range(LANES)
            with ExitStack() as c:
                def sb(n, shape, dt=F32):
                    return c.enter_context(nc.sbuf_tensor(f"sf_{n}", shape, dt))
                wr, wi, co, si = sb("wr", [P, D]), sb("wi", [P, D]), sb("co", [P, D]), sb("si", [P, D])
                sn = sb("sn", [P, D])
                at, bt = sb("at", [P, D]), sb("bt", [P, D])
                m = sb("m", [P, D])
                bias = sb("bias", [P, D])
                xb = [sb(f"xb{l}", [P, T, D]) for l in lanes]
                with nc.Block() as block:
                    @block.sync
                    def _(sp):
                        for w, n in ((wr, "F2_wr"), (wi, "F2_wi"), (co, "dft_cos"), (si, "dft_sin"), (bias, "F2_bias")):
                            load(sp, w[:, :], n)
                        sp.wait_ge(loaded, loads[0])
                with nc.Block() as block:
                    @block.tensor
                    def _(pe):
                        pe.wait_ge(sp_s["a"], 1)
                        nc.tensor.matmul(PS[:, 0, 0:D], wr[:, :], co[:, :], start=True, stop=False)
                        nc.tensor.matmul(PS[:, 0, 0:D], wi[:, :], si[:, :], start=False, stop=True)
                        nc.tensor.matmul(PS[:, 1, 0:D], wr[:, :], si[:, :], start=True, stop=False)
                        nc.tensor.matmul(PS[:, 1, 0:D], wi[:, :], sn[:, :], start=False, stop=True).then_inc(sp_s["p1"], 1)
                        pe.wait_ge(sp_s["a"], 2)
                        nc.tensor.matmul(PS[:, 2, 0:D], at[:, :], co[:, :], start=True, stop=False)
                        nc.tensor.matmul(PS[:, 2, 0:D], bt[:, :], si[:, :], start=False, stop=True).then_inc(sp_s["p2"], 1)

                    @block.vector
                    def _(dve):
                        nc.vector.tensor_scalar(sn[:, :], co[:, :], -1.0, None, ALU.mult).then_inc(sp_s["a"], 1)
                        dve.wait_ge(sp_s["p1"], 1)
                        nc.vector.tensor_copy(at[:, :], PS[:, 0, 0:D])
                        nc.vector.tensor_copy(bt[:, :], PS[:, 1, 0:D]).then_inc(sp_s["a"], 1)
                        dve.wait_ge(sp_s["p2"], 1)
                        nc.vector.tensor_scalar(m[:, :], PS[:, 2, 0:D], 1.0 / D, None, ALU.mult).then_inc(sp_s["b"], 1)
                        dve.wait_ge(sp_s["b"], 1)

                with nc.Block() as block:
                    @block.gpsimd
                    def _(pool):
                        with pool.Fori(0, STEPS) as i:
                            for l in lanes:
                                ln_rstd(pool, 2 * i + l + 1, l, 1e-5)
                                hold(pool, "pool", sf_lane[l], i + 1)
                                nc.gpsimd.tensor_tensor(xb[l][:, :, :], rows(X, i, l),
                                                        bias[:, :].unsqueeze(1).to_broadcast([P, T, D]), ALU.add
                                                        ).then_inc(sp_s["bias"], 1)

                    @block.vector
                    def _(dve):
                        for lane in sf_lane:
                            dve.sem_inc(lane, 1)
                        with dve.Fori(0, STEPS) as i:
                            for l in lanes:
                                hold(dve, "dve", sf_lane[l], i + 1)
                                ln_stats(dve, 2 * i + l + 1, l, lambda t: row(X, i, l, t))
                            for l in lanes:
                                ln_norm(dve, 2 * i + l + 1, l, lambda t: row(X, i, l, t), lambda t: h[l][:, t, :])
                            for l in lanes:
                                hold(dve, "dve", sp_s["bias"], 2 * i + l + 1)
                                hold(dve, "dve", sp_s["out"], 2 * i + l + 1)
                                nc.vector.tensor_tensor(rows(X, i, l), banks(l, 1).rearrange("p (t c) -> p t c", t=T),
                                                        xb[l][:, :, :], ALU.add).then_inc(sf_lane[l], 1)

                    @block.scalar
                    def _(act):
                        with act.Fori(0, STEPS) as i:
                            for l in lanes:
                                act.wait_ge(ln["hTp"], 2 * i + l + 1)
                                nc.scalar.activation(hT[l][:, :], banks(l, 0), ACT.Copy).then_inc(ln["hT"], 1)

                    @block.tensor
                    def _(pe):
                        with pe.Fori(0, STEPS) as i:
                            for l in lanes:
                                pe.wait_ge(ln["norm"], 2 * i + l + 1)
                                transposes(banks(l, 0), h[l]).then_inc(ln["hTp"], 1)
                            for l in lanes:
                                pe.wait_ge(ln["hT"], 2 * i + l + 1)
                                for t in range(T):
                                    op = nc.tensor.matmul(banks(l, 1)[:, t * P:(t + 1) * P], hT[l][:, t * P:(t + 1) * P],
                                                          m[:, :], start=True, stop=True)
                                op.then_inc(sp_s["out"], 1)


        def decoder_layer():
            dl_cg = [sem(f"dl_context{l}") for l in range(LANES)]
            dl_lane = [sem(f"dl_lane_done{l}") for l in range(LANES)]
            dl = {n: sem("dl_" + n) for n in (
                "xTp", "xT", "p0", "p1", "q0", "q1", "k0", "k1", "sc0", "sc1", "mx0", "mx1", "sub0", "sub1", "exp0", "exp1",
                "sum0", "sum1", "rs0", "rs1", "pn0", "pn1", "pTp0", "pTp1", "pT0", "pT1", "av0", "av1", "aT0", "aT1",
                "aTp0", "aTp1", "add0", "add1", "add2", "gm", "gb", "nb", "nTp", "nT", "w1", "f", "hid", "w2")}
            lanes = range(LANES)
            EPS = 0.001
            SCALE = 1.0 / math.sqrt(SEQ)
            with ExitStack() as c:
                def sb(n, shape, dt=F32):
                    return c.enter_context(nc.sbuf_tensor(f"dl_{n}", shape, dt))
                w = {n: sb(n, [P, D]) for n in ("wq1", "wk1", "wv1", "wq2", "wk2", "wv2", "w1", "w2", "b2", "gamma", "beta")}
                cg = [sb(f"cg{l}", [P, ROWS]) for l in lanes]
                qT = [sb(f"qT{l}", [P, ROWS]) for l in lanes]
                kT = [sb(f"kT{l}", [P, ROWS]) for l in lanes]
                va = [sb(f"va{l}", [P, T, D]) for l in lanes]
                pr = [sb(f"pr{l}", [P, T, SEQ]) for l in lanes]
                pT = [sb(f"pT{l}", [P, 2, P]) for l in lanes]
                aT = [sb(f"aT{l}", [P, T, 2, SEQ]) for l in lanes]
                mx = [sb(f"mx{l}", [P, T]) for l in lanes]
                sm = [sb(f"sm{l}", [P, T]) for l in lanes]
                rs = [sb(f"rs{l}", [P, T]) for l in lanes]
                n1 = [sb(f"n1{l}", [P, T, D]) for l in lanes]
                n2 = [sb(f"n2{l}", [P, T, D]) for l in lanes]
                n2b = [sb(f"n2b{l}", [P, T, D]) for l in lanes]
                n3 = [sb(f"n3{l}", [P, T, D]) for l in lanes]
                nT = [sb(f"nT{l}", [P, ROWS]) for l in lanes]
                fT = [sb(f"fT{l}", [P, ROWS]) for l in lanes]
                hd = [sb(f"hd{l}", [P, ROWS]) for l in lanes]
                with nc.Block() as block:
                    @block.sync
                    def _(sp):
                        for n in w:
                            load(sp, w[n][:, :], f"A3_{n}")
                        sp.wait_ge(loaded, loads[0])

                def lnv(i, k, l):
                    return 8 * i + (2 * k + l + 1)

                def all_tiles(v):
                    return v[:, :].unsqueeze(1).to_broadcast([P, T, D])

                with nc.Block() as block:
                    @block.sync
                    def _(sp):
                        with sp.Fori(0, STEPS) as i:
                            for l in lanes:
                                hold(sp, "sp", dl_lane[l], i + 1)
                                sp.dma_start(cg[l][:, :], ctxT[:, bass.ds(2 * ROWS * i + ROWS * l, ROWS)]
                                             ).then_inc(dl_cg[l], 16)

                    @block.gpsimd
                    def _(pool):
                        def gamma_beta(i, k, l, t):
                            v = 6 * i + (2 * (k - 1) + l + 1)
                            hold(pool, "pool", ln["norm"], lnv(i, k, l))
                            nc.gpsimd.tensor_tensor(t[:, :, :], t[:, :, :], all_tiles(w["gamma"]), ALU.mult
                                                    ).then_inc(dl["gm"], 1)
                            hold(pool, "pool", dl["gm"], v)
                            nc.gpsimd.tensor_tensor(t[:, :, :], t[:, :, :], all_tiles(w["beta"]), ALU.add
                                                    ).then_inc(dl["gb"], 1)

                        with pool.Fori(0, STEPS) as i:
                            for l in lanes:
                                ln_rstd(pool, lnv(i, 0, l), l, 1e-5)
                            for l in lanes:
                                ln_rstd(pool, lnv(i, 1, l), l, EPS)
                            for l in lanes:
                                gamma_beta(i, 1, l, n1[l])
                            for l in lanes:
                                ln_rstd(pool, lnv(i, 2, l), l, EPS)
                            for l in lanes:
                                gamma_beta(i, 2, l, n2[l])
                            for l in lanes:
                                hold(pool, "pool", dl["gb"], 6 * i + (2 + l + 1))
                                nc.gpsimd.tensor_tensor(n2b[l][:, :, :], n2[l][:, :, :], all_tiles(w["b2"]), ALU.add
                                                        ).then_inc(dl["nb"], 1)
                            for l in lanes:
                                ln_rstd(pool, lnv(i, 3, l), l, EPS)
                            for l in lanes:
                                gamma_beta(i, 3, l, n3[l])

                    @block.vector
                    def _(dve):
                        def tiles(bank):
                            return bank.rearrange("p (t c) -> p t c", t=T)

                        def attention(i, a):
                            for l in lanes:
                                v = 2 * i + l + 1
                                hold(dve, "dve", dl[f"p{a}"], v)
                                nc.vector.tensor_copy(kT[l][:, :], banks(l, 2)).then_inc(dl[f"k{a}"], 1)
                            for l in lanes:
                                v = 2 * i + l + 1
                                S = banks(l, 0)[:, 0:T * SEQ].rearrange("p (n k) -> p n k", k=SEQ)
                                dve.wait_ge(dl[f"sc{a}"], v)
                                nc.vector.tensor_reduce(mx[l][:, :], S, op=ALU.max, axis=AX).then_inc(dl[f"mx{a}"], 1)
                                dve.wait_ge(dl[f"mx{a}"], v)
                                nc.vector.tensor_tensor(pr[l][:, :, :], S, mx[l][:, :].unsqueeze(2).to_broadcast([P, T, SEQ]),
                                                        ALU.subtract).then_inc(dl[f"sub{a}"], 1)
                            for l in lanes:
                                v = 2 * i + l + 1
                                dve.wait_ge(dl[f"exp{a}"], v)
                                nc.vector.tensor_reduce(sm[l][:, :], pr[l][:, :, :], op=ALU.add, axis=AX
                                                        ).then_inc(dl[f"sum{a}"], 1)
                                dve.wait_ge(dl[f"sum{a}"], v)
                                nc.vector.reciprocal(rs[l][:, :], sm[l][:, :]).then_inc(dl[f"rs{a}"], 1)
                                dve.wait_ge(dl[f"rs{a}"], v)
                                nc.vector.tensor_tensor(pr[l][:, :, :], pr[l][:, :, :],
                                                        rs[l][:, :].unsqueeze(2).to_broadcast([P, T, SEQ]), ALU.mult
                                                        ).then_inc(dl[f"pn{a}"], 1)

                        for lane in dl_lane:
                            dve.sem_inc(lane, 1)
                        with dve.Fori(0, STEPS) as i:
                            for l in lanes:
                                hold(dve, "dve", dl_lane[l], i + 1)
                                ln_stats(dve, lnv(i, 0, l), l, lambda t: row(X, i, l, t))
                            for l in lanes:
                                ln_norm(dve, lnv(i, 0, l), l, lambda t: row(X, i, l, t), lambda t: h[l][:, t, :])
                            attention(i, 0)
                            for l in lanes:
                                v = 2 * i + l + 1
                                dve.wait_ge(dl["aTp0"], v)
                                nc.vector.tensor_tensor(n1[l][:, :, :], tiles(banks(l, 0)), h[l][:, :, :], ALU.add
                                                        ).then_inc(dl["add0"], 1)
                                hold(dve, "dve", dl["add0"], v)
                                ln_stats(dve, lnv(i, 1, l), l, lambda t: n1[l][:, t, :])
                            for l in lanes:
                                ln_norm(dve, lnv(i, 1, l), l, lambda t: n1[l][:, t, :], lambda t: n1[l][:, t, :])
                            attention(i, 1)
                            for l in lanes:
                                v = 2 * i + l + 1
                                dve.wait_ge(dl["gb"], 6 * i + (l + 1))
                                dve.wait_ge(dl["aTp1"], v)
                                nc.vector.tensor_tensor(n2[l][:, :, :], tiles(banks(l, 0)), n1[l][:, :, :], ALU.add
                                                        ).then_inc(dl["add1"], 1)
                                hold(dve, "dve", dl["add1"], v)
                                ln_stats(dve, lnv(i, 2, l), l, lambda t: n2[l][:, t, :])
                            for l in lanes:
                                ln_norm(dve, lnv(i, 2, l), l, lambda t: n2[l][:, t, :], lambda t: n2[l][:, t, :])
                            for l in lanes:
                                v = 2 * i + l + 1
                                dve.wait_ge(dl["f"], v)
                                nc.vector.scalar_tensor_tensor(hd[l][:, :], fT[l][:, :], 0.2, fT[l][:, :], ALU.mult, ALU.max
                                                               ).then_inc(dl["hid"], 1)
                            for l in lanes:
                                v = 2 * i + l + 1
                                dve.wait_ge(dl["nb"], v)
                                dve.wait_ge(dl["w2"], v)
                                nc.vector.tensor_tensor(n3[l][:, :, :], tiles(banks(l, 3)), n2b[l][:, :, :], ALU.add
                                                        ).then_inc(dl["add2"], 1)
                                hold(dve, "dve", dl["add2"], v)
                                ln_stats(dve, lnv(i, 3, l), l, lambda t: n3[l][:, t, :])
                            for l in lanes:
                                ln_norm(dve, lnv(i, 3, l), l, lambda t: n3[l][:, t, :], lambda t: n3[l][:, t, :])
                            for l in lanes:
                                hold(dve, "dve", dl["gb"], 6 * i + (4 + l + 1))
                                nc.vector.scalar_tensor_tensor(rows(X, i, l), n3[l][:, :, :], 0.0, rows(X, i, l),
                                                               ALU.max, ALU.add).then_inc(dl_lane[l], 1)

                    @block.scalar
                    def _(act):
                        def attention(i, a):
                            for l in lanes:
                                v = 2 * i + l + 1
                                act.wait_ge(dl[f"p{a}"], v)
                                nc.scalar.activation(qT[l][:, :], banks(l, 1), ACT.Copy)
                                nc.scalar.activation(va[l][:, :, :].rearrange("p t c -> p (t c)"), banks(l, 3), ACT.Copy
                                                     ).then_inc(dl[f"q{a}"], 1)
                            for l in lanes:
                                v = 2 * i + l + 1
                                act.wait_ge(dl[f"sub{a}"], v)
                                nc.scalar.activation(pr[l][:, :, :], pr[l][:, :, :], ACT.Exp, scale=SCALE
                                                     ).then_inc(dl[f"exp{a}"], 1)
                            for l in lanes:
                                v = 2 * i + l + 1
                                act.wait_ge(dl[f"pTp{a}"], v)
                                nc.scalar.activation(pT[l][:, :, :].rearrange("p u c -> p (u c)"), banks(l, 1)[:, 0:2 * P],
                                                     ACT.Copy).then_inc(dl[f"pT{a}"], 1)
                            for l in lanes:
                                v = 2 * i + l + 1
                                act.wait_ge(dl[f"av{a}"], v)
                                for x_ in range(2):
                                    op = nc.scalar.activation(aT[l][:, :, x_, :],
                                                              banks(l, 2 + x_)[:, 0:T * SEQ].rearrange("p (t q) -> p t q", t=T),
                                                              ACT.Copy)
                                op.then_inc(dl[f"aT{a}"], 1)

                        with act.Fori(0, STEPS) as i:
                            for l in lanes:
                                act.wait_ge(dl["xTp"], 2 * i + l + 1)
                                nc.scalar.activation(hT[l][:, :], banks(l, 0), ACT.Copy).then_inc(dl["xT"], 1)
                            attention(i, 0)
                            attention(i, 1)
                            for l in lanes:
                                act.wait_ge(dl["nTp"], 2 * i + l + 1)
                                nc.scalar.activation(nT[l][:, :], banks(l, 1), ACT.Copy).then_inc(dl["nT"], 1)
                            for l in lanes:
                                act.wait_ge(dl["w1"], 2 * i + l + 1)
                                nc.scalar.activation(fT[l][:, :], banks(l, 2), ACT.Identity, bias=column("A3_b1")
                                                     ).then_inc(dl["f"], 1)

                    @block.tensor
                    def _(pe):
                        def project(l, a, q_of, kv_of):
                            nc.tensor.matmul(banks(l, 1), w[f"wq{a + 1}"][:, :], q_of, start=True, stop=True)
                            nc.tensor.matmul(banks(l, 2), w[f"wk{a + 1}"][:, :], kv_of, start=True, stop=True)
                            for t in range(T):
                                op = nc.tensor.matmul(banks(l, 3)[:, t * P:(t + 1) * P], kv_of[:, t * P:(t + 1) * P],
                                                      w[f"wv{a + 1}"][:, :], start=True, stop=True)
                            op.then_inc(dl[f"p{a}"], 1)

                        def attention(i, a):
                            for l in lanes:
                                v = 2 * i + l + 1
                                hold(pe, "pe", dl[f"q{a}"], v)
                                hold(pe, "pe", dl[f"k{a}"], v)
                                if a == 0:
                                    nc.tensor.matmul(banks(l, 0)[:, 0:T * SEQ].rearrange("p (n k) -> p n k", k=SEQ),
                                                     ident_bf[:, :], causal_bf[:, :].unsqueeze(1).to_broadcast([P, T, SEQ]),
                                                     start=True, stop=False, skip_group_check=True)
                                for u in range(2):
                                    for b in range(2):
                                        for x_ in range(2):
                                            s = SEQ * (4 * u + 2 * b + x_)
                                            op = nc.tensor.matmul(
                                                banks(l, 0)[SEQ * b:SEQ * (b + 1), SEQ * (2 * u + x_):SEQ * (2 * u + x_ + 1)],
                                                qT[l][:, s:s + SEQ], kT[l][:, s:s + SEQ], start=(a == 1), stop=True,
                                                skip_group_check=True)
                                op.then_inc(dl[f"sc{a}"], 1)
                            for l in lanes:
                                v = 2 * i + l + 1
                                pe.wait_ge(dl[f"pn{a}"], v)
                                for u in range(2):
                                    op = nc.tensor.transpose(banks(l, 1)[:, u * P:(u + 1) * P],
                                                             pr[l][:, 2 * u:2 * u + 2, :].rearrange("p n k -> p (n k)"),
                                                             ident[:, :])
                                op.then_inc(dl[f"pTp{a}"], 1)
                            for l in lanes:
                                v = 2 * i + l + 1
                                hold(pe, "pe", dl[f"pT{a}"], v)
                                for t in range(T):
                                    for x_ in range(2):
                                        r = slice(SEQ * x_, SEQ * (x_ + 1))
                                        op = nc.tensor.matmul(banks(l, 2 + x_)[:, SEQ * t:SEQ * (t + 1)], va[l][r, t, :],
                                                              pT[l][r, t // 2, SEQ * (t % 2):SEQ * (t % 2 + 1)],
                                                              start=True, stop=True)
                                op.then_inc(dl[f"av{a}"], 1)
                            for l in lanes:
                                v = 2 * i + l + 1
                                pe.wait_ge(dl[f"aT{a}"], v)
                                for t in range(T):
                                    op = nc.tensor.transpose(banks(l, 0)[:, t * P:(t + 1) * P],
                                                             aT[l][:, t, :, :].rearrange("p x q -> p (x q)"), ident[:, :])
                                op.then_inc(dl[f"aTp{a}"], 1)

                        with pe.Fori(0, STEPS) as i:
                            for l in lanes:
                                pe.wait_ge(ln["norm"], lnv(i, 0, l))
                                transposes(banks(l, 0), h[l]).then_inc(dl["xTp"], 1)
                            for l in lanes:
                                pe.wait_ge(dl["xT"], 2 * i + l + 1)
                                project(l, 0, hT[l][:, :], hT[l][:, :])
                            attention(i, 0)
                            for l in lanes:
                                pe.wait_ge(dl_cg[l], 16 * i + 16)
                                project(l, 1, aT[l][:, :, :, :].rearrange("p t x q -> p (t x q)"), cg[l][:, :])
                            attention(i, 1)
                            for l in lanes:
                                pe.wait_ge(dl["gb"], 6 * i + (2 + l + 1))
                                transposes(banks(l, 1), n2[l]).then_inc(dl["nTp"], 1)
                            for l in lanes:
                                pe.wait_ge(dl["nT"], 2 * i + l + 1)
                                nc.tensor.matmul(banks(l, 2), w["w1"][:, :], nT[l][:, :], start=True, stop=True
                                                 ).then_inc(dl["w1"], 1)
                            for l in lanes:
                                pe.wait_ge(dl["hid"], 2 * i + l + 1)
                                for t in range(T):
                                    op = nc.tensor.matmul(banks(l, 3)[:, t * P:(t + 1) * P], hd[l][:, t * P:(t + 1) * P],
                                                          w["w2"][:, :], start=True, stop=True)
                                op.then_inc(dl["w2"], 1)


        def start_stream(Y):
            y0_lane = [sem(f"y0_lane_done{l}") for l in range(LANES)]
            with nc.Block() as block:
                @block.gpsimd
                def _(pool):
                    with pool.Fori(0, STEPS) as i:
                        for l in range(LANES):
                            ln_rstd(pool, 2 * i + l + 1, l, 1e-5)

                @block.vector
                def _(dve):
                    for lane in y0_lane:
                        dve.sem_inc(lane, 1)
                    with dve.Fori(0, STEPS) as i:
                        for l in range(LANES):
                            hold(dve, "dve", y0_lane[l], i + 1)
                            ln_stats(dve, 2 * i + l + 1, l, lambda t: row(X, i, l, t))
                        for l in range(LANES):
                            ln_norm(dve, 2 * i + l + 1, l, lambda t: row(X, i, l, t), lambda t: row(Y, i, l, t))
                            hold(dve, "dve", ln["norm"], 2 * i + l + 1)
                            nc.vector.memset(ve[l][:, :], 1.0).then_inc(y0_lane[l], 1)

        NEWTON = 11

        def window_attention(lyr, Y):
            wa_lane = [sem(f"wa_lane_done{l}") for l in range(LANES)]
            wa = {n: sem("wa_" + n) for n in (
                "tab", "sh", "shr", "shl", "hTp", "hT", "qkv", "sq", "n2", "ab", "sum", "nw", "qkn", "qkTp", "qkT", "sc", "mx",
                "sub", "exp", "den", "rden", "pn", "pTp", "pT", "av", "o0", "o1", "wo", "yT", "yTp")}
            lanes = range(LANES)
            pre = f"F3_{lyr}_"
            with ExitStack() as c:
                def sb(n, shape, dt=F32):
                    return c.enter_context(nc.sbuf_tensor(f"wa{lyr}_{n}", shape, dt))
                wqkv = sb("wqkv", [P, 3 * INNER])
                wo = sb("wo", [P, 4, D])
                shift = sb("shift", [P, P])
                rope = sb("rope", [P, 4 * HEAD_DIM])
                tab = sb("tab", [P, 4, HEAD_DIM])
                hs = [sb(f"hs{l}", [P, T, D]) for l in lanes]
                sq = [sb(f"sq{l}", [P, 2 * INNER]) for l in lanes]
                qk = [sb(f"qk{l}", [P, T, 2 * INNER]) for l in lanes]
                tb = [sb(f"tb{l}", [P, 2 * INNER]) for l in lanes]
                va = [sb(f"va{l}", [P, T, INNER]) for l in lanes]
                ss = [sb(f"ss{l}", [P, T, 2 * HEADS]) for l in lanes]
                y_ = [sb(f"y{l}", [P, T * 2 * HEADS]) for l in lanes]
                t_ = [sb(f"t{l}", [P, T * 2 * HEADS]) for l in lanes]
                qkT = [sb(f"qkT{l}", [P, 8, P]) for l in lanes]
                pr = [sb(f"pr{l}", [P, 8, SEQ]) for l in lanes]
                pT = [sb(f"pT{l}", [P, 4, P]) for l in lanes]
                mx = [sb(f"mx{l}", [P, 8]) for l in lanes]
                den = [sb(f"den{l}", [P, 8]) for l in lanes]
                rden = [sb(f"rden{l}", [P, 8]) for l in lanes]
                oT = [sb(f"oT{l}", [P, 4, ROWS]) for l in lanes]
                yT = [sb(f"yT{l}", [P, ROWS]) for l in lanes]
                with nc.Block() as block:
                    @block.sync
                    def _(sp):
                        load(sp, wqkv[:, :], pre + "wqkv")
                        load(sp, wo[:, :, :].rearrange("p a b -> p (a b)"), pre + "wo")
                        load(sp, shift[:, :], "shift")
                        load(sp, rope[:, :], "rope")
                        load(sp, tab[:, :, :].rearrange("p a b -> p (a b)"), pre + "scales")
                        sp.wait_ge(loaded, loads[0])
                with nc.Block() as block:
                    @block.vector
                    def _(dve):
                        flat = tab[:, :, :].rearrange("p a b -> p (a b)")
                        nc.vector.tensor_tensor(flat, flat, rope[:, :], ALU.mult).then_inc(wa["tab"], 1)
                        dve.wait_ge(wa["tab"], 1)

                def gv(i, l):
                    return 2 * i + l + 1

                def tv(i, t, l):
                    return 8 * i + (2 * t + l + 1)

                with nc.Block() as block:
                    @block.gpsimd
                    def _(pool):
                        with pool.Fori(0, STEPS) as i:
                            for l in lanes:
                                hold(pool, "pool", wa_lane[l], i + 1)
                                nc.gpsimd.tensor_copy(hs[l][:, :, 0:D // 2], rows(Y, i, l)[:, :, 0:D // 2]
                                                      ).then_inc(wa["shl"], 1)
                            for t in range(T):
                                for l in lanes:
                                    hold(pool, "pool", wa["ab"], tv(i, t, l))
                                    nc.gpsimd.tensor_tensor(qk[l][:, t, :], qk[l][:, t, :], tb[l][:, :], ALU.add
                                                            ).then_inc(wa["sum"], 1)
                            for t in range(T):
                                for l in lanes:
                                    if t == 0:
                                        hold(pool, "pool", wa["nw"], 2 * NEWTON * i + NEWTON * (l + 1))
                                        hold(pool, "pool", wa["sum"], tv(i, T - 1, l))
                                    q = qk[l][:, t, :].rearrange("p (n d) -> p n d", d=HEAD_DIM)
                                    r = y_[l][:, 2 * HEADS * t:2 * HEADS * (t + 1)].unsqueeze(2).to_broadcast(
                                        [P, 2 * HEADS, HEAD_DIM])
                                    nc.gpsimd.tensor_tensor(q, q, r, ALU.mult).then_inc(wa["qkn"], 1)

                    @block.vector
                    def _(dve):
                        def inverse_roots(i, l):
                            k = [0]
                            s = ss[l][:, :, :].rearrange("p t n -> p (t n)")
                            y, t = y_[l][:, :], t_[l][:, :]

                            def step(op):
                                k[0] += 1
                                op.then_inc(wa["nw"], 1)
                                if k[0] < NEWTON:
                                    hold(dve, "dve", wa["nw"], 2 * NEWTON * i + (NEWTON * l + k[0]))

                            step(nc.vector.tensor_scalar(s, s, 1e-24, None, ALU.max))
                            step(nc.vector.tensor_scalar(y.bitcast(I32), s.bitcast(I32), -0.5, RSQRT_SEED, ALU.mult, ALU.add))
                            for _ in range(3):
                                step(nc.vector.scalar_tensor_tensor(t, y, -0.5, y, ALU.mult, ALU.mult))
                                step(nc.vector.tensor_tensor(t, t, s, ALU.mult))
                                step(nc.vector.scalar_tensor_tensor(y, t, 1.5, y, ALU.add, ALU.mult))
                            assert k[0] == NEWTON

                        for lane in wa_lane:
                            dve.sem_inc(lane, 1)
                        with dve.Fori(0, STEPS) as i:
                            for t in range(T):
                                for l in lanes:
                                    v = tv(i, t, l)
                                    both = banks(l, 0, 2)
                                    hold(dve, "dve", wa["sq"], v)
                                    nc.vector.tensor_reduce(ss[l][:, t, :], sq[l][:, :].rearrange("p (n d) -> p n d", d=HEAD_DIM),
                                                            op=ALU.add, axis=AX).then_inc(wa["n2"], 1)
                                    v4 = lambda ap: ap.rearrange("p (a h d) -> p a h d", a=2, d=HEAD_DIM)
                                    nc.vector.tensor_tensor(v4(qk[l][:, t, :]), v4(both),
                                                            tab[:, 0:2, :].unsqueeze(2).to_broadcast([P, 2, HEADS, HEAD_DIM]),
                                                            ALU.mult)
                                    if t:
                                        hold(dve, "dve", wa["sum"], tv(i, t - 1, l))
                                    hd = HEAD_DIM // 2
                                    for lo, hi in ((0, hd), (hd, 0)):
                                        op = nc.vector.tensor_tensor(
                                            v4(tb[l][:, :])[:, :, :, lo:lo + hd], v4(both)[:, :, :, hi:hi + hd],
                                            tab[:, 2:4, lo:lo + hd].unsqueeze(2).to_broadcast([P, 2, HEADS, hd]), ALU.mult)
                                    op.then_inc(wa["ab"], 1)
                            for l in lanes:
                                hold(dve, "dve", wa["n2"], tv(i, T - 1, l))
                                inverse_roots(i, l)
                            for t in range(T):
                                for l in lanes:
                                    v = tv(i, t, l)
                                    S = banks(l, 2).rearrange("p (n k) -> p n k", k=SEQ)
                                    dve.wait_ge(wa["sc"], v)
                                    nc.vector.tensor_reduce(mx[l][:, :], S, op=ALU.max, axis=AX).then_inc(wa["mx"], 1)
                                    dve.wait_ge(wa["mx"], v)
                                    nc.vector.tensor_tensor(pr[l][:, :, :], S, mx[l][:, :].unsqueeze(2).to_broadcast(
                                        [P, 8, SEQ]), ALU.subtract).then_inc(wa["sub"], 1)
                                for l in lanes:
                                    v = tv(i, t, l)
                                    dve.wait_ge(wa["exp"], v)
                                    nc.vector.tensor_reduce(den[l][:, :], pr[l][:, :, :], op=ALU.add, axis=AX
                                                            ).then_inc(wa["den"], 1)
                                    dve.wait_ge(wa["den"], v)
                                    nc.vector.reciprocal(rden[l][:, :], den[l][:, :]).then_inc(wa["rden"], 1)
                                    dve.wait_ge(wa["rden"], v)
                                    nc.vector.tensor_tensor(pr[l][:, :, :], pr[l][:, :, :], rden[l][:, :].unsqueeze(2)
                                                            .to_broadcast([P, 8, SEQ]), ALU.mult).then_inc(wa["pn"], 1)
                                for l in lanes:
                                    v = tv(i, t, l)
                                    hold(dve, "dve", wa["av"], v)
                                    nc.vector.tensor_copy(oT[l][:, :, t * P + SEQ:(t + 1) * P],
                                                          banks(l, 1)[:, 0:4 * SEQ].rearrange("p (c q) -> p c q", c=4)
                                                          ).then_inc(wa["o1"], 1)
                            for l in lanes:
                                hold(dve, "dve", wa["yTp"], gv(i, l))
                                nc.vector.tensor_tensor(rows(Y, i, l), banks(l, 3).rearrange("p (t c) -> p t c", t=T),
                                                        rows(Y, i, l), ALU.add).then_inc(wa_lane[l], 1)

                    @block.scalar
                    def _(act):
                        with act.Fori(0, STEPS) as i:
                            for l in lanes:
                                act.wait_ge(wa["sh"], gv(i, l))
                                nc.scalar.activation(hs[l][:, :, D // 2:D],
                                                     banks(l, 0)[:, 0:T * D // 2].rearrange("p (t c) -> p t c", t=T),
                                                     ACT.Copy).then_inc(wa["shr"], 1)
                            for l in lanes:
                                act.wait_ge(wa["hTp"], gv(i, l))
                                nc.scalar.activation(hT[l][:, :], banks(l, 1), ACT.Copy).then_inc(wa["hT"], 1)
                            for t in range(T):
                                for l in lanes:
                                    act.wait_ge(wa["qkv"], tv(i, t, l))
                                    if t:
                                        act.wait_ge(wa["n2"], tv(i, t - 1, l))
                                    nc.scalar.activation(sq[l][:, :], banks(l, 0, 2), ACT.Square)
                                    nc.scalar.activation(va[l][:, t, :], banks(l, 2), ACT.Copy).then_inc(wa["sq"], 1)
                            for t in range(T):
                                for l in lanes:
                                    act.wait_ge(wa["qkTp"], tv(i, t, l))
                                    nc.scalar.activation(qkT[l][:, :, :].rearrange("p c q -> p (c q)"), banks(l, 0, 2),
                                                         ACT.Copy).then_inc(wa["qkT"], 1)
                                for l in lanes:
                                    act.wait_ge(wa["sub"], tv(i, t, l))
                                    nc.scalar.activation(pr[l][:, :, :], pr[l][:, :, :], ACT.Exp).then_inc(wa["exp"], 1)
                                for l in lanes:
                                    act.wait_ge(wa["pTp"], tv(i, t, l))
                                    nc.scalar.activation(pT[l][:, :, :].rearrange("p c q -> p (c q)"), banks(l, 3), ACT.Copy
                                                         ).then_inc(wa["pT"], 1)
                                for l in lanes:
                                    act.wait_ge(wa["av"], tv(i, t, l))
                                    nc.scalar.activation(oT[l][:, :, t * P:t * P + SEQ],
                                                         banks(l, 0)[:, 0:4 * SEQ].rearrange("p (c q) -> p c q", c=4),
                                                         ACT.Copy).then_inc(wa["o0"], 1)
                            for l in lanes:
                                act.wait_ge(wa["wo"], gv(i, l))
                                nc.scalar.activation(yT[l][:, :], banks(l, 2), ACT.Copy).then_inc(wa["yT"], 1)

                    @block.tensor
                    def _(pe):
                        with pe.Fori(0, STEPS) as i:
                            for l in lanes:
                                hold(pe, "pe", wa_lane[l], i + 1)
                                nc.tensor.matmul(banks(l, 0)[:, 0:T * D // 2].rearrange("p (t c) -> p t c", t=T),
                                                 shift[:, :], rows(Y, i, l)[:, :, D // 2:D], start=True, stop=True
                                                 ).then_inc(wa["sh"], 1)
                            for l in lanes:
                                hold(pe, "pe", wa["shl"], gv(i, l))
                                pe.wait_ge(wa["shr"], gv(i, l))
                                transposes(banks(l, 1), hs[l]).then_inc(wa["hTp"], 1)
                            for t in range(T):
                                for l in lanes:
                                    if t == 0:
                                        pe.wait_ge(wa["hT"], gv(i, l))
                                    else:
                                        pe.wait_ge(wa["ab"], tv(i, t - 1, l))
                                    for j in range(3):
                                        op = nc.tensor.matmul(banks(l, j), hT[l][:, t * P:(t + 1) * P],
                                                              wqkv[:, j * INNER:(j + 1) * INNER], start=True, stop=True)
                                    op.then_inc(wa["qkv"], 1)
                            for t in range(T):
                                for l in lanes:
                                    if t:
                                        hold(pe, "pe", wa["o0"], tv(i, t - 1, l))
                                        hold(pe, "pe", wa["o1"], tv(i, t - 1, l))
                                    pe.wait_ge(wa["qkn"], tv(i, t, l))
                                    for k in range(8):
                                        op = nc.tensor.transpose(banks(l, 0, 2)[:, k * P:(k + 1) * P],
                                                                 qk[l][:, t, k * P:(k + 1) * P], ident[:, :])
                                    op.then_inc(wa["qkTp"], 1)
                                for l in lanes:
                                    pe.wait_ge(wa["qkT"], tv(i, t, l))
                                    nc.tensor.matmul(banks(l, 2).rearrange("p (n k) -> p n k", k=SEQ), ident_bf[:, :],
                                                     causal_bf[:, :].unsqueeze(1).to_broadcast([P, 8, SEQ]),
                                                     start=True, stop=False, skip_group_check=True)
                                    for k in range(4):
                                        for b in range(2):
                                            for hh in range(2):
                                                r = slice(SEQ * hh, SEQ * (hh + 1))
                                                s = slice(SEQ * b, SEQ * (b + 1))
                                                op = nc.tensor.matmul(
                                                    banks(l, 2)[r, SEQ * (2 * k + b):SEQ * (2 * k + b + 1)],
                                                    qkT[l][r, k, s], qkT[l][r, 4 + k, s], start=False, stop=True,
                                                    skip_group_check=True)
                                    op.then_inc(wa["sc"], 1)
                                for l in lanes:
                                    pe.wait_ge(wa["pn"], tv(i, t, l))
                                    for k in range(4):
                                        op = nc.tensor.transpose(banks(l, 3)[:, k * P:(k + 1) * P],
                                                                 pr[l][:, 2 * k:2 * k + 2, :].rearrange("p n k -> p (n k)"),
                                                                 ident[:, :])
                                    op.then_inc(wa["pTp"], 1)
                                for l in lanes:
                                    hold(pe, "pe", wa["pT"], tv(i, t, l))
                                    for k in range(4):
                                        for b in range(2):
                                            for hh in range(2):
                                                s = slice(SEQ * b, SEQ * (b + 1))
                                                head = 2 * k + hh
                                                op = nc.tensor.matmul(
                                                    banks(l, b)[SEQ * hh:SEQ * (hh + 1), SEQ * k:SEQ * (k + 1)],
                                                    va[l][s, t, HEAD_DIM * head:HEAD_DIM * (head + 1)],
                                                    pT[l][s, k, SEQ * hh:SEQ * (hh + 1)], start=True, stop=True)
                                    op.then_inc(wa["av"], 1)
                            for l in lanes:
                                hold(pe, "pe", wa["o0"], tv(i, T - 1, l))
                                pe.wait_ge(wa["o1"], tv(i, T - 1, l))
                                for k in range(4):
                                    op = nc.tensor.matmul(banks(l, 2), wo[:, k, :], oT[l][:, k, :], start=(k == 0), stop=(k == 3))
                                op.then_inc(wa["wo"], 1)
                            for l in lanes:
                                pe.wait_ge(wa["yT"], gv(i, l))
                                for t in range(T):
                                    op = nc.tensor.transpose(banks(l, 3)[:, t * P:(t + 1) * P], yT[l][:, t * P:(t + 1) * P],
                                                             ident[:, :])
                                op.then_inc(wa["yTp"], 1)


        def gated_ffn(lyr, Y, last):
            stored = [sem(f"stored{l}") for l in range(LANES)]
            gf_lane = [sem(f"gf_lane_done{l}") for l in range(LANES)]
            gf = {n: sem("gf_" + n) for n in ("sh", "shr", "shl", "hTp", "hT", "ag", "gl", "u", "w2", "yT", "yTp", "add", "sum")}
            lanes = range(LANES)
            pre = f"F3_{lyr}_"
            with ExitStack() as c:
                def sb(n, shape, dt=F32):
                    return c.enter_context(nc.sbuf_tensor(f"gf{lyr}_{n}", shape, dt))
                w1 = sb("w1", [P, 2 * HID])
                w2 = sb("w2", [P, NHC, D])
                shift = sb("shift", [P, P])
                hs = [sb(f"hs{l}", [P, T, D]) for l in lanes]
                gl = [[sb(f"gl{l}{k}", [P, ROWS]) for k in range(NHC)] for l in lanes]
                uT = [[sb(f"uT{l}{k}", [P, ROWS]) for k in range(NHC)] for l in lanes]
                yT = [sb(f"yT{l}", [P, ROWS]) for l in lanes]
                xo = [sb(f"xo{l}", [P, T, D]) for l in lanes]
                with nc.Block() as block:
                    @block.sync
                    def _(sp):
                        load(sp, w1[:, :], pre + "w1")
                        load(sp, w2[:, :, :].rearrange("p a b -> p (a b)"), pre + "w2")
                        load(sp, shift[:, :], "shift")
                        sp.wait_ge(loaded, loads[0])

                def gv(i, l):
                    return 2 * i + l + 1

                def cv(i, k, l):
                    return 2 * NHC * i + (2 * k + l + 1)

                def pair(k):
                    return (2, 3) if k % 2 == 0 else (0, 1)

                with nc.Block() as block:
                    if last:
                        @block.sync
                        def _(sp):
                            for l in lanes:
                                sp.sem_inc(stored[l], 16)
                            with sp.Fori(0, STEPS) as i:
                                for l in lanes:
                                    hold(sp, "sp", gf_lane[l], i + 2)
                                    sp.dma_start(out[bass.ds(2 * ROWS * i + ROWS * l, ROWS), :].rearrange(
                                        "(t p) c -> p t c", p=P), xo[l][:, :, :]).then_inc(stored[l], 16)
                            for l in lanes:
                                sp.wait_ge(stored[l], 16 * (STEPS + 1))

                    @block.gpsimd
                    def _(pool):
                        with pool.Fori(0, STEPS) as i:
                            for l in lanes:
                                hold(pool, "pool", gf_lane[l], i + 1)
                                nc.gpsimd.tensor_copy(hs[l][:, :, 0:D // 2], rows(Y, i, l)[:, :, 0:D // 2]
                                                      ).then_inc(gf["shl"], 1)
                            for l in lanes:
                                ln_rstd(pool, 2 * i + l + 1, l, 1e-5)

                    @block.vector
                    def _(dve):
                        for lane in gf_lane:
                            dve.sem_inc(lane, 1)
                        with dve.Fori(0, STEPS) as i:
                            for l in lanes:
                                hold(dve, "dve", gf["shl"], gv(i, l))
                                hold(dve, "dve", gf["shr"], gv(i, l))
                                ln_stats(dve, 2 * i + l + 1, l, lambda t: hs[l][:, t, :])
                            for l in lanes:
                                ln_norm(dve, 2 * i + l + 1, l, lambda t: hs[l][:, t, :], lambda t: h[l][:, t, :])
                            for k, (at, m) in enumerate(HID_CHUNKS):
                                for l in lanes:
                                    hold(dve, "dve", gf["gl"], cv(i, k, l))
                                    nc.vector.scalar_tensor_tensor(uT[l][k][0:m, :], banks(l, pair(k)[0])[0:m, :],
                                                                   column(pre + "b1", k)[0:m], gl[l][k][0:m, :],
                                                                   ALU.add, ALU.mult).then_inc(gf["u"], 1)
                            for l in lanes:
                                hold(dve, "dve", gf["yTp"], gv(i, l))
                                if not last:
                                    nc.vector.tensor_tensor(rows(Y, i, l), banks(l, 1).rearrange("p (t c) -> p t c", t=T),
                                                            rows(Y, i, l), ALU.add).then_inc(gf_lane[l], 1)
                                else:
                                    hold(dve, "dve", stored[l], 16 * i + 16)
                                    nc.vector.tensor_tensor(xo[l][:, :, :], banks(l, 1).rearrange("p (t c) -> p t c", t=T),
                                                            rows(Y, i, l), ALU.add).then_inc(gf["add"], 1)
                                    hold(dve, "dve", gf["add"], 2 * i + l + 1)
                                    nc.vector.tensor_tensor(xo[l][:, :, :], xo[l][:, :, :], rows(X, i, l), ALU.add
                                                            ).then_inc(gf_lane[l], 1)

                    @block.scalar
                    def _(act):
                        with act.Fori(0, STEPS) as i:
                            for l in lanes:
                                act.wait_ge(gf["sh"], gv(i, l))
                                nc.scalar.activation(hs[l][:, :, D // 2:D],
                                                     banks(l, 0)[:, 0:T * D // 2].rearrange("p (t c) -> p t c", t=T),
                                                     ACT.Copy).then_inc(gf["shr"], 1)
                            for l in lanes:
                                act.wait_ge(gf["hTp"], gv(i, l))
                                nc.scalar.activation(hT[l][:, :], banks(l, 1), ACT.Identity, scale=column(pre + "lg"),
                                                     bias=column(pre + "lb")).then_inc(gf["hT"], 1)
                            for k, (at, m) in enumerate(HID_CHUNKS):
                                for l in lanes:
                                    act.wait_ge(gf["ag"], cv(i, k, l))
                                    nc.scalar.activation(gl[l][k][0:m, :], banks(l, pair(k)[1])[0:m, :], ACT.Gelu,
                                                         bias=column(pre + "b1", NHC + k)[0:m]).then_inc(gf["gl"], 1)
                            for l in lanes:
                                act.wait_ge(gf["w2"], gv(i, l))
                                nc.scalar.activation(yT[l][:, :], banks(l, 0), ACT.Identity, bias=column(pre + "b2")
                                                     ).then_inc(gf["yT"], 1)

                    @block.tensor
                    def _(pe):
                        with pe.Fori(0, STEPS) as i:
                            for l in lanes:
                                hold(pe, "pe", gf_lane[l], i + 1)
                                nc.tensor.matmul(banks(l, 0)[:, 0:T * D // 2].rearrange("p (t c) -> p t c", t=T),
                                                 shift[:, :], rows(Y, i, l)[:, :, D // 2:D], start=True, stop=True
                                                 ).then_inc(gf["sh"], 1)
                            for l in lanes:
                                pe.wait_ge(ln["norm"], 2 * i + l + 1)
                                transposes(banks(l, 1), h[l]).then_inc(gf["hTp"], 1)
                            for k, (at, m) in enumerate(HID_CHUNKS):
                                for l in lanes:
                                    if k == 0:
                                        pe.wait_ge(gf["hT"], gv(i, l))
                                    elif k > 1:
                                        pe.wait_ge(gf["u"], cv(i, k - 2, l))
                                    for j in range(2):
                                        op = nc.tensor.matmul(banks(l, pair(k)[j])[0:m, :], w1[:, j * HID + at:j * HID + at + m],
                                                              hT[l][:, :], start=True, stop=True)
                                    op.then_inc(gf["ag"], 1)
                            for l in lanes:
                                for k, (at, m) in enumerate(HID_CHUNKS):
                                    pe.wait_ge(gf["u"], cv(i, max(k, 1), l))
                                    op = nc.tensor.matmul(banks(l, 0), w2[0:m, k, :], uT[l][k][0:m, :], start=(k == 0),
                                                          stop=(k == NHC - 1))
                                op.then_inc(gf["w2"], 1)
                            for l in lanes:
                                pe.wait_ge(gf["yT"], gv(i, l))
                                for t in range(T):
                                    op = nc.tensor.transpose(banks(l, 1)[:, t * P:(t + 1) * P], yT[l][:, t * P:(t + 1) * P],
                                                             ident[:, :])
                                op.then_inc(gf["yTp"], 1)

        stages = [
            lambda: small_attention("A0", False, False, 1.0 / math.sqrt(SMALL_DIM), 0), int8_ffn,
            lambda: small_attention("A1", True, False, 1.0 / math.sqrt(D), 1), routed_ffn,
            lambda: small_attention("A2", True, True, 1.0 / math.sqrt(SMALL_DIM), 2), spectral_ffn]
        stages += [decoder_layer]
        for stage in stages:
            run_stage(stage)
        Y = ctx.enter_context(nc.sbuf_tensor("Y", [P, TILES, D], F32))
        run_stage(lambda: start_stream(Y))
        for lyr in range(DEPTH):
            run_stage(lambda: window_attention(lyr, Y))
            run_stage(lambda: gated_ffn(lyr, Y, lyr == DEPTH - 1))


def host_layout(inputs):
    def rep(v):
        v = np.asarray(v, np.float32)
        return np.broadcast_to(v[None, :], (P, v.shape[0]))

    def block_diagonal(w):
        out = np.zeros((D, D), np.float32)
        for n in range(SMALL_HEADS):
            out[8 * n:8 * n + 8, 8 * n:8 * n + 8] = w
        return out

    p = np.arange(P)
    angle = 2 * np.pi * ((p[:, None] * p[None, :]) % D) / D
    half = np.arange(0, HEAD_DIM, 2, dtype=np.float32)
    inv = (1.0 / 10000.0 ** (half / HEAD_DIM)).astype(np.float32)
    n = (p % SEQ).astype(np.float32)
    freq = (n[:, None] * inv[None, :]).astype(np.float32)
    base = ((half + 0.4 * HEAD_DIM) / (1.4 * HEAD_DIM)).astype(np.float32)
    scale = (base[None, :] ** ((n[:, None] - SEQ // 2) / 32.0).astype(np.float32)).astype(np.float32)
    cos, sin = np.cos(freq), np.sin(freq)
    two = lambda a, b: np.concatenate([a, b], axis=1)
    k = {
        "ident": np.eye(P), "ones": np.ones((P, P)), "tri": p[:, None] <= p[None, :],
        "shift": (p[:, None] + 1 == p[None, :]) & (p[None, :] % SEQ != 0),
        "causal": np.where(np.arange(SEQ)[None, :] > (p % SEQ)[:, None], MASKED, 0.0),
        "head_cols": ((p // 8) % 4)[:, None] == np.arange(4)[None, :],
        "sum_cols": np.concatenate([(np.arange(32) // 8)[None, :] == (2 * m + p // SEQ)[:, None] for m in range(2)], axis=1),
        "tie": np.broadcast_to((EXPERTS - np.arange(EXPERTS))[None, :], (P, EXPERTS)),
        "dft_cos": np.cos(angle), "dft_sin": np.sin(angle),
        "rope": np.concatenate([two(cos, cos) * two(scale, scale) * 8, two(cos, cos) / two(scale, scale),
                                two(-sin, sin) * two(scale, scale) * 8, two(-sin, sin) / two(scale, scale)], axis=1),
    }
    i = inputs
    w = {
        "A0_wo": i["L0_xattn_w_proj"].T, "A0_bo": rep(i["L0_xattn_b_proj"]), "F0_rhsT": i["L0_ffn_rhs"].T,
        "A1_wq": block_diagonal(i["L1_xattn_Wq"].T), "A1_wk": block_diagonal(i["L1_xattn_Wk"].T),
        "A1_wv": block_diagonal(i["L1_xattn_Wv"].T), "A1_wo": i["L1_xattn_Wo"].T, "A1_bo": rep(i["L1_xattn_bo"]),
        "F1_we": np.concatenate([i["L1_ffn_We"], i["L1_ffn_Wg"]], axis=1), "F1_be": rep(i["L1_ffn_be"]),
        "A2_wq": i["L2_xattn_Wq"], "A2_wk": i["L2_xattn_Wk"], "A2_wv": i["L2_xattn_Wv"], "A2_wo": i["L2_xattn_Wo"],
        "A2_bo": rep(i["L2_xattn_bo"]),
        "F2_wr": i["L2_ffn_w_freq_real"], "F2_wi": i["L2_ffn_w_freq_imag"], "F2_bias": rep(i["L2_ffn_bias"]),
        "A3_b2": rep(i["L3_xattn_b2"]), "A3_gamma": rep(i["L3_xattn_gamma"]),
        "A3_beta": rep(i["L3_xattn_beta"]), "A3_w1": i["L3_xattn_W1"], "A3_w2": i["L3_xattn_W2"],
    }
    for m in ("q1", "k1", "v1", "q2", "k2", "v2"):
        w["A3_w" + m] = i["L3_xattn_W" + m]
    cols = {"A2_bq": i["L2_xattn_bq"], "A2_bk": i["L2_xattn_bk"], "A2_bv": i["L2_xattn_bv"], "A3_b1": i["L3_xattn_b1"]}
    for l in range(2):
        f = f"F3_{l}_"
        qs, ks = i["L3_ffn_q_scale"][l], i["L3_ffn_k_scale"][l]
        hd = HEAD_DIM // 2
        swap = lambda v: np.concatenate([v[hd:], v[:hd]])
        w[f + "wqkv"] = i["L3_ffn_wqkv"][l]
        w[f + "scales"] = rep(np.concatenate([qs, ks, swap(qs), swap(ks)]))
        w[f + "wo"] = i["L3_ffn_wo"][l].reshape(4, P, D).transpose(1, 0, 2).reshape(P, 4 * D)
        cols[f + "lg"], cols[f + "lb"], cols[f + "b2"] = i["L3_ffn_ln_g"][l], i["L3_ffn_ln_b"][l], i["L3_ffn_b2"][l]
        w[f + "w1"] = i["L3_ffn_w1"][l]
        b1, w2 = np.zeros((P, 2 * NHC), np.float32), np.zeros((P, NHC, D), np.float32)
        for c, (at, m) in enumerate(HID_CHUNKS):
            b1[:m, c] = i["L3_ffn_b1"][l][at:at + m]
            b1[:m, NHC + c] = i["L3_ffn_b1"][l][HID + at:HID + at + m]
            w2[:m, c] = i["L3_ffn_w2"][l][at:at + m]
        for c in range(2 * NHC):
            cols[f"{f}b1{c}"] = b1[:, c]
        w[f + "w2"] = w2.reshape(P, NHC * D)
    w["columns"] = np.stack([np.asarray(cols[n], np.float32) for n in COLUMNS], axis=1)
    out = np.zeros((P, WEIGHT_COLS), np.float32)
    for name, n in LAYOUT:
        a = OFFSET[name][0]
        out[:, a:a + n] = w[name] if name in w else k[name]
    return out


def kernel(**inputs):
    from concourse import bacc
    from concourse.bass_utils import run_bass_kernel_spmd

    inputs = {n: np.asarray(v) for n, v in inputs.items()}
    tokens = BATCH * SEQ
    arrays = {
        "x_rows": np.ascontiguousarray(inputs["x"].reshape(tokens, D)),
        "ctx_t": np.ascontiguousarray(inputs["ctx_1024"].reshape(tokens, D).T),
        "mask_batch": np.ascontiguousarray(inputs["mask_Bx1xSxS2_ik1"].reshape(tokens, SEQ)),
        "mask_all": np.ascontiguousarray(inputs["mask_1x1xSxS2_if1"].reshape(SEQ, SEQ)),
        "weights": host_layout(inputs),
    }
    nc = bacc.Bacc("TRN2", target_bir_lowering=False, num_devices=1)
    args = [nc.dram_tensor(n, a.shape, mybir.dt.from_np(a.dtype), kind="ExternalInput").ap() for n, a in arrays.items()]
    out = nc.dram_tensor("y_rows", (tokens, D), F32, kind="ExternalOutput").ap()
    transformer_program(nc, *args, out)
    r = run_bass_kernel_spmd(nc, [arrays], core_ids=[0])
    return r.results[0]["y_rows"].reshape(BATCH, SEQ, D)
```

```python
import math
from contextlib import ExitStack

import numpy as np
import concourse.bass as bass
from concourse import mybir

F32 = mybir.dt.float32
BF16 = mybir.dt.bfloat16
I32 = mybir.dt.int32
ALU = mybir.AluOpType
ACT = mybir.ActivationFunctionType
AX = mybir.AxisListType.X

BATCH, SEQ, D = 128, 64, 128
P = 128
TILES = BATCH * SEQ // P
T = 4
ROWS = T * P
NB = ROWS // SEQ
GROUPS = TILES // T
LANES = 2
STEPS = GROUPS // LANES
WIDE = 4
WIDE_STEPS = GROUPS // WIDE
SMALL_HEADS, SMALL_DIM = 16, 8
Q4 = 4
HEADS, HEAD_DIM = 8, 64
INNER = HEADS * HEAD_DIM
DEPTH = 2
HID = int(D * 4 * 2 / 3)
HID_CHUNKS = [(c, min(P, HID - c)) for c in range(0, HID, P)]
NHC = len(HID_CHUNKS)
EXPERTS = 8
CAPACITY = BATCH * SEQ // EXPERTS
MASKED = -1.0e30
ROUND = 12582912.0
INT8_MAX = 127.0
RSQRT_SEED = float(0x5F3759DF)

COLUMNS = ["A2_bq", "A2_bk", "A2_bv", "A3_b1"]
for _l in range(2):
    COLUMNS += [f"F3_{_l}_lg", f"F3_{_l}_lb", f"F3_{_l}_b2"] + [f"F3_{_l}_b1{_k}" for _k in range(2 * NHC)]
LAYOUT = [
    ("columns", len(COLUMNS)),
    ("ident", P), ("ones", P), ("tri", P), ("shift", P), ("causal", SEQ), ("head_cols", Q4),
    ("tie", EXPERTS),
    ("A0_wo", D), ("A0_bo", D),
    ("F0_rhsT", D),
    ("A1_wq", D), ("A1_wk", D), ("A1_wv", D), ("A1_wo", D), ("A1_bo", D),
    ("F1_we", D + EXPERTS), ("F1_be", D),
    ("A2_wq", D), ("A2_wk", D), ("A2_wv", D), ("A2_wo", D), ("A2_bo", D),
    ("F2_wr", D), ("F2_wi", D), ("F2_bias", D), ("dft_cos", D), ("dft_sin", D),
    ("A3_wq1", D), ("A3_wk1", D), ("A3_wv1", D), ("A3_wq2", D), ("A3_wk2", D), ("A3_wv2", D),
    ("A3_w1", D), ("A3_w2", D), ("A3_b2", D), ("A3_gamma", D), ("A3_beta", D),
    ("rope", 4 * HEAD_DIM),
]
for _l in range(2):
    LAYOUT += [(f"F3_{_l}_wqkv", 3 * INNER), (f"F3_{_l}_scales", 4 * HEAD_DIM), (f"F3_{_l}_wo", 4 * D),
               (f"F3_{_l}_w1", 2 * HID), (f"F3_{_l}_w2", NHC * D)]
OFFSET, _at = {}, 0
for _name, _n in LAYOUT:
    OFFSET[_name] = (_at, _n)
    _at += _n
WEIGHT_COLS = _at
FIRST_COLS = OFFSET["A1_wq"][0]
EARLY_COLS = OFFSET["rope"][0]


def transformer_program(nc, x, ctxT, mask1, mask2, weights, out):
    ctx = ExitStack()
    with ctx:
        def keep(name):
            return ctx.enter_context(nc.semaphore(name))

        stage_sems, stages_run = [], [0]

        def sem(name):
            s = nc.alloc_semaphore(name=f"{name}_{stages_run[0]}")
            stage_sems.append(s)
            return s

        X = ctx.enter_context(nc.sbuf_tensor("X", [P, TILES, D], F32))
        ident = ctx.enter_context(nc.sbuf_tensor("ident", [P, P], F32))
        ident_bf = ctx.enter_context(nc.sbuf_tensor("ident_bf", [P, P], BF16))
        causal_bf = ctx.enter_context(nc.sbuf_tensor("causal_bf", [P, SEQ], BF16))
        columns = ctx.enter_context(nc.sbuf_tensor("columns", [P, len(COLUMNS)], F32))
        mhalf = ctx.enter_context(nc.sbuf_tensor("mhalf", [P, 1], F32))
        st = [ctx.enter_context(nc.sbuf_tensor(f"st{l}", [P, T, 6], F32)) for l in range(WIDE)]
        mv = [ctx.enter_context(nc.sbuf_tensor(f"mv{l}", [P, T, 2], F32)) for l in range(WIDE)]
        ve = [ctx.enter_context(nc.sbuf_tensor(f"ve{l}", [P, T], F32)) for l in range(WIDE)]
        rstd = [ctx.enter_context(nc.sbuf_tensor(f"rstd{l}", [P, T], F32)) for l in range(WIDE)]
        h = [ctx.enter_context(nc.sbuf_tensor(f"h{l}", [P, T, D], F32)) for l in range(WIDE)]
        hT = [ctx.enter_context(nc.sbuf_tensor(f"hT{l}", [P, ROWS], F32)) for l in range(WIDE)]
        PS = ctx.enter_context(nc.psum_tensor("PS", [P, 8, 512], F32))

        def banks(l, k, n=1):
            return PS[:, 4 * l + k:4 * l + k + n, :].rearrange("p b c -> p (b c)")

        def wide_banks(l, k, n=1):
            return PS[:, 2 * l + k:2 * l + k + n, :].rearrange("p b c -> p (b c)")

        loads = [0]
        loaded = keep("loaded")
        ticks = {e: keep(f"tick_{e}") for e in ("pe", "act", "dve", "pool", "sp")}

        def hold(eng, name, s, v):
            eng.wait_ge(s, v)
            eng.sem_inc(ticks[name], 1)

        def load(sp, dst, name, first=0, n=None):
            a, cols = OFFSET[name]
            n = cols if n is None else n
            sp.dma_start(dst, weights[:, a + first:a + first + n]).then_inc(loaded, 16)
            loads[0] += 16

        early_stages = ExitStack()
        early = early_stages.enter_context(nc.sbuf_tensor("early", [P, EARLY_COLS], F32))
        rest_loaded = keep("rest_loaded")
        x_loaded = [keep("x_first_loaded"), keep("x_rest_loaded")]

        def constant(name):
            a, cols = OFFSET[name]
            return early[:, a:a + cols]

        def column(name, k=None):
            at = COLUMNS.index(name if k is None else f"{name}{k}")
            return columns[:, at:at + 1]

        def wide_rows(t, i, l):
            return t[:, bass.ds(WIDE * T * i + T * l, T), :]

        def wide_row(t, i, l, k):
            return t[:, bass.ds(WIDE * T * i + (T * l + k), 1), :].rearrange("p a c -> p (a c)")

        with nc.Block() as block:
            @block.sync
            def _(sp):
                load(sp, ident[:, :], "ident")
                load(sp, columns[:, :], "columns")
                sp.dma_start(early[:, 0:FIRST_COLS], weights[:, 0:FIRST_COLS]).then_inc(loaded, 16)
                loads[0] += 16
                for part, tiles in enumerate((slice(0, T * T), slice(T * T, TILES))):
                    sp.dma_start(X[:, tiles, :], x[P * tiles.start:P * tiles.stop, :].rearrange("(t p) c -> p t c", p=P)
                                 ).then_inc(x_loaded[part], 16)
                sp.dma_start(early[:, FIRST_COLS:EARLY_COLS], weights[:, FIRST_COLS:EARLY_COLS]).then_inc(rest_loaded, 16)
                sp.wait_ge(loaded, loads[0])

        base_ready = keep("base_ready")
        with nc.Block() as block:
            @block.vector
            def _(dve):
                nc.vector.memset(mhalf[:, :], -0.5)
                nc.vector.tensor_copy(ident_bf[:, :], ident[:, :])
                nc.vector.tensor_copy(causal_bf[:, :], constant("causal")[:, 0:SEQ]).then_inc(base_ready, 1)
                dve.wait_ge(base_ready, 1)

        ln = {}

        def run_stage(stage):
            ln.update({n: sem("ln_" + n) for n in ("bn", "var", "ve", "rstd", "norm", "hTp", "hT")})
            stage()
            with nc.Block() as block:
                @block.gpsimd
                def _(pool):
                    nc.clear_and_free_semaphores(stage_sems)
            stage_sems.clear()
            stages_run[0] += 1

        def ln_stats(dve, v, l, src, ev=ln):
            for t in range(T):
                op = nc.vector.bn_stats(st[l][:, t, :], src(t))
            op.then_inc(ev["bn"], 1)
            hold(dve, "dve", ev["bn"], v)
            for t in range(T):
                op = nc.vector.bn_aggr(mv[l][:, t, :], st[l][:, t, :])
            op.then_inc(ev["var"], 1)

        def ln_rstd(pool, v, l, eps, ev=ln):
            hold(pool, "pool", ev["var"], v)
            nc.gpsimd.tensor_scalar(ve[l][:, :], mv[l][:, :, 1], 1.0, eps, ALU.mult, ALU.add).then_inc(ev["ve"], 1)
            pool.wait_ge(ev["ve"], v)
            nc.gpsimd.tensor_tensor(rstd[l][:, :], ve[l][:, :], mhalf[:, 0:1].to_broadcast([P, T]), ALU.pow
                                    ).then_inc(ev["rstd"], 1)

        def ln_norm(dve, v, l, src, dst, ev=ln):
            hold(dve, "dve", ev["rstd"], v)
            for t in range(T):
                op = nc.vector.tensor_scalar(dst(t), src(t), mv[l][:, t, 0:1], rstd[l][:, t:t + 1],
                                             ALU.subtract, ALU.mult)
            op.then_inc(ev["norm"], 1)

        def transposes(dst, src):
            for t in range(T):
                op = nc.tensor.transpose(dst[:, t * P:(t + 1) * P], src[:, t, :], ident[:, :])
            return op


        def exists(i, k, unit, count):
            return not isinstance(i, int) or 0 <= unit * i + k < count

        def tile_exists(i, k):
            return exists(i, k, 2 * T, TILES)

        def group_exists(i, m):
            return exists(i, m, 2, GROUPS)

        def run_steps(eng, steps, step, lag=0):
            for i in range(-2, 1 + lag):
                for n in range(steps):
                    step(i, n)
            with eng.Fori(1 + lag, STEPS - 2) as i:
                for n in range(steps):
                    step(i, n)
            for i in range(STEPS - 2, STEPS + 1 + lag):
                for n in range(steps):
                    step(i, n)

        def gv(i, m):
            return 2 * i + (m + 1)

        def group_rows(t, i, m):
            return t[:, bass.ds(2 * T * i + T * m, T), :]

        def group_row(t, i, m, k):
            return t[:, bass.ds(2 * T * i + (T * m + k), 1), :].rearrange("p a c -> p (a c)")


        def bf(ap):
            return ap.bitcast(BF16)

        def quantised_weights(i8, sb):
            rhsT, ones = constant("F0_rhsT"), constant("ones")
            ws, wr = sb("ws", [P, 1]), sb("wr", [P, 1])
            wdiag, wqf, wqT = sb("wdiag", [P, P]), sb("wqf", [P, D]), sb("wqT", [P, D], BF16)
            wq, wscale = sb("wq8", [P, D], BF16), sb("wscale", [P, D])
            with nc.Block() as block:
                @block.vector
                def _(dve):
                    nc.vector.tensor_reduce(ws[:, :], rhsT[:, :], op=ALU.max, axis=AX, apply_absolute_value=True
                                            ).then_inc(i8["w"], 1)
                    dve.wait_ge(i8["w"], 1)
                    nc.vector.tensor_scalar(ws[:, :], ws[:, :], 1e-12, 1.0 / INT8_MAX, ALU.max, ALU.mult
                                            ).then_inc(i8["w"], 1)
                    dve.wait_ge(i8["w"], 2)
                    nc.vector.reciprocal(wr[:, :], ws[:, :])
                    nc.vector.tensor_scalar(wdiag[:, :], ident[:, :], ws[:, 0:1], None, ALU.mult).then_inc(i8["w"], 1)
                    dve.wait_ge(i8["w"], 3)
                    nc.vector.tensor_scalar(wqf[:, :], rhsT[:, :], wr[:, 0:1], ROUND, ALU.mult, ALU.add
                                            ).then_inc(i8["w"], 1)
                    dve.wait_ge(i8["w"], 4)
                    nc.vector.tensor_scalar(wqf[:, :], wqf[:, :], ROUND + INT8_MAX, ROUND - INT8_MAX, ALU.min, ALU.max
                                            ).then_inc(i8["w"], 1)
                    dve.wait_ge(i8["w"], 5)
                    nc.vector.tensor_scalar(wqT[:, :], wqf[:, :], ROUND, None, ALU.subtract).then_inc(i8["w"], 1)
                    dve.wait_ge(i8["w"], 8)
                    nc.vector.tensor_copy(wq[:, :], bf(PS[:, 0, 0:64]))
                    nc.vector.tensor_copy(wscale[:, :], PS[:, 1, 0:D]).then_inc(i8["w"], 1)
                    dve.wait_ge(i8["w"], 9)

                @block.tensor
                def _(pe):
                    pe.wait_ge(i8["w"], 6)
                    nc.tensor.transpose(bf(PS[:, 0, 0:64]), wqT[:, :], ident_bf[:, :]).then_inc(i8["w"], 1)
                    nc.tensor.matmul(PS[:, 1, 0:D], ones[:, :], wdiag[:, :], start=True, stop=True
                                     ).then_inc(i8["w"], 1)
            return wq, wscale


        def spectral_matrix(sf, sb):
            wr, wi, co, si = (constant(n) for n in ("F2_wr", "F2_wi", "dft_cos", "dft_sin"))
            sn, at, bt, m = (sb(n, [P, D]) for n in ("sn", "at", "bt", "m"))
            with nc.Block() as block:
                @block.tensor
                def _(pe):
                    pe.wait_ge(sf["a"], 1)
                    nc.tensor.matmul(PS[:, 0, 0:D], wr[:, :], co[:, :], start=True, stop=False)
                    nc.tensor.matmul(PS[:, 0, 0:D], wi[:, :], si[:, :], start=False, stop=True)
                    nc.tensor.matmul(PS[:, 1, 0:D], wr[:, :], si[:, :], start=True, stop=False)
                    nc.tensor.matmul(PS[:, 1, 0:D], wi[:, :], sn[:, :], start=False, stop=True).then_inc(sf["p1"], 1)
                    pe.wait_ge(sf["a"], 2)
                    nc.tensor.matmul(PS[:, 2, 0:D], at[:, :], co[:, :], start=True, stop=False)
                    nc.tensor.matmul(PS[:, 2, 0:D], bt[:, :], si[:, :], start=False, stop=True).then_inc(sf["p2"], 1)

                @block.vector
                def _(dve):
                    nc.vector.tensor_scalar(sn[:, :], co[:, :], -1.0, None, ALU.mult).then_inc(sf["a"], 1)
                    dve.wait_ge(sf["p1"], 1)
                    nc.vector.tensor_copy(at[:, :], PS[:, 0, 0:D])
                    nc.vector.tensor_copy(bt[:, :], PS[:, 1, 0:D]).then_inc(sf["a"], 1)
                    dve.wait_ge(sf["p2"], 1)
                    nc.vector.tensor_scalar(m[:, :], PS[:, 2, 0:D], 1.0 / D, None, ALU.mult).then_inc(sf["b"], 1)
                    dve.wait_ge(sf["b"], 1)
            return m


        def small_attention(name, project, biased, score_scale, mask_kind, int8=False, spectral=False):
            sa_mk = [sem(f"sa_mask{l}") for l in range(LANES)]
            sa_ready = sem("sa_ready")
            sa_cg = [sem(f"sa_context{l}") for l in range(LANES)]
            sa = {n: sem("sa_" + n) for n in (
                "kvp", "kT", "vT", "kb", "vdp", "vb", "qp", "q", "bias", "scores", "max", "sub",
                "exp", "sum", "rec", "pn", "ptp", "pt", "av", "o", "out", "ob", "X", "mask")}
            if int8:
                i8 = {n: sem("i8_" + n) for n in ("w", "amax", "scale", "rec", "round", "clip", "q", "qTp", "qT", "acc",
                                                  "ac", "tmp", "X")}
            if spectral:
                sf = {n: sem("sf_" + n) for n in ("p1", "a", "p2", "b", "bias", "hTp", "hT", "out", "ac", "X")}
            if int8 or spectral:
                lnf = {n: sem("lnf_" + n) for n in ("bn", "var", "ve", "rstd", "norm")}
            with ExitStack() as c:
                def sb(n, shape, dt=F32):
                    return c.enter_context(nc.sbuf_tensor(f"{name}_{n}", shape, dt))
                wo, bo, head_cols = constant(f"{name}_wo"), constant(f"{name}_bo"), constant("head_cols")
                if project:
                    wq, wk, wv = (constant(f"{name}_{n}") for n in ("wq", "wk", "wv"))
                bq, bk, bv = (column(f"{name}_{n}") if biased else 0.0 for n in ("bq", "bk", "bv"))
                lanes = range(LANES)
                xb = [sb(f"xb{l}", [P, 2, D]) for l in lanes]
                ob = [sb(f"ob{l}", [P, 2, D]) for l in lanes]
                cg = [sb(f"cg{l}", [P, ROWS]) for l in lanes]
                kT = [sb(f"kT{l}", [P, ROWS]) if project else cg[l] for l in lanes]
                vT = [sb(f"vT{l}", [P, NB, 2, SEQ]) for l in lanes]
                kb = [sb(f"kb{l}", [P, NB, Q4, SEQ]) for l in lanes]
                vb = [sb(f"vb{l}", [P, NB, 8, 32]) for l in lanes]
                qT = [sb(f"qT{l}", [P, ROWS]) if project else hT[l] for l in lanes]
                pr = [sb(f"pr{l}", [P, 2048]) for l in lanes]
                pT = sb("pT", [P, 2, 8, P])
                mx, sums = sb("mx", [P, 32]), sb("sums", [P, 32])
                rec = [sb(f"rec{l}", [P, 32]) for l in lanes]
                oT = [sb(f"oT{l}", [P, 2 * P]) for l in lanes]
                if mask_kind == 1:
                    nm = [sb(f"nm{l}", [P, T, SEQ], BF16) for l in lanes]
                    mraw = [sb(f"mraw{l}", [P, T, SEQ], I32) for l in lanes]
                elif mask_kind == 2:
                    nm = sb("nm", [P, SEQ], BF16)
                    mraw = sb("mraw", [P, SEQ], I32)

                if int8:
                    wq8, wscale = quantised_weights(i8, sb)
                    am, rc = sb("am", [P, T]), sb("rc", [P, T])
                    sc = [sb(f"sc{l}", [P, T]) for l in lanes]
                    qr, tmp, ac = (sb(n, [P, T, D]) for n in ("qr", "tmp", "ac"))
                    qb, qT8 = sb("qb", [P, T, D], BF16), sb("qT8", [P, ROWS], BF16)

                if spectral:
                    M, bias = spectral_matrix(sf, sb), constant("F2_bias")
                    ac = sb("ac", [P, T, D])

                def seen(mask, ones):
                    return nc.vector.tensor_scalar(mask, ones, 0.0, MASKED, ALU.is_equal, ALU.mult).then_inc(sa["mask"], 1)

                with nc.Block() as block:
                    @block.gpsimd
                    def _(pool):
                        for l in lanes:
                            op = nc.gpsimd.memset(vb[l][:, :, :, :], 0.0)
                        op.then_inc(sa_ready, 1)
                        pool.wait_ge(sa_ready, 1)

                    if mask_kind == 2:
                        @block.sync
                        def _(sp):
                            for b in range(2):
                                sp.dma_start(mraw[SEQ * b:SEQ * (b + 1), :], mask2).then_inc(loaded, 16)
                                loads[0] += 16

                        @block.vector
                        def _(dve):
                            dve.wait_ge(loaded, loads[0])
                            seen(nm[:, :], mraw[:, :])
                            dve.wait_ge(sa["mask"], 1)

                HALVES = 4
                SC = PS[:, 0:4, :].rearrange("p b c -> p (b c)")
                PTP = PS[:, 4:8, :].rearrange("p b c -> p (b c)")
                O = PS[:, 4, 0:2 * P]
                OUT = PS[:, 3, 0:2 * P]
                VD = PS[:, 5, :]
                KP = HP = PS[:, 6, :]
                VP = QP = PS[:, 7, :]
                I8 = PS[:, 7, :]

                def half_exists(i, k):
                    return exists(i, k, HALVES, 2 * GROUPS)

                def hv(i, k):
                    return HALVES * i + (k + 1)

                def half_rows(t, i, k):
                    return t[:, bass.ds(2 * T * i + 2 * k, 2), :]

                def loaded_for(sems, i, m):
                    return sems[m % 2], 16 * i + 16 * (m // 2 + 1)

                with nc.Block() as block:
                    @block.sync
                    def _(sp):
                        def load_group(i, l):
                            rows = bass.ds(2 * ROWS * i + ROWS * l, ROWS)
                            if mask_kind == 1:
                                sp.dma_start(mraw[l][:, :, :], mask1[rows, :].rearrange("(t p) k -> p t k", p=P)
                                             ).then_inc(sa_mk[l], 16)
                            sp.dma_start(cg[l][:, :], ctxT[:, rows]).then_inc(sa_cg[l], 16)

                        for l in lanes:
                            load_group(0, l)
                        with sp.Fori(1, STEPS) as i:
                            for l in lanes:
                                for event in ("kvp",) if project else ("kb", "vT"):
                                    hold(sp, "sp", sa[event], 2 * i + (l - 1))
                                if mask_kind == 1:
                                    hold(sp, "sp", sa["mask"], 2 * i + (l - 1))
                                load_group(i, l)
                        if name == "A0":
                            sp.wait_ge(rest_loaded, 16)

                    @block.gpsimd
                    def _(pool):
                        def step(i, n):
                            m, odd = divmod(n, 2)
                            if spectral and not odd and group_exists(i, m - 3):
                                hold(pool, "pool", lnf["norm"], gv(i, m - 3))
                                nc.gpsimd.tensor_tensor(group_rows(X, i, m - 3), group_rows(X, i, m - 3),
                                                        bias.unsqueeze(1).to_broadcast([P, T, D]), ALU.add
                                                        ).then_inc(sf["bias"], 1)
                            if (int8 or spectral) and odd and group_exists(i, m - 2):
                                ln_rstd(pool, gv(i, m - 2), 2 + m % 2, 1e-5, lnf)
                            if not odd and group_exists(i, m + 2):
                                ln_rstd(pool, gv(i, m + 2), (m + 2) % 2, 1e-5)
                            if not odd and group_exists(i, m + 1):
                                l = (m + 1) % 2
                                if project:
                                    hold(pool, "pool", sa["kT"], gv(i, m + 1))
                                else:
                                    hold(pool, "pool", *loaded_for(sa_cg, i, m + 1))
                                for j in range(Q4):
                                    op = nc.gpsimd.tensor_scalar(
                                        kb[l][:, :, j, :], kT[l][:, :].rearrange("p (b k) -> p b k", b=NB),
                                        bk, head_cols[:, j:j + 1], ALU.add, ALU.mult)
                                op.then_inc(sa["kb"], 1)
                            if half_exists(i, n - 2):
                                if half_exists(i, n - 4):
                                    hold(pool, "pool", sa["X"], hv(i, n - 4))
                                nc.gpsimd.tensor_tensor(xb[n % 2][:, :, :], half_rows(X, i, n - 2),
                                                        bo[:, :].unsqueeze(1).to_broadcast([P, 2, D]), ALU.add
                                                        ).then_inc(sa["bias"], 1)
                            if half_exists(i, n):
                                q = pr[n % 2][:, :].rearrange("p (n k) -> p n k", k=SEQ)
                                hold(pool, "pool", sa["rec"], hv(i, n))
                                nc.gpsimd.tensor_tensor(q, q, rec[n % 2][:, :].unsqueeze(2).to_broadcast([P, 32, SEQ]),
                                                        ALU.mult).then_inc(sa["pn"], 1)

                        run_steps(pool, HALVES, step, lag=int(int8 or spectral))

                    @block.vector
                    def _(dve):
                        def quantise(i, m):
                            l, v = m % 2, gv(i, m)
                            hb = h[2 + l]
                            ln_norm(dve, v, 2 + l, lambda t: group_row(X, i, m, t), lambda t: hb[:, t, :], lnf)
                            dve.wait_ge(lnf["norm"], v)
                            nc.vector.tensor_reduce(am[:, :], hb[:, :, :], op=ALU.max, axis=AX, apply_absolute_value=True
                                                    ).then_inc(i8["amax"], 1)
                            dve.wait_ge(i8["amax"], v)
                            nc.vector.tensor_scalar(sc[l][:, :], am[:, :], 1e-12, 1.0 / INT8_MAX, ALU.max, ALU.mult
                                                    ).then_inc(i8["scale"], 1)
                            dve.wait_ge(i8["scale"], v)
                            nc.vector.reciprocal(rc[:, :], sc[l][:, :]).then_inc(i8["rec"], 1)
                            dve.wait_ge(i8["rec"], v)
                            for t in range(T):
                                op = nc.vector.tensor_scalar(qr[:, t, :], hb[:, t, :], rc[:, t:t + 1], ROUND,
                                                             ALU.mult, ALU.add)
                            op.then_inc(i8["round"], 1)
                            dve.wait_ge(i8["round"], v)
                            nc.vector.tensor_scalar(qr[:, :, :], qr[:, :, :], ROUND + INT8_MAX, ROUND - INT8_MAX,
                                                    ALU.min, ALU.max).then_inc(i8["clip"], 1)
                            dve.wait_ge(i8["clip"], v)
                            if group_exists(i, m - 1):
                                hold(dve, "dve", i8["qTp"], gv(i, m - 1))
                            nc.vector.tensor_scalar(qb[:, :, :], qr[:, :, :], ROUND, None, ALU.subtract
                                                    ).then_inc(i8["q"], 1)

                        def dequantise(i, m):
                            v = gv(i, m)
                            hold(dve, "dve", i8["ac"], v)
                            if group_exists(i, m - 1):
                                hold(dve, "dve", i8["X"], gv(i, m - 1))
                            for t in range(T):
                                op = nc.vector.scalar_tensor_tensor(tmp[:, t, :], ac[:, t, :], sc[m % 2][:, t:t + 1],
                                                                    wscale[:, :], ALU.mult, ALU.mult)
                            op.then_inc(i8["tmp"], 1)
                            hold(dve, "dve", i8["tmp"], v)
                            nc.vector.tensor_tensor(group_rows(X, i, m), group_rows(X, i, m), tmp[:, :, :], ALU.add
                                                    ).then_inc(i8["X"], 1)

                        def step(i, n):
                            m, odd = divmod(n, 2)
                            if half_exists(i, n):
                                q, v = n % 2, hv(i, n)
                                S, R = (t.rearrange("p (n k) -> p n k", k=SEQ) for t in (SC, pr[q][:, :]))
                                dve.wait_ge(sa["scores"], v)
                                nc.vector.tensor_reduce(mx[:, :], S, op=ALU.max, axis=AX).then_inc(sa["max"], 1)
                                dve.wait_ge(sa["max"], v)
                                nc.vector.tensor_tensor(R, S, mx[:, :].unsqueeze(2).to_broadcast([P, 32, SEQ]),
                                                        ALU.subtract).then_inc(sa["sub"], 1)
                            k = n - 3
                            if half_exists(i, k):
                                hold(dve, "dve", sa["bias"], hv(i, k))
                                hold(dve, "dve", sa["ob"], hv(i, k))
                                nc.vector.tensor_tensor(half_rows(X, i, k), ob[k % 2][:, :, :], xb[k % 2][:, :, :], ALU.add
                                                        ).then_inc(sa["X"], 1)
                            if not odd and mask_kind == 1 and group_exists(i, m + 1):
                                l = (m + 1) % 2
                                hold(dve, "dve", *loaded_for(sa_mk, i, m + 1))
                                seen(nm[l][:, :, :], mraw[l][:, :, :])
                            if odd and group_exists(i, m + 3):
                                if name == "A0" and isinstance(i, int) and 2 * i + m + 3 == 0:
                                    dve.wait_ge(x_loaded[0], 16)
                                if name == "A0" and isinstance(i, int) and 2 * i + m + 3 == T:
                                    dve.wait_ge(x_loaded[1], 16)
                                ln_stats(dve, gv(i, m + 3), (m + 3) % 2, lambda t: group_row(X, i, m + 3, t))
                            if not odd and group_exists(i, m + 2):
                                ln_norm(dve, gv(i, m + 2), m % 2, lambda t: group_row(X, i, m + 2, t),
                                        lambda t: h[m % 2][:, t, :])
                            if int8 or spectral:
                                if not odd and group_exists(i, m - 2):
                                    hold(dve, "dve", sa["X"], hv(i, 2 * m - 3))
                                    ln_stats(dve, gv(i, m - 2), 2 + m % 2, lambda t: group_row(X, i, m - 2, t), lnf)
                                if odd and group_exists(i, m - 2):
                                    if int8:
                                        quantise(i, m - 2)
                                    else:
                                        ln_norm(dve, gv(i, m - 2), 2 + m % 2, lambda t: group_row(X, i, m - 2, t),
                                                lambda t: h[2 + m % 2][:, t, :], lnf)
                                if not odd and group_exists(i, m - 4):
                                    if int8:
                                        dequantise(i, m - 4)
                                    else:
                                        hold(dve, "dve", sf["bias"], gv(i, m - 4))
                                        hold(dve, "dve", sf["ac"], gv(i, m - 4))
                                        nc.vector.tensor_tensor(group_rows(X, i, m - 4), group_rows(X, i, m - 4),
                                                                ac[:, :, :], ALU.add).then_inc(sf["X"], 1)
                            if half_exists(i, n):
                                dve.wait_ge(sa["exp"], v)
                                nc.vector.tensor_reduce(sums[:, :], R, op=ALU.add, axis=AX).then_inc(sa["sum"], 1)
                                dve.wait_ge(sa["sum"], v)
                                nc.vector.reciprocal(rec[q][:, :], sums[:, :]).then_inc(sa["rec"], 1)

                        run_steps(dve, HALVES, step, lag=int(int8 or spectral))

                    @block.scalar
                    def _(act):
                        def step(i, n):
                            m, odd = divmod(n, 2)
                            k = n - 3
                            if half_exists(i, k):
                                act.wait_ge(sa["out"], hv(i, k))
                                if half_exists(i, k - 2):
                                    act.wait_ge(sa["X"], hv(i, k - 2))
                                nc.scalar.activation(ob[k % 2][:, :, :].rearrange("p t c -> p (t c)"), OUT, ACT.Copy
                                                     ).then_inc(sa["ob"], 1)
                            k = n - 2
                            if half_exists(i, k):
                                act.wait_ge(sa["ptp"], hv(i, k))
                                nc.scalar.activation(pT[:, :, :, :].rearrange("p t n q -> p (t n q)"), PTP, ACT.Copy
                                                     ).then_inc(sa["pt"], 1)
                            if spectral and not odd and group_exists(i, m - 3):
                                act.wait_ge(sf["hTp"], gv(i, m - 3))
                                nc.scalar.activation(hT[2][:, :], PS[:, 4, :], ACT.Copy).then_inc(sf["hT"], 1)
                            if spectral and odd and group_exists(i, m - 3):
                                act.wait_ge(sf["out"], gv(i, m - 3))
                                if group_exists(i, m - 4):
                                    act.wait_ge(sf["X"], gv(i, m - 4))
                                nc.scalar.activation(ac[:, :, :].rearrange("p t c -> p (t c)"), PS[:, 4, :], ACT.Copy
                                                     ).then_inc(sf["ac"], 1)
                            k = n + 1
                            if half_exists(i, k):
                                act.wait_ge(sa["vdp"], hv(i, k))
                                l, b = k // 2 % 2, slice(4 * (k % 2), 4 * (k % 2) + 4)
                                for head in range(4):
                                    r = slice(SEQ * (head % 2), SEQ * (head % 2 + 1))
                                    src = VD[r, :].rearrange("p (n q d) -> p n q d", q=4, d=8)[:, :, head, :]
                                    dst = vb[l][r, b, :, :].rearrange("p b t c -> p (b t c)").rearrange(
                                        "p (n q c) -> p n q c", q=2, c=32)[:, :, head // 2, 8 * head:8 * head + 8]
                                    op = nc.scalar.activation(dst, src, ACT.Copy)
                                op.then_inc(sa["vb"], 1)
                            if not odd and group_exists(i, m + 1):
                                l = (m + 1) % 2
                                twice = vT[l][:, :, :, :]
                                v_in = lambda t: t.rearrange("p (b k) -> p b k", b=NB).unsqueeze(2).to_broadcast([P, NB, 2, SEQ])
                                if project:
                                    act.wait_ge(sa["kvp"], gv(i, m + 1))
                                    nc.scalar.activation(kT[l][:, :], KP, ACT.Copy).then_inc(sa["kT"], 1)
                                    nc.scalar.activation(twice, v_in(VP), ACT.Identity, bias=bv).then_inc(sa["vT"], 1)
                                else:
                                    act.wait_ge(*loaded_for(sa_cg, i, m + 1))
                                    act.wait_ge(sa["vdp"], hv(i, n + 1))
                                    nc.scalar.activation(twice, v_in(cg[l][:, :]), ACT.Copy).then_inc(sa["vT"], 1)
                            if odd and group_exists(i, m + 2):
                                act.wait_ge(ln["hTp"], gv(i, m + 2))
                                nc.scalar.activation(hT[m % 2][:, :], HP, ACT.Copy).then_inc(ln["hT"], 1)
                            if odd and project and group_exists(i, m + 1):
                                act.wait_ge(sa["qp"], gv(i, m + 1))
                                nc.scalar.activation(qT[(m + 1) % 2][:, :], QP, ACT.Identity, bias=bq).then_inc(sa["q"], 1)
                            k = n - 2
                            if int8 and not odd and group_exists(i, m - 3):
                                act.wait_ge(i8["qTp"], gv(i, m - 3))
                                nc.scalar.activation(qT8[:, :], bf(I8[:, 0:ROWS // 2]), ACT.Copy).then_inc(i8["qT"], 1)
                            if int8 and odd and group_exists(i, m - 3):
                                act.wait_ge(i8["acc"], gv(i, m - 3))
                                if group_exists(i, m - 4):
                                    act.wait_ge(i8["tmp"], gv(i, m - 4))
                                nc.scalar.activation(ac[:, :, :].rearrange("p t c -> p (t c)"), I8, ACT.Copy
                                                     ).then_inc(i8["ac"], 1)
                            if half_exists(i, k):
                                act.wait_ge(sa["av"], hv(i, k))
                                nc.scalar.activation(oT[k % 2][:, :], O, ACT.Copy).then_inc(sa["o"], 1)
                            if half_exists(i, n):
                                act.wait_ge(sa["sub"], hv(i, n))
                                nc.scalar.activation(pr[n % 2][:, :], pr[n % 2][:, :], ACT.Exp, scale=score_scale
                                                     ).then_inc(sa["exp"], 1)

                        run_steps(act, HALVES, step, lag=int(int8 or spectral))

                    @block.tensor
                    def _(pe):
                        def project_output(i, k):
                            pe.wait_ge(sa["o"], hv(i, k))
                            if half_exists(i, k + 2):
                                hold(pe, "pe", sa["sub"], hv(i, k + 2))
                            for t in range(2):
                                op = nc.tensor.matmul(OUT[:, t * P:(t + 1) * P], oT[k % 2][:, t * P:(t + 1) * P],
                                                      wo[:, :], start=True, stop=True)
                            op.then_inc(sa["out"], 1)

                        def transpose_probabilities(i, k):
                            pe.wait_ge(sa["pn"], hv(i, k))
                            for c in [*range(4, 16), *range(4)]:
                                if c == 0 and half_exists(i, k - 1):
                                    project_output(i, k - 1)
                                t, pair = divmod(c, 8)
                                op = nc.tensor.transpose(
                                    PTP[:, c * P:(c + 1) * P],
                                    pr[k % 2][:, :].rearrange("p (r t m c) -> p r t m c", r=Q4, t=2, m=2)[
                                        :, pair // 2, t, pair % 2, :], ident[:, :])
                            op.then_inc(sa["ptp"], 1)

                        def small_products_are_read(i, n):
                            m, odd = divmod(n, 2)
                            if half_exists(i, n + 1):
                                hold(pe, "pe", sa["vb"], hv(i, n + 1))
                            if not odd and project and group_exists(i, m + 1):
                                hold(pe, "pe", sa["vT"], gv(i, m + 1))
                            if odd and group_exists(i, m + 2):
                                hold(pe, "pe", ln["hT"], gv(i, m + 2))
                            if odd and project and group_exists(i, m + 1):
                                hold(pe, "pe", sa["q"], gv(i, m + 1))
                            if int8 and group_exists(i, m - 3):
                                hold(pe, "pe", i8["ac" if odd else "qT"], gv(i, m - 3))

                        def projection_is_read(i, n, r, t):
                            if r == 3 and t == 0 and half_exists(i, n - 3):
                                hold(pe, "pe", sa["ob"], hv(i, n - 3))

                        def scores(i, n):
                            m, half = divmod(n, 2)
                            l = m % 2
                            if half == 0:
                                hold(pe, "pe", sa["q"] if project else ln["hT"], gv(i, m))
                                hold(pe, "pe", sa["kb"], gv(i, m))
                                if mask_kind == 1:
                                    hold(pe, "pe", sa["mask"], gv(i, m))
                            if half_exists(i, n - 1):
                                hold(pe, "pe", sa["sub"], hv(i, n - 1))
                            for r in range(Q4):
                                bank = PS[:, r, :].rearrange("p (t n k) -> p t n k", t=2, n=Q4)
                                if mask_kind:
                                    if mask_kind == 1:
                                        mask = nm[l][:, 2 * half:2 * half + 2, :].unsqueeze(2)
                                    else:
                                        mask = nm[:, :].unsqueeze(1).unsqueeze(1)
                                    projection_is_read(i, n, r, 0)
                                    nc.tensor.matmul(bank, ident_bf[:, :], mask.to_broadcast([P, 2, Q4, SEQ]),
                                                     start=True, stop=False, skip_group_check=True)
                            for t in range(2):
                                for r in range(Q4):
                                    bank = PS[:, r, :].rearrange("p (t c) -> p t c", t=2)
                                    if not mask_kind:
                                        projection_is_read(i, n, r, t)
                                    for b in range(2):
                                        seq = 4 * half + 2 * t + b
                                        op = nc.tensor.matmul(
                                            bank[SEQ * b:SEQ * (b + 1), t, :],
                                            qT[l][32 * r:32 * r + 32, SEQ * seq:SEQ * (seq + 1)],
                                            kb[l][32 * r:32 * r + 32, seq, :, :].rearrange("p n k -> p (n k)"),
                                            start=(not mask_kind and t == 0), stop=True, skip_group_check=True)
                            op.then_inc(sa["scores"], 1)

                        def attend(i, k):
                            l = k // 2 % 2
                            hold(pe, "pe", sa["pt"], hv(i, k))
                            for t in range(2):
                                for b in range(2):
                                    seq = 4 * (k % 2) + 2 * t + b
                                    for pair in range(2):
                                        for r in range(Q4):
                                            op = nc.tensor.matmul(
                                                O[32 * r:32 * r + 32, t * P + b * SEQ:t * P + (b + 1) * SEQ],
                                                vb[l][:, seq, 2 * r + pair, :],
                                                pT[:, t, 2 * r + pair, b * SEQ:(b + 1) * SEQ],
                                                start=(pair == 0), stop=(pair == 1))
                            op.then_inc(sa["av"], 1)

                        def step(i, n):
                            m, odd = divmod(n, 2)
                            small_products_are_read(i, n - 1)
                            if half_exists(i, n - 2):
                                transpose_probabilities(i, n - 2)
                            elif half_exists(i, n - 3):
                                project_output(i, n - 3)
                            if half_exists(i, n):
                                scores(i, n)
                            if half_exists(i, n - 2):
                                hold(pe, "pe", sa["pt"], hv(i, n - 2))
                            if spectral and group_exists(i, m - 3):
                                if not odd:
                                    pe.wait_ge(lnf["norm"], gv(i, m - 3))
                                    transposes(PS[:, 4, :], h[2 + (m - 3) % 2]).then_inc(sf["hTp"], 1)
                                else:
                                    for t in range(T):
                                        op = nc.tensor.matmul(PS[:, 4, t * P:(t + 1) * P], hT[2][:, t * P:(t + 1) * P],
                                                              M[:, :], start=True, stop=True)
                                    op.then_inc(sf["out"], 1)
                            k = n + 1
                            if half_exists(i, k):
                                hold(pe, "pe", sa["vT"], gv(i, k // 2))
                                for b in range(4):
                                    op = nc.tensor.transpose(
                                        VD[:, b * P:(b + 1) * P],
                                        vT[k // 2 % 2][:, 4 * (k % 2) + b, :, :].rearrange("p a k -> p (a k)"), ident[:, :])
                                op.then_inc(sa["vdp"], 1)
                            if not odd and project and group_exists(i, m + 1):
                                l = (m + 1) % 2
                                pe.wait_ge(*loaded_for(sa_cg, i, m + 1))
                                nc.tensor.matmul(KP, wk[:, :], cg[l][:, :], start=True, stop=True)
                                nc.tensor.matmul(VP, wv[:, :], cg[l][:, :], start=True, stop=True).then_inc(sa["kvp"], 1)
                            if odd and group_exists(i, m + 2):
                                pe.wait_ge(ln["norm"], gv(i, m + 2))
                                transposes(HP, h[m % 2]).then_inc(ln["hTp"], 1)
                            if odd and project and group_exists(i, m + 1):
                                nc.tensor.matmul(QP, wq[:, :], hT[(m + 1) % 2][:, :], start=True, stop=True
                                                 ).then_inc(sa["qp"], 1)
                            if int8 and not odd and group_exists(i, m - 3):
                                pe.wait_ge(i8["q"], gv(i, m - 3))
                                for t in range(T):
                                    op = nc.tensor.transpose(bf(I8[:, 64 * t:64 * t + 64]), qb[:, t, :], ident_bf[:, :])
                                op.then_inc(i8["qTp"], 1)
                            if int8 and odd and group_exists(i, m - 3):
                                for t in range(T):
                                    op = nc.tensor.matmul(I8[:, t * P:(t + 1) * P], qT8[:, t * P:(t + 1) * P], wq8[:, :],
                                                          start=True, stop=True)
                                op.then_inc(i8["acc"], 1)
                            if spectral and group_exists(i, m - 3):
                                hold(pe, "pe", sf["ac" if odd else "hT"], gv(i, m - 3))
                            if half_exists(i, n - 2):
                                attend(i, n - 2)

                        run_steps(pe, HALVES, step, lag=int(int8 or spectral))


        def routed_ffn():
            mo_lane = [sem(f"mo_lane_done{l}") for l in range(WIDE)]
            mo = {n: sem("mo_" + n) for n in ("lin", "lm", "ls", "ex", "den", "eq", "tie", "tm", "oh", "ohf", "pre", "pos",
                                              "run", "fit", "keep", "kp", "cf", "lt", "zero")}
            lanes = range(WIDE)
            E = EXPERTS
            with ExitStack() as c:
                def sb(n, shape, dt=F32):
                    return c.enter_context(nc.sbuf_tensor(f"mo_{n}", shape, dt))
                we, be, tie = constant("F1_we"), constant("F1_be"), constant("tie")
                trif, onesf = constant("tri"), constant("ones")
                tri, ones = sb("tri", [P, P], BF16), sb("ones", [P, P], BF16)
                run = sb("run", [P, WIDE, T, E])
                lm = [sb(f"lm{l}", [P, T]) for l in lanes]
                ls = [sb(f"ls{l}", [P, T, E]) for l in lanes]
                ex = [sb(f"ex{l}", [P, T, E]) for l in lanes]
                den = [sb(f"den{l}", [P, T]) for l in lanes]
                gate = [sb(f"gate{l}", [P, T]) for l in lanes]
                eq = [sb(f"eq{l}", [P, T, E]) for l in lanes]
                tm = [sb(f"tm{l}", [P, T]) for l in lanes]
                oh = [sb(f"oh{l}", [P, T, E], BF16) for l in lanes]
                pos = [sb(f"pos{l}", [P, T, E]) for l in lanes]
                kp = [sb(f"kp{l}", [P, T]) for l in lanes]
                cf = [sb(f"cf{l}", [P, T]) for l in lanes]
                lt = [sb(f"lt{l}", [P, T, D]) for l in lanes]
                with nc.Block() as block:
                    @block.vector
                    def _(dve):
                        nc.vector.tensor_copy(tri[:, :], trif[:, :])
                        nc.vector.tensor_copy(ones[:, :], onesf[:, :])
                        nc.vector.memset(run[:, :, :, :], 0.0).then_inc(mo["zero"], 1)
                        dve.wait_ge(mo["zero"], 1)

                def lin(l):
                    return wide_banks(l, 0, 2).rearrange("p (b c) -> p b c", b=2)[:, :, 0:2 * (D + E)].rearrange(
                        "p b (t c) -> p b t c", t=2)

                def counts(l):
                    return wide_banks(l, 1)[:, 512 - 2 * T * E:512]

                def halves(ap):
                    return ap.rearrange("p (b t) c -> p b t c", b=2)

                def over(ap):
                    return ap.unsqueeze(2).to_broadcast([P, T, E])

                with nc.Block() as block:
                    @block.gpsimd
                    def _(pool):
                        with pool.Fori(0, WIDE_STEPS) as i:
                            for l in lanes:
                                ln_rstd(pool, WIDE * i + l + 1, l, 1e-5)

                    @block.vector
                    def _(dve):
                        for lane in mo_lane:
                            dve.sem_inc(lane, 1)
                        with dve.Fori(0, WIDE_STEPS) as i:
                            for l in lanes:
                                hold(dve, "dve", mo_lane[l], i + 1)
                                ln_stats(dve, WIDE * i + l + 1, l, lambda t: wide_row(X, i, l, t))
                            for l in lanes:
                                ln_norm(dve, WIDE * i + l + 1, l, lambda t: wide_row(X, i, l, t), lambda t: h[l][:, t, :])
                            for l in lanes:
                                g = WIDE * i + l
                                dve.wait_ge(mo["lin"], g + 1)
                                nc.vector.tensor_reduce(lm[l][:, :].rearrange("p (b t) -> p b t", b=2), lin(l)[:, :, :, D:D + E],
                                                        op=ALU.max, axis=AX).then_inc(mo["lm"], 1)
                                nc.vector.tensor_tensor(lt[l][:, :, :].rearrange("p (b t) c -> p b t c", b=2),
                                                        lin(l)[:, :, :, 0:D],
                                                        be[:, :].unsqueeze(1).unsqueeze(1).to_broadcast([P, 2, 2, D]),
                                                        ALU.add).then_inc(mo["lt"], 1)
                                dve.wait_ge(mo["lm"], g + 1)
                                nc.vector.tensor_tensor(halves(ls[l][:, :, :]), lin(l)[:, :, :, D:D + E],
                                                        halves(over(lm[l][:, :])), ALU.subtract).then_inc(mo["ls"], 1)
                                dve.wait_ge(mo["ls"], g + 1)
                                nc.vector.tensor_scalar(eq[l][:, :, :], ls[l][:, :, :], 0.0, None, ALU.is_equal
                                                        ).then_inc(mo["eq"], 1)
                                dve.wait_ge(mo["eq"], g + 1)
                                nc.vector.tensor_tensor(eq[l][:, :, :], eq[l][:, :, :],
                                                        tie[:, :].unsqueeze(1).to_broadcast([P, T, E]), ALU.mult
                                                        ).then_inc(mo["tie"], 1)
                                dve.wait_ge(mo["tie"], g + 1)
                                nc.vector.tensor_reduce(tm[l][:, :], eq[l][:, :, :], op=ALU.max, axis=AX
                                                        ).then_inc(mo["tm"], 1)
                                dve.wait_ge(mo["tm"], g + 1)
                                nc.vector.tensor_tensor(oh[l][:, :, :], eq[l][:, :, :], over(tm[l][:, :]), ALU.is_equal
                                                        ).then_inc(mo["oh"], 1)
                            for l in lanes:
                                g = WIDE * i + l
                                dve.wait_ge(mo["ex"], g + 1)
                                nc.vector.tensor_reduce(den[l][:, :], ex[l][:, :, :], op=ALU.add, axis=AX
                                                        ).then_inc(mo["den"], 1)
                                dve.wait_ge(mo["den"], g + 1)
                                nc.vector.reciprocal(gate[l][:, :], den[l][:, :])
                                dve.wait_ge(mo["pre"], g + 1)
                                total = counts(l)[:, T * E:2 * T * E].rearrange("p (t e) -> p t e", t=T)
                                for t in range(T):
                                    nxt = run[:, l, t + 1, :] if t < T - 1 else run[:, (l + 1) % WIDE, 0, :]
                                    nc.vector.tensor_tensor(nxt, run[:, l, t, :], total[:, t, :], ALU.add
                                                            ).then_inc(mo["run"], 1)
                                    dve.wait_ge(mo["run"], T * g + t + 1)
                                nc.vector.tensor_tensor(pos[l][:, :, :], run[:, l, :, :],
                                                        counts(l)[:, 0:T * E].rearrange("p (t e) -> p t e", t=T), ALU.add
                                                        ).then_inc(mo["pos"], 1)
                                dve.wait_ge(mo["pos"], g + 1)
                                nc.vector.tensor_scalar(pos[l][:, :, :], pos[l][:, :, :], float(CAPACITY), None, ALU.is_le
                                                        ).then_inc(mo["fit"], 1)
                                dve.wait_ge(mo["fit"], g + 1)
                                nc.vector.tensor_tensor(pos[l][:, :, :], pos[l][:, :, :], oh[l][:, :, :], ALU.mult
                                                        ).then_inc(mo["keep"], 1)
                                dve.wait_ge(mo["keep"], g + 1)
                                nc.vector.tensor_reduce(kp[l][:, :], pos[l][:, :, :], op=ALU.add, axis=AX
                                                        ).then_inc(mo["kp"], 1)
                                dve.wait_ge(mo["kp"], g + 1)
                                nc.vector.tensor_tensor(cf[l][:, :], kp[l][:, :], gate[l][:, :], ALU.mult
                                                        ).then_inc(mo["cf"], 1)
                                hold(dve, "dve", mo["cf"], g + 1)
                                for t in range(T):
                                    op = nc.vector.scalar_tensor_tensor(wide_row(X, i, l, t), lt[l][:, t, :], cf[l][:, t:t + 1],
                                                                        wide_row(X, i, l, t), ALU.mult, ALU.add)
                                op.then_inc(mo_lane[l], 1)

                    @block.scalar
                    def _(act):
                        with act.Fori(0, WIDE_STEPS) as i:
                            for l in lanes:
                                act.wait_ge(ln["hTp"], WIDE * i + l + 1)
                                nc.scalar.activation(hT[l][:, :], wide_banks(l, 0), ACT.Copy).then_inc(ln["hT"], 1)
                            for l in lanes:
                                act.wait_ge(mo["ls"], WIDE * i + l + 1)
                                nc.scalar.activation(ex[l][:, :, :], ls[l][:, :, :], ACT.Exp).then_inc(mo["ex"], 1)

                    @block.tensor
                    def _(pe):
                        with pe.Fori(0, WIDE_STEPS) as i:
                            for l in lanes:
                                pe.wait_ge(ln["norm"], WIDE * i + l + 1)
                                transposes(wide_banks(l, 0), h[l]).then_inc(ln["hTp"], 1)
                            for l in lanes:
                                pe.wait_ge(ln["hT"], WIDE * i + l + 1)
                                for t in range(T):
                                    op = nc.tensor.matmul(lin(l)[:, t // 2, t % 2, :], hT[l][:, t * P:(t + 1) * P], we[:, :],
                                                          start=True, stop=True)
                                op.then_inc(mo["lin"], 1)
                            for l in lanes:
                                pe.wait_ge(mo["oh"], WIDE * i + l + 1)
                                flat = oh[l][:, :, :].rearrange("p t e -> p (t e)")
                                nc.tensor.matmul(counts(l)[:, 0:T * E], tri[:, :], flat, start=True, stop=True)
                                nc.tensor.matmul(counts(l)[:, T * E:2 * T * E], ones[:, :], flat, start=True, stop=True
                                                 ).then_inc(mo["pre"], 1)


        def decoder_layer():
            dl_cg = [sem(f"dl_context{l}") for l in range(WIDE)]
            dl_lane = [sem(f"dl_lane_done{l}") for l in range(WIDE)]
            dl = {n: sem("dl_" + n) for n in (
                "xTp", "xT", "p0", "p1", "pq0", "pq1", "pv0", "pv1", "q0", "q1", "v0", "v1", "k0", "k1", "sc0", "sc1",
                "mx0", "mx1", "sub0", "sub1", "exp0", "exp1", "sum0", "sum1", "rs0", "rs1", "pn0", "pn1", "pTp0", "pTp1",
                "pT0", "pT1", "av0", "av1", "aT0", "aT1", "aTp0", "aTp1", "add0", "add1", "add2", "gm1", "gm2", "gm3",
                "gb1", "gb2", "gb3", "nb", "nTp", "nT", "w1", "f", "hid", "w2")}
            norms = [ln] + [{n: sem(f"dl_{n}{k}") for n in ("bn", "var", "ve", "rstd", "norm")} for k in range(1, 4)]
            lanes = range(WIDE)
            EPS = 0.001
            SCALE = 1.0 / math.sqrt(SEQ)
            with ExitStack() as c:
                def sb(n, shape, dt=F32):
                    return c.enter_context(nc.sbuf_tensor(f"dl_{n}", shape, dt))
                w = {n: constant(f"A3_{n}") for n in ("wq1", "wk1", "wv1", "wq2", "wk2", "wv2", "w1", "w2", "b2", "gamma", "beta")}
                cg = [sb(f"cg{l}", [P, ROWS]) for l in lanes]
                qT = [sb(f"qT{l}", [P, ROWS]) for l in lanes]
                kT = [sb(f"kT{l}", [P, ROWS]) for l in lanes]
                va = [sb(f"va{l}", [P, T, D]) for l in lanes]
                pr = [sb(f"pr{l}", [P, T, SEQ]) for l in lanes]
                pT = [sb(f"pT{l}", [P, 2, P]) for l in lanes]
                aT = [sb(f"aT{l}", [P, T, 2, SEQ]) for l in lanes]
                mx = [sb(f"mx{l}", [P, T]) for l in lanes]
                sm = [sb(f"sm{l}", [P, T]) for l in lanes]
                rs = [sb(f"rs{l}", [P, T]) for l in lanes]
                n1 = [sb(f"n1{l}", [P, T, D]) for l in lanes]
                n2 = [sb(f"n2{l}", [P, T, D]) for l in lanes]
                n2b = [sb(f"n2b{l}", [P, T, D]) for l in lanes]
                n3 = [sb(f"n3{l}", [P, T, D]) for l in lanes]
                nT = [sb(f"nT{l}", [P, ROWS]) for l in lanes]
                fT = [sb(f"fT{l}", [P, ROWS]) for l in lanes]
                hd = [sb(f"hd{l}", [P, ROWS]) for l in lanes]
                PAIR_A, PAIR_B, NEXT_A = (0, 1), (2, 3), (4, 5)
                ORDER = (1, 0, 1, 1, 0, 1, 1, 0, 0, 0, 1, 1, 0, 1, 0, 1, 0)
                FIRST = ORDER.count(0)
                TURNS = [(half, ORDER[:n].count(half)) for n, half in enumerate(ORDER)]

                def cv(i, g):
                    return WIDE * i + (g + 1)

                def run_halves(eng, first, second):
                    def body(i, more):
                        for half, k in TURNS:
                            if half:
                                second(i, PAIR_A, k)
                            else:
                                first(i, PAIR_B, k)
                        for half, k in TURNS:
                            if half:
                                second(i, PAIR_B, k)
                            elif more:
                                first(i, NEXT_A, k)

                    for k in range(FIRST):
                        first(0, PAIR_A, k)
                    with eng.Fori(0, WIDE_STEPS - 1) as i:
                        body(i, True)
                    body(WIDE_STEPS - 1, False)

                def all_tiles(v):
                    return v[:, :].unsqueeze(1).to_broadcast([P, T, D])

                with nc.Block() as block:
                    @block.sync
                    def _(sp):
                        with sp.Fori(0, WIDE_STEPS) as i:
                            for l in lanes:
                                hold(sp, "sp", dl_lane[l], i + 1)
                                sp.dma_start(cg[l][:, :], ctxT[:, bass.ds(WIDE * ROWS * i + ROWS * l, ROWS)]
                                             ).then_inc(dl_cg[l], 16)

                    @block.gpsimd
                    def _(pool):
                        def rstd_of(i, k, groups):
                            for g in groups:
                                ln_rstd(pool, cv(i, g), g % WIDE, EPS if k else 1e-5, norms[k])

                        def gamma_beta(i, k, groups, rows):
                            for g in groups:
                                t = rows[g % WIDE]
                                hold(pool, "pool", norms[k]["norm"], cv(i, g))
                                nc.gpsimd.tensor_tensor(t[:, :, :], t[:, :, :], all_tiles(w["gamma"]), ALU.mult
                                                        ).then_inc(dl[f"gm{k}"], 1)
                                hold(pool, "pool", dl[f"gm{k}"], cv(i, g))
                                nc.gpsimd.tensor_tensor(t[:, :, :], t[:, :, :], all_tiles(w["beta"]), ALU.add
                                                        ).then_inc(dl[f"gb{k}"], 1)

                        def first(i, groups, k):
                            if k == 0:
                                rstd_of(i, 0, groups)
                            if k == 6:
                                rstd_of(i, 1, groups)
                            if k == 7:
                                gamma_beta(i, 1, groups, n1)

                        def second(i, groups, k):
                            if k == 3:
                                rstd_of(i, 2, groups)
                            if k == 4:
                                gamma_beta(i, 2, groups, n2)
                            if k == 5:
                                for g in groups:
                                    l = g % WIDE
                                    hold(pool, "pool", dl["gb2"], cv(i, g))
                                    nc.gpsimd.tensor_tensor(n2b[l][:, :, :], n2[l][:, :, :], all_tiles(w["b2"]), ALU.add
                                                            ).then_inc(dl["nb"], 1)
                            if k == 6:
                                rstd_of(i, 3, groups)
                            if k == 7:
                                gamma_beta(i, 3, groups, n3)

                        run_halves(pool, first, second)

                    @block.vector
                    def _(dve):
                        def tiles(bank):
                            return bank.rearrange("p (t c) -> p t c", t=T)

                        def keys(i, a, groups):
                            for g in groups:
                                l = g % WIDE
                                hold(dve, "dve", dl[f"p{a}"], cv(i, g))
                                nc.vector.tensor_copy(kT[l][:, :], wide_banks(l, 0)).then_inc(dl[f"k{a}"], 1)

                        def scores_less_maxima(i, a, groups):
                            for g in groups:
                                l, v = g % WIDE, cv(i, g)
                                S = wide_banks(l, 0)[:, 0:T * SEQ].rearrange("p (n k) -> p n k", k=SEQ)
                                dve.wait_ge(dl[f"sc{a}"], v)
                                nc.vector.tensor_reduce(mx[l][:, :], S, op=ALU.max, axis=AX).then_inc(dl[f"mx{a}"], 1)
                                dve.wait_ge(dl[f"mx{a}"], v)
                                nc.vector.tensor_tensor(pr[l][:, :, :], S, mx[l][:, :].unsqueeze(2).to_broadcast([P, T, SEQ]),
                                                        ALU.subtract).then_inc(dl[f"sub{a}"], 1)

                        def probabilities(i, a, groups):
                            for g in groups:
                                l, v = g % WIDE, cv(i, g)
                                dve.wait_ge(dl[f"exp{a}"], v)
                                nc.vector.tensor_reduce(sm[l][:, :], pr[l][:, :, :], op=ALU.add, axis=AX
                                                        ).then_inc(dl[f"sum{a}"], 1)
                                dve.wait_ge(dl[f"sum{a}"], v)
                                nc.vector.reciprocal(rs[l][:, :], sm[l][:, :]).then_inc(dl[f"rs{a}"], 1)
                                dve.wait_ge(dl[f"rs{a}"], v)
                                nc.vector.tensor_tensor(pr[l][:, :, :], pr[l][:, :, :],
                                                        rs[l][:, :].unsqueeze(2).to_broadcast([P, T, SEQ]), ALU.mult
                                                        ).then_inc(dl[f"pn{a}"], 1)

                        def stats(i, k, g, rows):
                            ln_stats(dve, cv(i, g), g % WIDE, rows, norms[k])

                        def norm(i, k, groups, rows):
                            for g in groups:
                                t_ = rows[g % WIDE]
                                ln_norm(dve, cv(i, g), g % WIDE, lambda t: t_[:, t, :], lambda t: t_[:, t, :], norms[k])

                        def first(i, groups, k):
                            if k == 0:
                                for g in groups:
                                    hold(dve, "dve", dl_lane[g % WIDE], i + (g // WIDE + 1))
                                    stats(i, 0, g, lambda t: wide_row(X, i, g, t))
                            if k == 1:
                                for g in groups:
                                    ln_norm(dve, cv(i, g), g % WIDE, lambda t: wide_row(X, i, g, t),
                                            lambda t: h[g % WIDE][:, t, :], norms[0])
                            if k == 2:
                                keys(i, 0, groups)
                            if k == 3:
                                scores_less_maxima(i, 0, groups)
                            if k == 4:
                                probabilities(i, 0, groups)
                            if k == 6:
                                for g in groups:
                                    l = g % WIDE
                                    dve.wait_ge(dl["aTp0"], cv(i, g))
                                    nc.vector.tensor_tensor(n1[l][:, :, :], tiles(wide_banks(l, 0)), h[l][:, :, :], ALU.add
                                                            ).then_inc(dl["add0"], 1)
                                    hold(dve, "dve", dl["add0"], cv(i, g))
                                    stats(i, 1, g, lambda t: n1[l][:, t, :])
                            if k == 7:
                                norm(i, 1, groups, n1)

                        def second(i, groups, k):
                            if k == 0:
                                keys(i, 1, groups)
                            if k == 1:
                                scores_less_maxima(i, 1, groups)
                            if k == 2:
                                probabilities(i, 1, groups)
                            if k == 3:
                                for g in groups:
                                    l = g % WIDE
                                    dve.wait_ge(dl["gb1"], cv(i, g))
                                    dve.wait_ge(dl["aTp1"], cv(i, g))
                                    nc.vector.tensor_tensor(n2[l][:, :, :], tiles(wide_banks(l, 0)), n1[l][:, :, :], ALU.add
                                                            ).then_inc(dl["add1"], 1)
                                    hold(dve, "dve", dl["add1"], cv(i, g))
                                    stats(i, 2, g, lambda t: n2[l][:, t, :])
                            if k == 4:
                                norm(i, 2, groups, n2)
                            if k == 5:
                                for g in groups:
                                    l = g % WIDE
                                    dve.wait_ge(dl["f"], cv(i, g))
                                    nc.vector.scalar_tensor_tensor(hd[l][:, :], fT[l][:, :], 0.2, fT[l][:, :], ALU.mult,
                                                                   ALU.max).then_inc(dl["hid"], 1)
                            if k == 6:
                                for g in groups:
                                    l = g % WIDE
                                    dve.wait_ge(dl["nb"], cv(i, g))
                                    dve.wait_ge(dl["w2"], cv(i, g))
                                    nc.vector.tensor_tensor(n3[l][:, :, :], tiles(wide_banks(l, 1)), n2b[l][:, :, :], ALU.add
                                                            ).then_inc(dl["add2"], 1)
                                    hold(dve, "dve", dl["add2"], cv(i, g))
                                    stats(i, 3, g, lambda t: n3[l][:, t, :])
                            if k == 7:
                                norm(i, 3, groups, n3)
                            if k == 8:
                                for g in groups:
                                    l = g % WIDE
                                    hold(dve, "dve", dl["gb3"], cv(i, g))
                                    nc.vector.scalar_tensor_tensor(wide_rows(X, i, g), n3[l][:, :, :], 0.0, wide_rows(X, i, g),
                                                                   ALU.max, ALU.add).then_inc(dl_lane[l], 1)

                        for lane in dl_lane:
                            dve.sem_inc(lane, 1)
                        run_halves(dve, first, second)

                    @block.scalar
                    def _(act):
                        def copy(event, done, i, groups, dst, src):
                            for g in groups:
                                l = g % WIDE
                                act.wait_ge(dl[event], cv(i, g))
                                nc.scalar.activation(dst(l), src(l), ACT.Copy).then_inc(dl[done], 1)

                        def queries(i, a, groups):
                            copy(f"pq{a}", f"q{a}", i, groups, lambda l: qT[l][:, :], lambda l: wide_banks(l, 1))

                        def values_and_exponentials(i, a, groups):
                            copy(f"pv{a}", f"v{a}", i, groups, lambda l: va[l][:, :, :].rearrange("p t c -> p (t c)"),
                                 lambda l: wide_banks(l, 1))
                            for g in groups:
                                l = g % WIDE
                                act.wait_ge(dl[f"sub{a}"], cv(i, g))
                                nc.scalar.activation(pr[l][:, :, :], pr[l][:, :, :], ACT.Exp, scale=SCALE
                                                     ).then_inc(dl[f"exp{a}"], 1)

                        def transposed(i, a, groups):
                            copy(f"pTp{a}", f"pT{a}", i, groups, lambda l: pT[l][:, :, :].rearrange("p u c -> p (u c)"),
                                 lambda l: wide_banks(l, 1)[:, 0:2 * P])

                        def attended(i, a, groups):
                            for g in groups:
                                l = g % WIDE
                                act.wait_ge(dl[f"av{a}"], cv(i, g))
                                for x_ in range(2):
                                    op = nc.scalar.activation(aT[l][:, :, x_, :], wide_banks(l, x_)[:, 0:T * SEQ].rearrange(
                                        "p (t q) -> p t q", t=T), ACT.Copy)
                                op.then_inc(dl[f"aT{a}"], 1)

                        def first(i, groups, k):
                            if k == 1:
                                copy("xTp", "xT", i, groups, lambda l: hT[l][:, :], lambda l: wide_banks(l, 0))
                            if k == 2:
                                queries(i, 0, groups)
                            if k == 3:
                                values_and_exponentials(i, 0, groups)
                            if k == 4:
                                transposed(i, 0, groups)
                            if k == 5:
                                attended(i, 0, groups)

                        def second(i, groups, k):
                            if k == 0:
                                queries(i, 1, groups)
                            if k == 1:
                                values_and_exponentials(i, 1, groups)
                            if k == 2:
                                transposed(i, 1, groups)
                            if k == 3:
                                attended(i, 1, groups)
                            if k == 5:
                                copy("nTp", "nT", i, groups, lambda l: nT[l][:, :], lambda l: wide_banks(l, 1))
                                for g in groups:
                                    l = g % WIDE
                                    act.wait_ge(dl["w1"], cv(i, g))
                                    nc.scalar.activation(fT[l][:, :], wide_banks(l, 0), ACT.Identity, bias=column("A3_b1")
                                                         ).then_inc(dl["f"], 1)

                        run_halves(act, first, second)

                    @block.tensor
                    def _(pe):
                        def project(i, a, groups, q_of, kv_of):
                            for g in groups:
                                l = g % WIDE
                                if a == 0:
                                    pe.wait_ge(dl["xT"], cv(i, g))
                                nc.tensor.matmul(wide_banks(l, 1), w[f"wq{a + 1}"][:, :], q_of(l), start=True, stop=True
                                                 ).then_inc(dl[f"pq{a}"], 1)
                                if a == 1:
                                    pe.wait_ge(dl["add0"], cv(i, g))
                                    pe.wait_ge(dl_cg[l], 16 * i + (16 * (g // WIDE) + 16))
                                nc.tensor.matmul(wide_banks(l, 0), w[f"wk{a + 1}"][:, :], kv_of(l), start=True, stop=True
                                                 ).then_inc(dl[f"p{a}"], 1)

                        def values_and_scores(i, a, groups, kv_of):
                            for g in groups:
                                l = g % WIDE
                                pe.wait_ge(dl[f"q{a}"], cv(i, g))
                                for t in range(T):
                                    op = nc.tensor.matmul(wide_banks(l, 1)[:, t * P:(t + 1) * P], kv_of(l)[:, t * P:(t + 1) * P],
                                                          w[f"wv{a + 1}"][:, :], start=True, stop=True)
                                op.then_inc(dl[f"pv{a}"], 1)
                            for g in groups:
                                l = g % WIDE
                                hold(pe, "pe", dl[f"k{a}"], cv(i, g))
                                if a == 0:
                                    nc.tensor.matmul(wide_banks(l, 0)[:, 0:T * SEQ].rearrange("p (n k) -> p n k", k=SEQ),
                                                     ident_bf[:, :], causal_bf[:, :].unsqueeze(1).to_broadcast([P, T, SEQ]),
                                                     start=True, stop=False, skip_group_check=True)
                                for u in range(2):
                                    for b in range(2):
                                        for x_ in range(2):
                                            s = SEQ * (4 * u + 2 * b + x_)
                                            op = nc.tensor.matmul(
                                                wide_banks(l, 0)[SEQ * b:SEQ * (b + 1),
                                                                 SEQ * (2 * u + x_):SEQ * (2 * u + x_ + 1)],
                                                qT[l][:, s:s + SEQ], kT[l][:, s:s + SEQ], start=(a == 1), stop=True,
                                                skip_group_check=True)
                                op.then_inc(dl[f"sc{a}"], 1)

                        def transpose_probabilities(i, a, groups):
                            for g in groups:
                                l = g % WIDE
                                hold(pe, "pe", dl[f"v{a}"], cv(i, g))
                                pe.wait_ge(dl[f"pn{a}"], cv(i, g))
                                for u in range(2):
                                    op = nc.tensor.transpose(wide_banks(l, 1)[:, u * P:(u + 1) * P],
                                                             pr[l][:, 2 * u:2 * u + 2, :].rearrange("p n k -> p (n k)"),
                                                             ident[:, :])
                                op.then_inc(dl[f"pTp{a}"], 1)

                        def attend(i, a, groups):
                            for g in groups:
                                l = g % WIDE
                                hold(pe, "pe", dl[f"pT{a}"], cv(i, g))
                                for t in range(T):
                                    for x_ in range(2):
                                        r = slice(SEQ * x_, SEQ * (x_ + 1))
                                        op = nc.tensor.matmul(wide_banks(l, x_)[:, SEQ * t:SEQ * (t + 1)], va[l][r, t, :],
                                                              pT[l][r, t // 2, SEQ * (t % 2):SEQ * (t % 2 + 1)],
                                                              start=True, stop=True)
                                op.then_inc(dl[f"av{a}"], 1)

                        def transpose_attended(i, a, groups):
                            for g in groups:
                                l = g % WIDE
                                pe.wait_ge(dl[f"aT{a}"], cv(i, g))
                                for t in range(T):
                                    op = nc.tensor.transpose(wide_banks(l, 0)[:, t * P:(t + 1) * P],
                                                             aT[l][:, t, :, :].rearrange("p x q -> p (x q)"), ident[:, :])
                                op.then_inc(dl[f"aTp{a}"], 1)

                        def first(i, groups, k):
                            own = lambda l: hT[l][:, :]
                            if k == 1:
                                for g in groups:
                                    pe.wait_ge(norms[0]["norm"], cv(i, g))
                                    transposes(wide_banks(g % WIDE, 0), h[g % WIDE]).then_inc(dl["xTp"], 1)
                            if k == 2:
                                project(i, 0, groups, own, own)
                            if k == 3:
                                values_and_scores(i, 0, groups, own)
                            if k == 4:
                                transpose_probabilities(i, 0, groups)
                            if k == 5:
                                attend(i, 0, groups)
                                transpose_attended(i, 0, groups)

                        def second(i, groups, k):
                            context = lambda l: cg[l][:, :]
                            if k == 0:
                                project(i, 1, groups, lambda l: aT[l][:, :, :, :].rearrange("p t x q -> p (t x q)"), context)
                            if k == 1:
                                values_and_scores(i, 1, groups, context)
                            if k == 2:
                                transpose_probabilities(i, 1, groups)
                            if k == 3:
                                attend(i, 1, groups)
                                transpose_attended(i, 1, groups)
                            if k == 5:
                                for g in groups:
                                    pe.wait_ge(dl["gb2"], cv(i, g))
                                    transposes(wide_banks(g % WIDE, 1), n2[g % WIDE]).then_inc(dl["nTp"], 1)
                                for g in groups:
                                    l = g % WIDE
                                    pe.wait_ge(dl["nT"], cv(i, g))
                                    nc.tensor.matmul(wide_banks(l, 0), w["w1"][:, :], nT[l][:, :], start=True, stop=True
                                                     ).then_inc(dl["w1"], 1)
                            if k == 6:
                                for g in groups:
                                    l = g % WIDE
                                    pe.wait_ge(dl["hid"], cv(i, g))
                                    for t in range(T):
                                        op = nc.tensor.matmul(wide_banks(l, 1)[:, t * P:(t + 1) * P],
                                                              hd[l][:, t * P:(t + 1) * P], w["w2"][:, :], start=True, stop=True)
                                    op.then_inc(dl["w2"], 1)

                        run_halves(pe, first, second)


        def start_stream(Y):
            y0_lane = [sem(f"y0_lane_done{l}") for l in range(WIDE)]
            with nc.Block() as block:
                @block.gpsimd
                def _(pool):
                    with pool.Fori(0, WIDE_STEPS) as i:
                        for l in range(WIDE):
                            ln_rstd(pool, WIDE * i + l + 1, l, 1e-5)

                @block.vector
                def _(dve):
                    for lane in y0_lane:
                        dve.sem_inc(lane, 1)
                    with dve.Fori(0, WIDE_STEPS) as i:
                        for l in range(WIDE):
                            hold(dve, "dve", y0_lane[l], i + 1)
                            ln_stats(dve, WIDE * i + l + 1, l, lambda t: wide_row(X, i, l, t))
                        for l in range(WIDE):
                            ln_norm(dve, WIDE * i + l + 1, l, lambda t: wide_row(X, i, l, t), lambda t: wide_row(Y, i, l, t))
                            hold(dve, "dve", ln["norm"], WIDE * i + l + 1)
                            nc.vector.memset(ve[l][:, :], 1.0).then_inc(y0_lane[l], 1)

        NEWTON = 11

        def window_attention(lyr, Y):
            wa = {n: sem("wa_" + n) for n in (
                "tab", "sh", "shr", "shl", "hTp", "hT", "pq", "pk", "pv", "sq", "va", "n2", "abq", "ab", "sum", "nw", "qkn", "qkTp", "qkT", "sc", "mx",
                "sub", "exp", "den", "rden", "pn", "pTp", "pT", "av", "o", "wo", "yT", "yTp", "Y")}
            lanes = range(LANES)
            pre = f"F3_{lyr}_"
            with ExitStack() as c:
                def sb(n, shape, dt=F32):
                    return c.enter_context(nc.sbuf_tensor(f"wa{lyr}_{n}", shape, dt))
                wqkv = sb("wqkv", [P, 3 * INNER])
                wo = sb("wo", [P, 4, D])
                shift = sb("shift", [P, P])
                rope = sb("rope", [P, 4 * HEAD_DIM])
                tab = sb("tab", [P, 4, HEAD_DIM])
                hs = sb("hs", [P, T, D])
                sq = sb("sq", [P, 2 * INNER])
                qk = [sb(f"qk{l}", [P, T, 2 * INNER]) for l in lanes]
                tb = [sb(f"tb{l}", [P, 2 * INNER]) for l in lanes]
                va = [sb(f"va{l}", [P, T, INNER]) for l in lanes]
                ss = [sb(f"ss{l}", [P, T, 2 * HEADS]) for l in lanes]
                y_ = [sb(f"y{l}", [P, T * 2 * HEADS]) for l in lanes]
                t_ = [sb(f"t{l}", [P, T * 2 * HEADS]) for l in lanes]
                qkT = [sb(f"qkT{l}", [P, 8, P]) for l in lanes]
                pr = [sb(f"pr{l}", [P, 8, SEQ]) for l in lanes]
                pT = sb("pT", [P, 4, P])
                mx, den, rden = sb("mx", [P, 8]), sb("den", [P, 8]), sb("rden", [P, 8])
                oT = [sb(f"oT{l}", [P, 4, ROWS]) for l in lanes]
                yT = sb("yT", [P, ROWS])
                with nc.Block() as block:
                    @block.sync
                    def _(sp):
                        load(sp, wqkv[:, :], pre + "wqkv")
                        load(sp, wo[:, :, :].rearrange("p a b -> p (a b)"), pre + "wo")
                        load(sp, shift[:, :], "shift")
                        load(sp, rope[:, :], "rope")
                        load(sp, tab[:, :, :].rearrange("p a b -> p (a b)"), pre + "scales")
                        sp.wait_ge(loaded, loads[0])
                with nc.Block() as block:
                    @block.vector
                    def _(dve):
                        flat = tab[:, :, :].rearrange("p a b -> p (a b)")
                        nc.vector.tensor_tensor(flat, flat, rope[:, :], ALU.mult).then_inc(wa["tab"], 1)
                        dve.wait_ge(wa["tab"], 1)

                UNITS = 2 * T
                AHEAD = 6
                QK = PS[:, 0:2, :].rearrange("p b c -> p (b c)")
                QKT = PS[:, 2:4, :].rearrange("p b c -> p (b c)")
                V, SC, PTP, AV = (PS[:, b, :] for b in range(4, 8))

                def uv(i, k):
                    return UNITS * i + (k + 1)

                def halves(bank0, bank1):
                    return [bank[:, 0:4 * SEQ].rearrange("p (c q) -> p c q", c=4) for bank in (bank0, bank1)]

                outputs = halves(AV, PTP)


                with nc.Block() as block:
                    @block.gpsimd
                    def _(pool):
                        def step(i, n):
                            g = n // T
                            if n % T == T - 1 and group_exists(i, g + 3):
                                if group_exists(i, g + 2):
                                    hold(pool, "pool", wa["hTp"], gv(i, g + 2))
                                nc.gpsimd.tensor_copy(hs[:, :, 0:D // 2], group_rows(Y, i, g + 3)[:, :, 0:D // 2]
                                                      ).then_inc(wa["shl"], 1)
                            k = n + AHEAD - 1
                            if tile_exists(i, k):
                                hold(pool, "pool", wa["ab"], uv(i, k))
                                q = qk[k // T % 2][:, k % T, :]
                                nc.gpsimd.tensor_tensor(q, q, tb[k % 2][:, :], ALU.add).then_inc(wa["sum"], 1)
                            k = n + 2
                            if tile_exists(i, k):
                                m = k // T
                                hold(pool, "pool", wa["nw"], 2 * NEWTON * i + NEWTON * (m + 1))
                                hold(pool, "pool", wa["sum"], uv(i, k))
                                q = qk[m % 2][:, k % T, :].rearrange("p (n d) -> p n d", d=HEAD_DIM)
                                r = y_[m % 2][:, 2 * HEADS * (k % T):2 * HEADS * (k % T + 1)].unsqueeze(2).to_broadcast(
                                    [P, 2 * HEADS, HEAD_DIM])
                                nc.gpsimd.tensor_tensor(q, q, r, ALU.mult).then_inc(wa["qkn"], 1)

                        run_steps(pool, UNITS, step)

                    @block.vector
                    def _(dve):
                        def inverse_root_step(i, m, k):
                            s = ss[m % 2][:, :, :].rearrange("p t n -> p (t n)")
                            y, t = y_[m % 2][:, :], t_[m % 2][:, :]
                            if k:
                                hold(dve, "dve", wa["nw"], 2 * NEWTON * i + (NEWTON * m + k))
                            if k == 0:
                                hold(dve, "dve", wa["n2"], uv(i, T * m + T - 1))
                                op = nc.vector.tensor_scalar(s, s, 1e-24, None, ALU.max)
                            elif k == 1:
                                op = nc.vector.tensor_scalar(y.bitcast(I32), s.bitcast(I32), -0.5, RSQRT_SEED,
                                                             ALU.mult, ALU.add)
                            elif k % 3 == 2:
                                op = nc.vector.scalar_tensor_tensor(t, y, -0.5, y, ALU.mult, ALU.mult)
                            elif k % 3 == 0:
                                op = nc.vector.tensor_tensor(t, t, s, ALU.mult)
                            else:
                                op = nc.vector.scalar_tensor_tensor(y, t, 1.5, y, ALU.add, ALU.mult)
                            op.then_inc(wa["nw"], 1)

                        def step(i, n):
                            g = n // T
                            done = [0]

                            def roots(count):
                                if n % T == 2 and group_exists(i, g + 1):
                                    for k in range(done[0], min(done[0] + count, NEWTON)):
                                        inverse_root_step(i, g + 1, k)
                                    done[0] += count

                            if n % T == T - 1 and group_exists(i, g - 1):
                                hold(dve, "dve", wa["yTp"], gv(i, g - 1))
                                nc.vector.tensor_tensor(group_rows(Y, i, g - 1), V.rearrange("p (t c) -> p t c", t=T),
                                                        group_rows(Y, i, g - 1), ALU.add).then_inc(wa["Y"], 1)
                            if tile_exists(i, n):
                                q = n % 2
                                v = uv(i, n)
                                S = SC.rearrange("p (n k) -> p n k", k=SEQ)
                                dve.wait_ge(wa["sc"], v)
                                nc.vector.tensor_reduce(mx[:, :], S, op=ALU.max, axis=AX).then_inc(wa["mx"], 1)
                                roots(1)
                                dve.wait_ge(wa["mx"], v)
                                nc.vector.tensor_tensor(pr[q][:, :, :], S, mx[:, :].unsqueeze(2).to_broadcast(
                                    [P, 8, SEQ]), ALU.subtract).then_inc(wa["sub"], 1)
                                roots(4)
                                dve.wait_ge(wa["exp"], v)
                                nc.vector.tensor_reduce(den[:, :], pr[q][:, :, :], op=ALU.add, axis=AX
                                                        ).then_inc(wa["den"], 1)
                                roots(1)
                                dve.wait_ge(wa["den"], v)
                                nc.vector.reciprocal(rden[:, :], den[:, :]).then_inc(wa["rden"], 1)
                                roots(1)
                                dve.wait_ge(wa["rden"], v)
                                nc.vector.tensor_tensor(pr[q][:, :, :], pr[q][:, :, :], rden[:, :].unsqueeze(2)
                                                        .to_broadcast([P, 8, SEQ]), ALU.mult).then_inc(wa["pn"], 1)
                            k = n + AHEAD
                            if tile_exists(i, k):
                                lane, t = k // T % 2, k % T
                                hold(dve, "dve", wa["sq"], uv(i, k))
                                roots(1)
                                nc.vector.tensor_reduce(ss[lane][:, t, :], sq[:, :].rearrange("p (n d) -> p n d", d=HEAD_DIM),
                                                        op=ALU.add, axis=AX).then_inc(wa["n2"], 1)
                                roots(1)
                                if tile_exists(i, k - 2):
                                    hold(dve, "dve", wa["sum"], uv(i, k - 2))
                                hd = HEAD_DIM // 2
                                for a, done_with in ((0, "abq"), (1, "ab")):
                                    r = slice(INNER * a, INNER * (a + 1))
                                    own, other, src = (ap[:, r].rearrange("p (h d) -> p h d", d=HEAD_DIM)
                                                       for ap in (qk[lane][:, t, :], tb[k % 2][:, :], QK))
                                    nc.vector.tensor_tensor(own, src, tab[:, a:a + 1, :].to_broadcast([P, HEADS, HEAD_DIM]),
                                                            ALU.mult)
                                    for lo, hi in ((0, hd), (hd, 0)):
                                        op = nc.vector.tensor_tensor(
                                            other[:, :, lo:lo + hd], src[:, :, hi:hi + hd],
                                            tab[:, 2 + a:3 + a, lo:lo + hd].to_broadcast([P, HEADS, hd]), ALU.mult)
                                    op.then_inc(wa[done_with], 1)
                                    roots(1)
                            roots(NEWTON)

                        run_steps(dve, UNITS, step)

                    @block.scalar
                    def _(act):
                        def step(i, n):
                            g = n // T
                            if tile_exists(i, n - 1):
                                act.wait_ge(wa["pTp"], uv(i, n - 1))
                                nc.scalar.activation(pT[:, :, :].rearrange("p c q -> p (c q)"), PTP, ACT.Copy
                                                     ).then_inc(wa["pT"], 1)
                            if tile_exists(i, n):
                                act.wait_ge(wa["sub"], uv(i, n))
                                nc.scalar.activation(pr[n % 2][:, :, :], pr[n % 2][:, :, :], ACT.Exp).then_inc(wa["exp"], 1)
                            k = n + AHEAD
                            if tile_exists(i, k):
                                if tile_exists(i, k - 1):
                                    act.wait_ge(wa["n2"], uv(i, k - 1))
                                act.wait_ge(wa["pq"], uv(i, k))
                                nc.scalar.activation(sq[:, 0:INNER], QK[:, 0:INNER], ACT.Square)
                                act.wait_ge(wa["pk"], uv(i, k))
                                nc.scalar.activation(sq[:, INNER:2 * INNER], QK[:, INNER:2 * INNER], ACT.Square
                                                     ).then_inc(wa["sq"], 1)
                                act.wait_ge(wa["pv"], uv(i, k))
                                nc.scalar.activation(va[k // T % 2][:, k % T, :], V, ACT.Copy).then_inc(wa["va"], 1)
                            if tile_exists(i, n + 1):
                                act.wait_ge(wa["qkTp"], uv(i, n + 1))
                                nc.scalar.activation(qkT[(n + 1) % 2][:, :, :].rearrange("p c q -> p (c q)"), QKT,
                                                     ACT.Copy).then_inc(wa["qkT"], 1)
                            k = n - 1
                            if tile_exists(i, k):
                                act.wait_ge(wa["av"], uv(i, k))
                                for b, o in enumerate(outputs):
                                    s = P * (k % T) + SEQ * b
                                    op = nc.scalar.activation(oT[k // T % 2][:, :, s:s + SEQ], o, ACT.Copy)
                                op.then_inc(wa["o"], 1)
                            if n % T == 0 and group_exists(i, g + 2):
                                act.wait_ge(wa["hTp"], gv(i, g + 2))
                                nc.scalar.activation(hT[g % 2][:, :], V, ACT.Copy).then_inc(wa["hT"], 1)
                            if n % T == 1 and group_exists(i, g - 1):
                                act.wait_ge(wa["wo"], gv(i, g - 1))
                                nc.scalar.activation(yT[:, :], V, ACT.Copy).then_inc(wa["yT"], 1)
                            if n % T == 3 and group_exists(i, g + 3):
                                act.wait_ge(wa["sh"], gv(i, g + 3))
                                nc.scalar.activation(hs[:, :, D // 2:D], V[:, 0:T * D // 2].rearrange("p (t c) -> p t c", t=T),
                                                     ACT.Copy).then_inc(wa["shr"], 1)

                        run_steps(act, UNITS, step)

                    @block.tensor
                    def _(pe):
                        def score(i, n):
                            q = n % 2
                            if tile_exists(i, n - 1):
                                pe.wait_ge(wa["sub"], uv(i, n - 1))
                            pe.wait_ge(wa["qkT"], uv(i, n))
                            nc.tensor.matmul(SC.rearrange("p (n k) -> p n k", k=SEQ), ident_bf[:, :],
                                             causal_bf[:, :].unsqueeze(1).to_broadcast([P, 8, SEQ]),
                                             start=True, stop=False, skip_group_check=True)
                            for k in range(4):
                                for b in range(2):
                                    for hh in range(2):
                                        r = slice(SEQ * hh, SEQ * (hh + 1))
                                        s = slice(SEQ * b, SEQ * (b + 1))
                                        op = nc.tensor.matmul(
                                            SC[r, SEQ * (2 * k + b):SEQ * (2 * k + b + 1)],
                                            qkT[q][r, k, s], qkT[q][r, 4 + k, s], start=False, stop=True,
                                            skip_group_check=True)
                            op.then_inc(wa["sc"], 1)

                        def project_tile(i, n):
                            k = n + AHEAD
                            t = k % T
                            if t == 0:
                                pe.wait_ge(wa["hT"], gv(i, k // T))
                            for j, (read, done_with) in enumerate((("abq", "pq"), ("ab", "pk"), ("va", "pv"))):
                                if tile_exists(i, k - 1):
                                    pe.wait_ge(wa[read], uv(i, k - 1))
                                if j == 2:
                                    g, last_use = divmod(n - 1, T)
                                    name, m = (("hT", g + 2), ("yT", g - 1), ("Y", g - 1), ("shr", g + 3))[last_use]
                                    if group_exists(i, m):
                                        pe.wait_ge(wa[name], gv(i, m))
                                op = nc.tensor.matmul(QK[:, j * INNER:(j + 1) * INNER] if j < 2 else V,
                                                      hT[k // T % 2][:, t * P:(t + 1) * P],
                                                      wqkv[:, j * INNER:(j + 1) * INNER], start=True, stop=True)
                                op.then_inc(wa[done_with], 1)

                        def transpose_probabilities(i, k):
                            pe.wait_ge(wa["pn"], uv(i, k))
                            if tile_exists(i, k - 1):
                                pe.wait_ge(wa["o"], uv(i, k - 1))
                            for c in range(4):
                                op = nc.tensor.transpose(PTP[:, c * P:(c + 1) * P],
                                                         pr[k % 2][:, 2 * c:2 * c + 2, :].rearrange("p n k -> p (n k)"),
                                                         ident[:, :])
                            op.then_inc(wa["pTp"], 1)

                        def transpose_heads(i, k):
                            pe.wait_ge(wa["qkn"], uv(i, k))
                            for c in range(8):
                                op = nc.tensor.transpose(QKT[:, c * P:(c + 1) * P],
                                                         qk[k // T % 2][:, k % T, c * P:(c + 1) * P], ident[:, :])
                            op.then_inc(wa["qkTp"], 1)

                        def attend(i, n):
                            hold(pe, "pe", wa["pT"], uv(i, n))
                            for k in range(4):
                                for b in range(2):
                                    for hh in range(2):
                                        s = slice(SEQ * b, SEQ * (b + 1))
                                        head = 2 * k + hh
                                        op = nc.tensor.matmul(
                                            outputs[b][SEQ * hh:SEQ * (hh + 1), k, :],
                                            va[n // T % 2][s, n % T, HEAD_DIM * head:HEAD_DIM * (head + 1)],
                                            pT[s, k, SEQ * hh:SEQ * (hh + 1)], start=True, stop=True)
                            op.then_inc(wa["av"], 1)

                        def step(i, n):
                            g = n // T
                            if tile_exists(i, n):
                                score(i, n)
                            if tile_exists(i, n - 1):
                                transpose_probabilities(i, n - 1)
                            if tile_exists(i, n + AHEAD):
                                project_tile(i, n)
                            if tile_exists(i, n + 1):
                                transpose_heads(i, n + 1)
                            if tile_exists(i, n - 1):
                                attend(i, n - 1)
                            if tile_exists(i, n + AHEAD):
                                pe.wait_ge(wa["va"], uv(i, n + AHEAD))
                            if n % T == 0 and group_exists(i, g + 2):
                                hold(pe, "pe", wa["shl"], gv(i, g + 2))
                                pe.wait_ge(wa["shr"], gv(i, g + 2))
                                transposes(V, hs).then_inc(wa["hTp"], 1)
                            if n % T == 1 and group_exists(i, g - 1):
                                hold(pe, "pe", wa["o"], uv(i, T * g - 1))
                                for k in range(4):
                                    op = nc.tensor.matmul(V, wo[:, k, :], oT[(g - 1) % 2][:, k, :], start=(k == 0),
                                                          stop=(k == 3))
                                op.then_inc(wa["wo"], 1)
                            if n % T == 2 and group_exists(i, g - 1):
                                pe.wait_ge(wa["yT"], gv(i, g - 1))
                                for t in range(T):
                                    op = nc.tensor.transpose(V[:, t * P:(t + 1) * P], yT[:, t * P:(t + 1) * P], ident[:, :])
                                op.then_inc(wa["yTp"], 1)
                            if n % T == 3 and group_exists(i, g + 3):
                                if group_exists(i, g - 1):
                                    pe.wait_ge(wa["Y"], gv(i, g - 1))
                                nc.tensor.matmul(V[:, 0:T * D // 2].rearrange("p (t c) -> p t c", t=T), shift[:, :],
                                                 group_rows(Y, i, g + 3)[:, :, D // 2:D], start=True, stop=True
                                                 ).then_inc(wa["sh"], 1)

                        run_steps(pe, UNITS, step)

        def gated_ffn(lyr, Y, last):
            stored = [sem(f"stored{l}") for l in range(WIDE)]
            gf_lane = [sem(f"gf_lane_done{l}") for l in range(WIDE)]
            gf = {n: sem("gf_" + n) for n in ("sh", "shr", "shl", "hTp", "hT", "ag", "gl", "u", "w2", "yT", "yTp", "add", "sum")}
            lanes = range(WIDE)
            pre = f"F3_{lyr}_"
            with ExitStack() as c:
                def sb(n, shape, dt=F32):
                    return c.enter_context(nc.sbuf_tensor(f"gf{lyr}_{n}", shape, dt))
                w1 = sb("w1", [P, 2 * HID])
                w2 = sb("w2", [P, NHC, D])
                shift = sb("shift", [P, P])
                hs = [sb(f"hs{l}", [P, T, D]) for l in lanes]
                gl = [[sb(f"gl{l}{k}", [P, ROWS]) for k in range(NHC)] for l in lanes]
                uT = [[sb(f"uT{l}{k}", [P, ROWS]) for k in range(NHC)] for l in lanes]
                yT = [sb(f"yT{l}", [P, ROWS]) for l in lanes]
                xo = [sb(f"xo{l}", [P, T, D]) for l in lanes]
                with nc.Block() as block:
                    @block.sync
                    def _(sp):
                        load(sp, w1[:, :], pre + "w1")
                        load(sp, w2[:, :, :].rearrange("p a b -> p (a b)"), pre + "w2")
                        load(sp, shift[:, :], "shift")
                        sp.wait_ge(loaded, loads[0])

                def gv(i, l):
                    return WIDE * i + l + 1

                def cv(i, k, l):
                    return WIDE * NHC * i + (WIDE * k + l + 1)

                with nc.Block() as block:
                    if last:
                        @block.sync
                        def _(sp):
                            for l in lanes:
                                sp.sem_inc(stored[l], 16)
                            with sp.Fori(0, WIDE_STEPS) as i:
                                for l in lanes:
                                    hold(sp, "sp", gf_lane[l], i + 2)
                                    sp.dma_start(out[bass.ds(WIDE * ROWS * i + ROWS * l, ROWS), :].rearrange(
                                        "(t p) c -> p t c", p=P), xo[l][:, :, :]).then_inc(stored[l], 16)
                            for l in lanes:
                                sp.wait_ge(stored[l], 16 * (WIDE_STEPS + 1))

                    @block.gpsimd
                    def _(pool):
                        with pool.Fori(0, WIDE_STEPS) as i:
                            for l in lanes:
                                hold(pool, "pool", gf_lane[l], i + 1)
                                nc.gpsimd.tensor_copy(hs[l][:, :, 0:D // 2], wide_rows(Y, i, l)[:, :, 0:D // 2]
                                                      ).then_inc(gf["shl"], 1)
                            for l in lanes:
                                ln_rstd(pool, WIDE * i + l + 1, l, 1e-5)

                    @block.vector
                    def _(dve):
                        for lane in gf_lane:
                            dve.sem_inc(lane, 1)
                        with dve.Fori(0, WIDE_STEPS) as i:
                            for l in lanes:
                                hold(dve, "dve", gf["shl"], gv(i, l))
                                hold(dve, "dve", gf["shr"], gv(i, l))
                                ln_stats(dve, WIDE * i + l + 1, l, lambda t: hs[l][:, t, :])
                            for l in lanes:
                                ln_norm(dve, WIDE * i + l + 1, l, lambda t: hs[l][:, t, :], lambda t: h[l][:, t, :])
                            for k, (at, m) in enumerate(HID_CHUNKS):
                                for l in lanes:
                                    hold(dve, "dve", gf["gl"], cv(i, k, l))
                                    nc.vector.scalar_tensor_tensor(uT[l][k][0:m, :], wide_banks(l, 0)[0:m, :],
                                                                   column(pre + "b1", k)[0:m], gl[l][k][0:m, :],
                                                                   ALU.add, ALU.mult).then_inc(gf["u"], 1)
                            for l in lanes:
                                hold(dve, "dve", gf["yTp"], gv(i, l))
                                if not last:
                                    nc.vector.tensor_tensor(wide_rows(Y, i, l), wide_banks(l, 1).rearrange("p (t c) -> p t c", t=T),
                                                            wide_rows(Y, i, l), ALU.add).then_inc(gf_lane[l], 1)
                                else:
                                    hold(dve, "dve", stored[l], 16 * i + 16)
                                    nc.vector.tensor_tensor(xo[l][:, :, :], wide_banks(l, 1).rearrange("p (t c) -> p t c", t=T),
                                                            wide_rows(Y, i, l), ALU.add).then_inc(gf["add"], 1)
                                    hold(dve, "dve", gf["add"], WIDE * i + l + 1)
                                    nc.vector.tensor_tensor(xo[l][:, :, :], xo[l][:, :, :], wide_rows(X, i, l), ALU.add
                                                            ).then_inc(gf_lane[l], 1)

                    @block.scalar
                    def _(act):
                        with act.Fori(0, WIDE_STEPS) as i:
                            for l in lanes:
                                act.wait_ge(gf["sh"], gv(i, l))
                                nc.scalar.activation(hs[l][:, :, D // 2:D],
                                                     wide_banks(l, 0)[:, 0:T * D // 2].rearrange("p (t c) -> p t c", t=T),
                                                     ACT.Copy).then_inc(gf["shr"], 1)
                            for l in lanes:
                                act.wait_ge(gf["hTp"], gv(i, l))
                                nc.scalar.activation(hT[l][:, :], wide_banks(l, 1), ACT.Identity, scale=column(pre + "lg"),
                                                     bias=column(pre + "lb")).then_inc(gf["hT"], 1)
                            for k, (at, m) in enumerate(HID_CHUNKS):
                                for l in lanes:
                                    act.wait_ge(gf["ag"], cv(i, k, l))
                                    nc.scalar.activation(gl[l][k][0:m, :], wide_banks(l, 1)[0:m, :], ACT.Gelu,
                                                         bias=column(pre + "b1", NHC + k)[0:m]).then_inc(gf["gl"], 1)
                            for l in lanes:
                                act.wait_ge(gf["w2"], gv(i, l))
                                nc.scalar.activation(yT[l][:, :], wide_banks(l, 0), ACT.Identity, bias=column(pre + "b2")
                                                     ).then_inc(gf["yT"], 1)

                    @block.tensor
                    def _(pe):
                        with pe.Fori(0, WIDE_STEPS) as i:
                            for l in lanes:
                                hold(pe, "pe", gf_lane[l], i + 1)
                                nc.tensor.matmul(wide_banks(l, 0)[:, 0:T * D // 2].rearrange("p (t c) -> p t c", t=T),
                                                 shift[:, :], wide_rows(Y, i, l)[:, :, D // 2:D], start=True, stop=True
                                                 ).then_inc(gf["sh"], 1)
                            for l in lanes:
                                pe.wait_ge(ln["norm"], WIDE * i + l + 1)
                                transposes(wide_banks(l, 1), h[l]).then_inc(gf["hTp"], 1)
                            for k, (at, m) in enumerate(HID_CHUNKS):
                                for l in lanes:
                                    if k == 0:
                                        pe.wait_ge(gf["hT"], gv(i, l))
                                    else:
                                        pe.wait_ge(gf["u"], cv(i, k - 1, l))
                                    for j in range(2):
                                        op = nc.tensor.matmul(wide_banks(l, j)[0:m, :], w1[:, j * HID + at:j * HID + at + m],
                                                              hT[l][:, :], start=True, stop=True)
                                    op.then_inc(gf["ag"], 1)
                            for l in lanes:
                                for k, (at, m) in enumerate(HID_CHUNKS):
                                    if k == 0:
                                        pe.wait_ge(gf["u"], cv(i, NHC - 1, l))
                                    op = nc.tensor.matmul(wide_banks(l, 0), w2[0:m, k, :], uT[l][k][0:m, :], start=(k == 0),
                                                          stop=(k == NHC - 1))
                                op.then_inc(gf["w2"], 1)
                            for l in lanes:
                                pe.wait_ge(gf["yT"], gv(i, l))
                                for t in range(T):
                                    op = nc.tensor.transpose(wide_banks(l, 1)[:, t * P:(t + 1) * P], yT[l][:, t * P:(t + 1) * P],
                                                             ident[:, :])
                                op.then_inc(gf["yTp"], 1)

        stages = [
            lambda: small_attention("A0", False, False, 1.0 / math.sqrt(SMALL_DIM), 0, int8=True),
            lambda: small_attention("A1", True, False, 1.0 / math.sqrt(D), 1), routed_ffn,
            lambda: small_attention("A2", True, True, 1.0 / math.sqrt(SMALL_DIM), 2, spectral=True)]
        stages += [decoder_layer]
        for stage in stages:
            run_stage(stage)
        early_stages.close()
        Y = ctx.enter_context(nc.sbuf_tensor("Y", [P, TILES, D], F32))
        run_stage(lambda: start_stream(Y))
        for lyr in range(DEPTH):
            run_stage(lambda: window_attention(lyr, Y))
            run_stage(lambda: gated_ffn(lyr, Y, lyr == DEPTH - 1))


def host_layout(inputs):
    def rep(v):
        v = np.asarray(v, np.float32)
        return np.broadcast_to(v[None, :], (P, v.shape[0]))

    def block_diagonal(w):
        out = np.zeros((D, D), np.float32)
        for n in range(SMALL_HEADS):
            out[8 * n:8 * n + 8, 8 * n:8 * n + 8] = w
        return out

    p = np.arange(P)
    angle = 2 * np.pi * ((p[:, None] * p[None, :]) % D) / D
    half = np.arange(0, HEAD_DIM, 2, dtype=np.float32)
    inv = (1.0 / 10000.0 ** (half / HEAD_DIM)).astype(np.float32)
    n = (p % SEQ).astype(np.float32)
    freq = (n[:, None] * inv[None, :]).astype(np.float32)
    base = ((half + 0.4 * HEAD_DIM) / (1.4 * HEAD_DIM)).astype(np.float32)
    scale = (base[None, :] ** ((n[:, None] - SEQ // 2) / 32.0).astype(np.float32)).astype(np.float32)
    cos, sin = np.cos(freq), np.sin(freq)
    two = lambda a, b: np.concatenate([a, b], axis=1)
    k = {
        "ident": np.eye(P), "ones": np.ones((P, P)), "tri": p[:, None] <= p[None, :],
        "shift": (p[:, None] + 1 == p[None, :]) & (p[None, :] % SEQ != 0),
        "causal": np.where(np.arange(SEQ)[None, :] > (p % SEQ)[:, None], MASKED, 0.0),
        "head_cols": ((p // 8) % 4)[:, None] == np.arange(4)[None, :],
        "tie": np.broadcast_to((EXPERTS - np.arange(EXPERTS))[None, :], (P, EXPERTS)),
        "dft_cos": np.cos(angle), "dft_sin": np.sin(angle),
        "rope": np.concatenate([two(cos, cos) * two(scale, scale) * 8, two(cos, cos) / two(scale, scale),
                                two(-sin, sin) * two(scale, scale) * 8, two(-sin, sin) / two(scale, scale)], axis=1),
    }
    i = inputs
    w = {
        "A0_wo": i["L0_xattn_w_proj"].T, "A0_bo": rep(i["L0_xattn_b_proj"]), "F0_rhsT": i["L0_ffn_rhs"].T,
        "A1_wq": block_diagonal(i["L1_xattn_Wq"].T), "A1_wk": block_diagonal(i["L1_xattn_Wk"].T),
        "A1_wv": block_diagonal(i["L1_xattn_Wv"].T), "A1_wo": i["L1_xattn_Wo"].T, "A1_bo": rep(i["L1_xattn_bo"]),
        "F1_we": np.concatenate([i["L1_ffn_We"], i["L1_ffn_Wg"]], axis=1), "F1_be": rep(i["L1_ffn_be"]),
        "A2_wq": i["L2_xattn_Wq"], "A2_wk": i["L2_xattn_Wk"], "A2_wv": i["L2_xattn_Wv"], "A2_wo": i["L2_xattn_Wo"],
        "A2_bo": rep(i["L2_xattn_bo"]),
        "F2_wr": i["L2_ffn_w_freq_real"], "F2_wi": i["L2_ffn_w_freq_imag"], "F2_bias": rep(i["L2_ffn_bias"]),
        "A3_b2": rep(i["L3_xattn_b2"]), "A3_gamma": rep(i["L3_xattn_gamma"]),
        "A3_beta": rep(i["L3_xattn_beta"]), "A3_w1": i["L3_xattn_W1"], "A3_w2": i["L3_xattn_W2"],
    }
    for m in ("q1", "k1", "v1", "q2", "k2", "v2"):
        w["A3_w" + m] = i["L3_xattn_W" + m]
    cols = {"A2_bq": i["L2_xattn_bq"], "A2_bk": i["L2_xattn_bk"], "A2_bv": i["L2_xattn_bv"], "A3_b1": i["L3_xattn_b1"]}
    for l in range(2):
        f = f"F3_{l}_"
        qs, ks = i["L3_ffn_q_scale"][l], i["L3_ffn_k_scale"][l]
        hd = HEAD_DIM // 2
        swap = lambda v: np.concatenate([v[hd:], v[:hd]])
        w[f + "wqkv"] = i["L3_ffn_wqkv"][l]
        w[f + "scales"] = rep(np.concatenate([qs, ks, swap(qs), swap(ks)]))
        w[f + "wo"] = i["L3_ffn_wo"][l].reshape(4, P, D).transpose(1, 0, 2).reshape(P, 4 * D)
        cols[f + "lg"], cols[f + "lb"], cols[f + "b2"] = i["L3_ffn_ln_g"][l], i["L3_ffn_ln_b"][l], i["L3_ffn_b2"][l]
        w[f + "w1"] = i["L3_ffn_w1"][l]
        b1, w2 = np.zeros((P, 2 * NHC), np.float32), np.zeros((P, NHC, D), np.float32)
        for c, (at, m) in enumerate(HID_CHUNKS):
            b1[:m, c] = i["L3_ffn_b1"][l][at:at + m]
            b1[:m, NHC + c] = i["L3_ffn_b1"][l][HID + at:HID + at + m]
            w2[:m, c] = i["L3_ffn_w2"][l][at:at + m]
        for c in range(2 * NHC):
            cols[f"{f}b1{c}"] = b1[:, c]
        w[f + "w2"] = w2.reshape(P, NHC * D)
    w["columns"] = np.stack([np.asarray(cols[n], np.float32) for n in COLUMNS], axis=1)
    out = np.zeros((P, WEIGHT_COLS), np.float32)
    for name, n in LAYOUT:
        a = OFFSET[name][0]
        out[:, a:a + n] = w[name] if name in w else k[name]
    return out


def kernel(**inputs):
    from concourse import bacc
    from concourse.bass_utils import run_bass_kernel_spmd

    inputs = {n: np.asarray(v) for n, v in inputs.items()}
    tokens = BATCH * SEQ
    arrays = {
        "x_rows": np.ascontiguousarray(inputs["x"].reshape(tokens, D)),
        "ctx_t": np.ascontiguousarray(inputs["ctx_1024"].reshape(tokens, D).T),
        "mask_batch": np.ascontiguousarray(inputs["mask_Bx1xSxS2_ik1"].reshape(tokens, SEQ)),
        "mask_all": np.ascontiguousarray(inputs["mask_1x1xSxS2_if1"].reshape(SEQ, SEQ)),
        "weights": host_layout(inputs),
    }
    nc = bacc.Bacc("TRN2", target_bir_lowering=False, num_devices=1)
    args = [nc.dram_tensor(n, a.shape, mybir.dt.from_np(a.dtype), kind="ExternalInput").ap() for n, a in arrays.items()]
    out = nc.dram_tensor("y_rows", (tokens, D), F32, kind="ExternalOutput").ap()
    transformer_program(nc, *args, out)
    r = run_bass_kernel_spmd(nc, [arrays], core_ids=[0])
    return r.results[0]["y_rows"].reshape(BATCH, SEQ, D)
```

```python
import math
from contextlib import ExitStack

import numpy as np
import concourse.bass as bass
from concourse import mybir

F32 = mybir.dt.float32
BF16 = mybir.dt.bfloat16
I32 = mybir.dt.int32
ALU = mybir.AluOpType
ACT = mybir.ActivationFunctionType
AX = mybir.AxisListType.X

BATCH, SEQ, D = 128, 64, 128
P = 128
TILES = BATCH * SEQ // P
T = 4
ROWS = T * P
NB = ROWS // SEQ
GROUPS = TILES // T
LANES = 2
STEPS = GROUPS // LANES
WIDE = 4
WIDE_STEPS = GROUPS // WIDE
SMALL_HEADS, SMALL_DIM = 16, 8
Q4 = 4
HEADS, HEAD_DIM = 8, 64
INNER = HEADS * HEAD_DIM
DEPTH = 2
HID = int(D * 4 * 2 / 3)
HID_CHUNKS = [(c, min(P, HID - c)) for c in range(0, HID, P)]
NHC = len(HID_CHUNKS)
EXPERTS = 8
CAPACITY = BATCH * SEQ // EXPERTS
MASKED = -1.0e30
ROUND = 12582912.0
INT8_MAX = 127.0
RSQRT_SEED = float(0x5F3759DF)

COLUMNS = ["A2_bq", "A2_bk", "A2_bv", "A3_b1"]
for _l in range(2):
    COLUMNS += [f"F3_{_l}_lg", f"F3_{_l}_lb", f"F3_{_l}_b2"] + [f"F3_{_l}_b1{_k}" for _k in range(2 * NHC)]
LAYOUT = [
    ("columns", len(COLUMNS)),
    ("ident", P), ("ones", P), ("tri", P), ("shift", P), ("causal", SEQ), ("head_cols", Q4),
    ("tie", EXPERTS),
    ("A0_wo", D), ("A0_bo", D),
    ("F0_rhsT", D),
    ("A1_wq", D), ("A1_wk", D), ("A1_wv", D), ("A1_wo", D), ("A1_bo", D),
    ("F1_we", D + EXPERTS), ("F1_be", D),
    ("A2_wq", D), ("A2_wk", D), ("A2_wv", D), ("A2_wo", D), ("A2_bo", D),
    ("F2_wr", D), ("F2_wi", D), ("F2_bias", D), ("dft_cos", D), ("dft_sin", D),
    ("A3_wq1", D), ("A3_wk1", D), ("A3_wv1", D), ("A3_wq2", D), ("A3_wk2", D), ("A3_wv2", D),
    ("A3_w1", D), ("A3_w2", D), ("A3_b2", D), ("A3_gamma", D), ("A3_beta", D),
    ("rope", 4 * HEAD_DIM),
]
for _l in range(2):
    LAYOUT += [(f"F3_{_l}_wqkv", 3 * INNER), (f"F3_{_l}_scales", 4 * HEAD_DIM), (f"F3_{_l}_wo", 4 * D),
               (f"F3_{_l}_w1", 2 * HID), (f"F3_{_l}_w2", NHC * D)]
OFFSET, _at = {}, 0
for _name, _n in LAYOUT:
    OFFSET[_name] = (_at, _n)
    _at += _n
WEIGHT_COLS = _at
FIRST_COLS = OFFSET["A1_wq"][0]
EARLY_COLS = OFFSET["rope"][0]


def transformer_program(nc, x, ctxT, mask1, mask2, weights, out):
    ctx = ExitStack()
    with ctx:
        def keep(name):
            return ctx.enter_context(nc.semaphore(name))

        stage_sems, stages_run = [], [0]

        def sem(name):
            s = nc.alloc_semaphore(name=f"{name}_{stages_run[0]}")
            stage_sems.append(s)
            return s

        X = ctx.enter_context(nc.sbuf_tensor("X", [P, TILES, D], F32))
        Y = ctx.enter_context(nc.sbuf_tensor("Y", [P, TILES, D], F32))
        ident = ctx.enter_context(nc.sbuf_tensor("ident", [P, P], F32))
        ident_bf = ctx.enter_context(nc.sbuf_tensor("ident_bf", [P, P], BF16))
        causal_bf = ctx.enter_context(nc.sbuf_tensor("causal_bf", [P, SEQ], BF16))
        columns = ctx.enter_context(nc.sbuf_tensor("columns", [P, len(COLUMNS)], F32))
        mhalf = ctx.enter_context(nc.sbuf_tensor("mhalf", [P, 1], F32))
        st = [ctx.enter_context(nc.sbuf_tensor(f"st{l}", [P, T, 6], F32)) for l in range(WIDE)]
        mv = [ctx.enter_context(nc.sbuf_tensor(f"mv{l}", [P, T, 2], F32)) for l in range(WIDE)]
        ve = [ctx.enter_context(nc.sbuf_tensor(f"ve{l}", [P, T], F32)) for l in range(WIDE)]
        rstd = [ctx.enter_context(nc.sbuf_tensor(f"rstd{l}", [P, T], F32)) for l in range(WIDE)]
        h = [ctx.enter_context(nc.sbuf_tensor(f"h{l}", [P, T, D], F32)) for l in range(WIDE)]
        hT = [ctx.enter_context(nc.sbuf_tensor(f"hT{l}", [P, ROWS], F32)) for l in range(WIDE)]
        PS = ctx.enter_context(nc.psum_tensor("PS", [P, 8, 512], F32))

        def wide_banks(l, k, n=1):
            return PS[:, 2 * l + k:2 * l + k + n, :].rearrange("p b c -> p (b c)")

        loads = [0]
        loaded = keep("loaded")
        ticks = {e: keep(f"tick_{e}") for e in ("pe", "act", "dve", "pool", "sp")}

        def hold(eng, name, s, v):
            eng.wait_ge(s, v)
            eng.sem_inc(ticks[name], 1)

        def load(sp, dst, name):
            a, cols = OFFSET[name]
            sp.dma_start(dst, weights[:, a:a + cols]).then_inc(loaded, 16)
            loads[0] += 16

        early_stages = ExitStack()
        early = early_stages.enter_context(nc.sbuf_tensor("early", [P, EARLY_COLS], F32))
        rest_loaded = keep("rest_loaded")
        x_loaded = [keep("x_first_loaded"), keep("x_rest_loaded")]

        def constant(name):
            a, cols = OFFSET[name]
            return early[:, a:a + cols]

        def column(name, k=None):
            at = COLUMNS.index(name if k is None else f"{name}{k}")
            return columns[:, at:at + 1]

        def wide_rows(t, i, l):
            return t[:, bass.ds(WIDE * T * i + T * l, T), :]

        def wide_row(t, i, l, k):
            return t[:, bass.ds(WIDE * T * i + (T * l + k), 1), :].rearrange("p a c -> p (a c)")

        with nc.Block() as block:
            @block.sync
            def _(sp):
                load(sp, ident[:, :], "ident")
                load(sp, columns[:, :], "columns")
                sp.dma_start(early[:, 0:FIRST_COLS], weights[:, 0:FIRST_COLS]).then_inc(loaded, 16)
                loads[0] += 16
                for part, tiles in enumerate((slice(0, T * T), slice(T * T, TILES))):
                    sp.dma_start(X[:, tiles, :], x[P * tiles.start:P * tiles.stop, :].rearrange("(t p) c -> p t c", p=P)
                                 ).then_inc(x_loaded[part], 16)
                sp.dma_start(early[:, FIRST_COLS:EARLY_COLS], weights[:, FIRST_COLS:EARLY_COLS]).then_inc(rest_loaded, 16)
                sp.wait_ge(loaded, loads[0])

        base_ready = keep("base_ready")
        with nc.Block() as block:
            @block.vector
            def _(dve):
                nc.vector.memset(mhalf[:, :], -0.5)
                nc.vector.tensor_copy(ident_bf[:, :], ident[:, :])
                nc.vector.tensor_copy(causal_bf[:, :], constant("causal")[:, 0:SEQ]).then_inc(base_ready, 1)
                dve.wait_ge(base_ready, 1)

        ln = {}

        def run_stage(stage):
            ln.update({n: sem("ln_" + n) for n in ("bn", "var", "ve", "rstd", "norm", "hTp", "hT")})
            stage()
            with nc.Block() as block:
                @block.gpsimd
                def _(pool):
                    nc.clear_and_free_semaphores(stage_sems)
            stage_sems.clear()
            stages_run[0] += 1

        def ln_stats(dve, v, l, src, ev=ln):
            for t in range(T):
                op = nc.vector.bn_stats(st[l][:, t, :], src(t))
            op.then_inc(ev["bn"], 1)
            hold(dve, "dve", ev["bn"], v)
            for t in range(T):
                op = nc.vector.bn_aggr(mv[l][:, t, :], st[l][:, t, :])
            op.then_inc(ev["var"], 1)

        def ln_rstd(pool, v, l, eps, ev=ln):
            hold(pool, "pool", ev["var"], v)
            nc.gpsimd.tensor_scalar(ve[l][:, :], mv[l][:, :, 1], 1.0, eps, ALU.mult, ALU.add).then_inc(ev["ve"], 1)
            pool.wait_ge(ev["ve"], v)
            nc.gpsimd.tensor_tensor(rstd[l][:, :], ve[l][:, :], mhalf[:, 0:1].to_broadcast([P, T]), ALU.pow
                                    ).then_inc(ev["rstd"], 1)

        def ln_norm(dve, v, l, src, dst, ev=ln):
            hold(dve, "dve", ev["rstd"], v)
            for t in range(T):
                op = nc.vector.tensor_scalar(dst(t), src(t), mv[l][:, t, 0:1], rstd[l][:, t:t + 1],
                                             ALU.subtract, ALU.mult)
            op.then_inc(ev["norm"], 1)

        def transposes(dst, src):
            for t in range(T):
                op = nc.tensor.transpose(dst[:, t * P:(t + 1) * P], src[:, t, :], ident[:, :])
            return op


        def exists(i, k, unit, count):
            return not isinstance(i, int) or 0 <= unit * i + k < count

        def tile_exists(i, k):
            return exists(i, k, 2 * T, TILES)

        def group_exists(i, m):
            return exists(i, m, 2, GROUPS)

        def run_steps(eng, steps, step, lag=0):
            for i in range(-2, 1 + lag):
                for n in range(steps):
                    step(i, n)
            with eng.Fori(1 + lag, STEPS - 2) as i:
                for n in range(steps):
                    step(i, n)
            for i in range(STEPS - 2, STEPS + 1 + lag):
                for n in range(steps):
                    step(i, n)

        PAIR_A, PAIR_B, NEXT_A = (0, 1), (2, 3), (4, 5)

        def cv(i, g):
            return WIDE * i + (g + 1)

        def run_halves(eng, order, first, second):
            turns = [(half, order[:n].count(half)) for n, half in enumerate(order)]

            def body(i, more):
                for half, k in turns:
                    if half:
                        second(i, PAIR_A, k)
                    else:
                        first(i, PAIR_B, k)
                for half, k in turns:
                    if half:
                        second(i, PAIR_B, k)
                    elif more:
                        first(i, NEXT_A, k)

            for k in range(order.count(0)):
                first(0, PAIR_A, k)
            with eng.Fori(0, WIDE_STEPS - 1) as i:
                body(i, True)
            body(WIDE_STEPS - 1, False)

        def gv(i, m):
            return 2 * i + (m + 1)

        def group_rows(t, i, m):
            return t[:, bass.ds(2 * T * i + T * m, T), :]

        def group_row(t, i, m, k):
            return t[:, bass.ds(2 * T * i + (T * m + k), 1), :].rearrange("p a c -> p (a c)")


        def bf(ap):
            return ap.bitcast(BF16)

        def quantised_weights(i8, sb):
            rhsT, ones = constant("F0_rhsT"), constant("ones")
            ws, wr = sb("ws", [P, 1]), sb("wr", [P, 1])
            wdiag, wqf, wqT = sb("wdiag", [P, P]), sb("wqf", [P, D]), sb("wqT", [P, D], BF16)
            wq, wscale = sb("wq8", [P, D], BF16), sb("wscale", [P, D])
            with nc.Block() as block:
                @block.vector
                def _(dve):
                    nc.vector.tensor_reduce(ws[:, :], rhsT[:, :], op=ALU.max, axis=AX, apply_absolute_value=True
                                            ).then_inc(i8["w"], 1)
                    dve.wait_ge(i8["w"], 1)
                    nc.vector.tensor_scalar(ws[:, :], ws[:, :], 1e-12, 1.0 / INT8_MAX, ALU.max, ALU.mult
                                            ).then_inc(i8["w"], 1)
                    dve.wait_ge(i8["w"], 2)
                    nc.vector.reciprocal(wr[:, :], ws[:, :])
                    nc.vector.tensor_scalar(wdiag[:, :], ident[:, :], ws[:, 0:1], None, ALU.mult).then_inc(i8["w"], 1)
                    dve.wait_ge(i8["w"], 3)
                    nc.vector.tensor_scalar(wqf[:, :], rhsT[:, :], wr[:, 0:1], ROUND, ALU.mult, ALU.add
                                            ).then_inc(i8["w"], 1)
                    dve.wait_ge(i8["w"], 4)
                    nc.vector.tensor_scalar(wqf[:, :], wqf[:, :], ROUND + INT8_MAX, ROUND - INT8_MAX, ALU.min, ALU.max
                                            ).then_inc(i8["w"], 1)
                    dve.wait_ge(i8["w"], 5)
                    nc.vector.tensor_scalar(wqT[:, :], wqf[:, :], ROUND, None, ALU.subtract).then_inc(i8["w"], 1)
                    dve.wait_ge(i8["w"], 8)
                    nc.vector.tensor_copy(wq[:, :], bf(PS[:, 0, 0:64]))
                    nc.vector.tensor_copy(wscale[:, :], PS[:, 1, 0:D]).then_inc(i8["w"], 1)
                    dve.wait_ge(i8["w"], 9)

                @block.tensor
                def _(pe):
                    pe.wait_ge(i8["w"], 6)
                    nc.tensor.transpose(bf(PS[:, 0, 0:64]), wqT[:, :], ident_bf[:, :]).then_inc(i8["w"], 1)
                    nc.tensor.matmul(PS[:, 1, 0:D], ones[:, :], wdiag[:, :], start=True, stop=True
                                     ).then_inc(i8["w"], 1)
            return wq, wscale


        def spectral_matrix(sf, sb):
            wr, wi, co, si = (constant(n) for n in ("F2_wr", "F2_wi", "dft_cos", "dft_sin"))
            sn, at, bt, m = (sb(n, [P, D]) for n in ("sn", "at", "bt", "m"))
            with nc.Block() as block:
                @block.tensor
                def _(pe):
                    pe.wait_ge(sf["a"], 1)
                    nc.tensor.matmul(PS[:, 0, 0:D], wr[:, :], co[:, :], start=True, stop=False)
                    nc.tensor.matmul(PS[:, 0, 0:D], wi[:, :], si[:, :], start=False, stop=True)
                    nc.tensor.matmul(PS[:, 1, 0:D], wr[:, :], si[:, :], start=True, stop=False)
                    nc.tensor.matmul(PS[:, 1, 0:D], wi[:, :], sn[:, :], start=False, stop=True).then_inc(sf["p1"], 1)
                    pe.wait_ge(sf["a"], 2)
                    nc.tensor.matmul(PS[:, 2, 0:D], at[:, :], co[:, :], start=True, stop=False)
                    nc.tensor.matmul(PS[:, 2, 0:D], bt[:, :], si[:, :], start=False, stop=True).then_inc(sf["p2"], 1)

                @block.vector
                def _(dve):
                    nc.vector.tensor_scalar(sn[:, :], co[:, :], -1.0, None, ALU.mult).then_inc(sf["a"], 1)
                    dve.wait_ge(sf["p1"], 1)
                    nc.vector.tensor_copy(at[:, :], PS[:, 0, 0:D])
                    nc.vector.tensor_copy(bt[:, :], PS[:, 1, 0:D]).then_inc(sf["a"], 1)
                    dve.wait_ge(sf["p2"], 1)
                    nc.vector.tensor_scalar(m[:, :], PS[:, 2, 0:D], 1.0 / D, None, ALU.mult).then_inc(sf["b"], 1)
                    dve.wait_ge(sf["b"], 1)
            return m


        def small_attention(name, project, biased, score_scale, mask_kind, int8=False, routed=False, spectral=False):
            sa_mk = [sem(f"sa_mask{l}") for l in range(LANES)]
            sa_ready = sem("sa_ready")
            sa_cg = [sem(f"sa_context{l}") for l in range(LANES)]
            sa = {n: sem("sa_" + n) for n in (
                "kvp", "kT", "vT", "kb", "vdp", "vb", "qp", "q", "bias", "scores", "max", "sub",
                "exp", "sum", "rec", "pn", "ptp", "pt", "av", "o", "out", "ob", "X", "mask")}
            if int8:
                i8 = {n: sem("i8_" + n) for n in ("w", "amax", "scale", "rec", "round", "clip", "q", "qTp", "qT", "acc",
                                                  "ac", "tmp", "X")}
            if spectral:
                sf = {n: sem("sf_" + n) for n in ("p1", "a", "p2", "b", "bias", "hTp", "hT", "out", "ac", "X")}
            if routed:
                mo = {n: sem("mo_" + n) for n in (
                    "zero", "hTp", "hT", "lin", "ac", "lt", "e", "lg", "lm", "ls", "ex", "eq", "tie", "tm", "oh", "c", "ct",
                    "den", "run", "pos", "fit", "keep", "kp", "cf", "X")}
            if int8 or routed or spectral:
                lnf = {n: sem("lnf_" + n) for n in ("bn", "var", "ve", "rstd", "norm")}
            with ExitStack() as c:
                def sb(n, shape, dt=F32):
                    return c.enter_context(nc.sbuf_tensor(f"{name}_{n}", shape, dt))
                wo, bo, head_cols = constant(f"{name}_wo"), constant(f"{name}_bo"), constant("head_cols")
                if project:
                    wq, wk, wv = (constant(f"{name}_{n}") for n in ("wq", "wk", "wv"))
                bq, bk, bv = (column(f"{name}_{n}") if biased else 0.0 for n in ("bq", "bk", "bv"))
                lanes = range(LANES)
                xb = [sb(f"xb{l}", [P, 2, D]) for l in lanes]
                ob = [sb(f"ob{l}", [P, 2, D]) for l in lanes]
                cg = [sb(f"cg{l}", [P, ROWS]) for l in lanes]
                kT = [sb(f"kT{l}", [P, ROWS]) if project else cg[l] for l in lanes]
                vT = [sb(f"vT{l}", [P, NB, 2, SEQ]) for l in lanes]
                kb = [sb(f"kb{l}", [P, NB, Q4, SEQ]) for l in lanes]
                vb = [sb(f"vb{l}", [P, NB, 8, 32]) for l in lanes]
                qT = [sb(f"qT{l}", [P, ROWS]) if project else hT[l] for l in lanes]
                pr = [sb(f"pr{l}", [P, 2048]) for l in lanes]
                pT = sb("pT", [P, 2, 8, P])
                mx, sums = sb("mx", [P, 32]), sb("sums", [P, 32])
                rec = [sb(f"rec{l}", [P, 32]) for l in lanes]
                oT = [sb(f"oT{l}", [P, 2 * P]) for l in lanes]
                if mask_kind == 1:
                    nm = [sb(f"nm{l}", [P, T, SEQ], BF16) for l in lanes]
                    mraw = [sb(f"mraw{l}", [P, T, SEQ], I32) for l in lanes]
                elif mask_kind == 2:
                    nm = sb("nm", [P, SEQ], BF16)
                    mraw = sb("mraw", [P, SEQ], I32)

                if int8:
                    wq8, wscale = quantised_weights(i8, sb)
                    am, rc = sb("am", [P, T]), sb("rc", [P, T])
                    sc = [sb(f"sc{l}", [P, T]) for l in lanes]
                    qr, tmp, ac = (sb(n, [P, T, D]) for n in ("qr", "tmp", "ac"))
                    qb, qT8 = sb("qb", [P, T, D], BF16), sb("qT8", [P, ROWS], BF16)

                if routed:
                    E = EXPERTS
                    we, be, tie = constant("F1_we"), constant("F1_be"), constant("tie")
                    tri, ones = sb("tri", [P, P], BF16), sb("ones", [P, P], BF16)
                    run = sb("run", [P, 2, T, E])
                    ac, lt = sb("ac", [P, T, D]), sb("lt", [P, T, D])
                    lg, ls, ex, eq, pos = (sb(n, [P, T, E]) for n in ("lg", "ls", "ex", "eq", "pos"))
                    ct = sb("ct", [P, 2, T, E])
                    oh = sb("oh", [P, T, E], BF16)
                    lm, den, gate, tm, kp, cf = (sb(n, [P, T]) for n in ("lm", "den", "gate", "tm", "kp", "cf"))
                    LOGITS = PS[:, 3, 2 * P:2 * P + T * E]
                    COUNTS = PS[:, 3, 2 * P:2 * P + 2 * T * E]
                    with nc.Block() as block:
                        @block.vector
                        def _(dve):
                            nc.vector.tensor_copy(tri[:, :], constant("tri"))
                            nc.vector.tensor_copy(ones[:, :], constant("ones"))
                            nc.vector.memset(run[:, :, :, :], 0.0).then_inc(mo["zero"], 1)
                            dve.wait_ge(mo["zero"], 1)

                    def over(ap):
                        return ap.unsqueeze(2).to_broadcast([P, T, E])

                if spectral:
                    M, bias = spectral_matrix(sf, sb), constant("F2_bias")
                    ac = sb("ac", [P, T, D])

                def seen(mask, ones):
                    return nc.vector.tensor_scalar(mask, ones, 0.0, MASKED, ALU.is_equal, ALU.mult).then_inc(sa["mask"], 1)

                with nc.Block() as block:
                    @block.gpsimd
                    def _(pool):
                        for l in lanes:
                            op = nc.gpsimd.memset(vb[l][:, :, :, :], 0.0)
                        op.then_inc(sa_ready, 1)
                        pool.wait_ge(sa_ready, 1)

                    if mask_kind == 2:
                        @block.sync
                        def _(sp):
                            for b in range(2):
                                sp.dma_start(mraw[SEQ * b:SEQ * (b + 1), :], mask2).then_inc(loaded, 16)
                                loads[0] += 16

                        @block.vector
                        def _(dve):
                            dve.wait_ge(loaded, loads[0])
                            seen(nm[:, :], mraw[:, :])
                            dve.wait_ge(sa["mask"], 1)

                HALVES = 4
                SC = PS[:, 0:4, :].rearrange("p b c -> p (b c)")
                PTP = PS[:, 4:8, :].rearrange("p b c -> p (b c)")
                O = PS[:, 4, 0:2 * P]
                OUT = PS[:, 3, 0:2 * P]
                VD = PS[:, 5, :]
                KP = HP = PS[:, 6, :]
                VP = QP = PS[:, 7, :]
                I8 = PS[:, 7, :]

                def half_exists(i, k):
                    return exists(i, k, HALVES, 2 * GROUPS)

                def hv(i, k):
                    return HALVES * i + (k + 1)

                def half_rows(t, i, k):
                    return t[:, bass.ds(2 * T * i + 2 * k, 2), :]

                def loaded_for(sems, i, m):
                    return sems[m % 2], 16 * i + 16 * (m // 2 + 1)

                with nc.Block() as block:
                    @block.sync
                    def _(sp):
                        def load_group(i, l):
                            rows = bass.ds(2 * ROWS * i + ROWS * l, ROWS)
                            if mask_kind == 1:
                                sp.dma_start(mraw[l][:, :, :], mask1[rows, :].rearrange("(t p) k -> p t k", p=P)
                                             ).then_inc(sa_mk[l], 16)
                            sp.dma_start(cg[l][:, :], ctxT[:, rows]).then_inc(sa_cg[l], 16)

                        for l in lanes:
                            load_group(0, l)
                        with sp.Fori(1, STEPS) as i:
                            for l in lanes:
                                for event in ("kvp",) if project else ("kb", "vT"):
                                    hold(sp, "sp", sa[event], 2 * i + (l - 1))
                                if mask_kind == 1:
                                    hold(sp, "sp", sa["mask"], 2 * i + (l - 1))
                                load_group(i, l)
                        if name == "A0":
                            sp.wait_ge(rest_loaded, 16)

                    @block.gpsimd
                    def _(pool):
                        def step(i, n):
                            m, odd = divmod(n, 2)
                            if spectral and not odd and group_exists(i, m - 3):
                                hold(pool, "pool", lnf["norm"], gv(i, m - 3))
                                nc.gpsimd.tensor_tensor(group_rows(X, i, m - 3), group_rows(X, i, m - 3),
                                                        bias.unsqueeze(1).to_broadcast([P, T, D]), ALU.add
                                                        ).then_inc(sf["bias"], 1)
                            if routed and not odd and group_exists(i, m - 4):
                                hold(pool, "pool", mo["ac"], gv(i, m - 4))
                                if group_exists(i, m - 5):
                                    hold(pool, "pool", mo["X"], gv(i, m - 5))
                                nc.gpsimd.tensor_tensor(lt[:, :, :], ac[:, :, :], be.unsqueeze(1).to_broadcast([P, T, D]),
                                                        ALU.add).then_inc(mo["lt"], 1)
                            if (int8 or routed or spectral) and odd and group_exists(i, m - 2):
                                ln_rstd(pool, gv(i, m - 2), 2 + m % 2, 1e-5, lnf)
                            if not odd and group_exists(i, m + 2):
                                ln_rstd(pool, gv(i, m + 2), (m + 2) % 2, 1e-5)
                            if not odd and group_exists(i, m + 1):
                                l = (m + 1) % 2
                                if project:
                                    hold(pool, "pool", sa["kT"], gv(i, m + 1))
                                else:
                                    hold(pool, "pool", *loaded_for(sa_cg, i, m + 1))
                                for j in range(Q4):
                                    op = nc.gpsimd.tensor_scalar(
                                        kb[l][:, :, j, :], kT[l][:, :].rearrange("p (b k) -> p b k", b=NB),
                                        bk, head_cols[:, j:j + 1], ALU.add, ALU.mult)
                                op.then_inc(sa["kb"], 1)
                            if half_exists(i, n - 2):
                                if half_exists(i, n - 4):
                                    hold(pool, "pool", sa["X"], hv(i, n - 4))
                                nc.gpsimd.tensor_tensor(xb[n % 2][:, :, :], half_rows(X, i, n - 2),
                                                        bo[:, :].unsqueeze(1).to_broadcast([P, 2, D]), ALU.add
                                                        ).then_inc(sa["bias"], 1)
                            if half_exists(i, n):
                                q = pr[n % 2][:, :].rearrange("p (n k) -> p n k", k=SEQ)
                                hold(pool, "pool", sa["rec"], hv(i, n))
                                nc.gpsimd.tensor_tensor(q, q, rec[n % 2][:, :].unsqueeze(2).to_broadcast([P, 32, SEQ]),
                                                        ALU.mult).then_inc(sa["pn"], 1)

                        run_steps(pool, HALVES, step, lag=int(int8 or routed or spectral))

                    @block.vector
                    def _(dve):
                        def quantise(i, m):
                            l, v = m % 2, gv(i, m)
                            hb = h[2 + l]
                            ln_norm(dve, v, 2 + l, lambda t: group_row(X, i, m, t), lambda t: hb[:, t, :], lnf)
                            dve.wait_ge(lnf["norm"], v)
                            nc.vector.tensor_reduce(am[:, :], hb[:, :, :], op=ALU.max, axis=AX, apply_absolute_value=True
                                                    ).then_inc(i8["amax"], 1)
                            dve.wait_ge(i8["amax"], v)
                            nc.vector.tensor_scalar(sc[l][:, :], am[:, :], 1e-12, 1.0 / INT8_MAX, ALU.max, ALU.mult
                                                    ).then_inc(i8["scale"], 1)
                            dve.wait_ge(i8["scale"], v)
                            nc.vector.reciprocal(rc[:, :], sc[l][:, :]).then_inc(i8["rec"], 1)
                            dve.wait_ge(i8["rec"], v)
                            for t in range(T):
                                op = nc.vector.tensor_scalar(qr[:, t, :], hb[:, t, :], rc[:, t:t + 1], ROUND,
                                                             ALU.mult, ALU.add)
                            op.then_inc(i8["round"], 1)
                            dve.wait_ge(i8["round"], v)
                            nc.vector.tensor_scalar(qr[:, :, :], qr[:, :, :], ROUND + INT8_MAX, ROUND - INT8_MAX,
                                                    ALU.min, ALU.max).then_inc(i8["clip"], 1)
                            dve.wait_ge(i8["clip"], v)
                            if group_exists(i, m - 1):
                                hold(dve, "dve", i8["qTp"], gv(i, m - 1))
                            nc.vector.tensor_scalar(qb[:, :, :], qr[:, :, :], ROUND, None, ALU.subtract
                                                    ).then_inc(i8["q"], 1)

                        def choose(i, m):
                            v = gv(i, m)
                            dve.wait_ge(mo["lg"], v)
                            nc.vector.tensor_reduce(lm[:, :], lg[:, :, :], op=ALU.max, axis=AX).then_inc(mo["lm"], 1)
                            dve.wait_ge(mo["lm"], v)
                            nc.vector.tensor_tensor(ls[:, :, :], lg[:, :, :], over(lm[:, :]), ALU.subtract
                                                    ).then_inc(mo["ls"], 1)
                            dve.wait_ge(mo["ls"], v)
                            nc.vector.tensor_scalar(eq[:, :, :], ls[:, :, :], 0.0, None, ALU.is_equal).then_inc(mo["eq"], 1)
                            dve.wait_ge(mo["eq"], v)
                            nc.vector.tensor_tensor(eq[:, :, :], eq[:, :, :], tie.unsqueeze(1).to_broadcast([P, T, E]),
                                                    ALU.mult).then_inc(mo["tie"], 1)
                            dve.wait_ge(mo["tie"], v)
                            nc.vector.tensor_reduce(tm[:, :], eq[:, :, :], op=ALU.max, axis=AX).then_inc(mo["tm"], 1)
                            dve.wait_ge(mo["tm"], v)
                            nc.vector.tensor_tensor(oh[:, :, :], eq[:, :, :], over(tm[:, :]), ALU.is_equal
                                                    ).then_inc(mo["oh"], 1)

                        def admit(i, m):
                            l, v = m % 2, gv(i, m)
                            dve.wait_ge(mo["ex"], v)
                            nc.vector.tensor_reduce(den[:, :], ex[:, :, :], op=ALU.add, axis=AX).then_inc(mo["den"], 1)
                            dve.wait_ge(mo["den"], v)
                            nc.vector.reciprocal(gate[:, :], den[:, :])
                            dve.wait_ge(mo["ct"], v)
                            for t in range(T):
                                nxt = run[:, l, t + 1, :] if t < T - 1 else run[:, 1 - l, 0, :]
                                nc.vector.tensor_tensor(nxt, run[:, l, t, :], ct[:, 1, t, :], ALU.add
                                                        ).then_inc(mo["run"], 1)
                                dve.wait_ge(mo["run"], 2 * T * i + (T * m + t + 1))
                            nc.vector.tensor_tensor(pos[:, :, :], run[:, l, :, :], ct[:, 0, :, :], ALU.add
                                                    ).then_inc(mo["pos"], 1)
                            dve.wait_ge(mo["pos"], v)
                            nc.vector.tensor_scalar(pos[:, :, :], pos[:, :, :], float(CAPACITY), None, ALU.is_le
                                                    ).then_inc(mo["fit"], 1)
                            dve.wait_ge(mo["fit"], v)
                            nc.vector.tensor_tensor(pos[:, :, :], pos[:, :, :], oh[:, :, :], ALU.mult
                                                    ).then_inc(mo["keep"], 1)
                            dve.wait_ge(mo["keep"], v)
                            nc.vector.tensor_reduce(kp[:, :], pos[:, :, :], op=ALU.add, axis=AX).then_inc(mo["kp"], 1)
                            dve.wait_ge(mo["kp"], v)
                            nc.vector.tensor_tensor(cf[:, :], kp[:, :], gate[:, :], ALU.mult).then_inc(mo["cf"], 1)
                            hold(dve, "dve", mo["cf"], v)
                            hold(dve, "dve", mo["lt"], v)
                            for t in range(T):
                                op = nc.vector.scalar_tensor_tensor(group_row(X, i, m, t), lt[:, t, :], cf[:, t:t + 1],
                                                                    group_row(X, i, m, t), ALU.mult, ALU.add)
                            op.then_inc(mo["X"], 1)

                        def dequantise(i, m):
                            v = gv(i, m)
                            hold(dve, "dve", i8["ac"], v)
                            if group_exists(i, m - 1):
                                hold(dve, "dve", i8["X"], gv(i, m - 1))
                            for t in range(T):
                                op = nc.vector.scalar_tensor_tensor(tmp[:, t, :], ac[:, t, :], sc[m % 2][:, t:t + 1],
                                                                    wscale[:, :], ALU.mult, ALU.mult)
                            op.then_inc(i8["tmp"], 1)
                            hold(dve, "dve", i8["tmp"], v)
                            nc.vector.tensor_tensor(group_rows(X, i, m), group_rows(X, i, m), tmp[:, :, :], ALU.add
                                                    ).then_inc(i8["X"], 1)

                        def step(i, n):
                            m, odd = divmod(n, 2)
                            if routed and group_exists(i, m - 4):
                                if odd:
                                    admit(i, m - 4)
                                else:
                                    choose(i, m - 4)
                            if half_exists(i, n):
                                q, v = n % 2, hv(i, n)
                                S, R = (t.rearrange("p (n k) -> p n k", k=SEQ) for t in (SC, pr[q][:, :]))
                                dve.wait_ge(sa["scores"], v)
                                nc.vector.tensor_reduce(mx[:, :], S, op=ALU.max, axis=AX).then_inc(sa["max"], 1)
                                dve.wait_ge(sa["max"], v)
                                nc.vector.tensor_tensor(R, S, mx[:, :].unsqueeze(2).to_broadcast([P, 32, SEQ]),
                                                        ALU.subtract).then_inc(sa["sub"], 1)
                            k = n - 3
                            if half_exists(i, k):
                                hold(dve, "dve", sa["bias"], hv(i, k))
                                hold(dve, "dve", sa["ob"], hv(i, k))
                                nc.vector.tensor_tensor(half_rows(X, i, k), ob[k % 2][:, :, :], xb[k % 2][:, :, :], ALU.add
                                                        ).then_inc(sa["X"], 1)
                            if not odd and mask_kind == 1 and group_exists(i, m + 1):
                                l = (m + 1) % 2
                                hold(dve, "dve", *loaded_for(sa_mk, i, m + 1))
                                seen(nm[l][:, :, :], mraw[l][:, :, :])
                            if odd and group_exists(i, m + 3):
                                if name == "A0" and isinstance(i, int) and 2 * i + m + 3 == 0:
                                    dve.wait_ge(x_loaded[0], 16)
                                if name == "A0" and isinstance(i, int) and 2 * i + m + 3 == T:
                                    dve.wait_ge(x_loaded[1], 16)
                                ln_stats(dve, gv(i, m + 3), (m + 3) % 2, lambda t: group_row(X, i, m + 3, t))
                            if not odd and group_exists(i, m + 2):
                                ln_norm(dve, gv(i, m + 2), m % 2, lambda t: group_row(X, i, m + 2, t),
                                        lambda t: h[m % 2][:, t, :])
                            if int8 or routed or spectral:
                                if not odd and group_exists(i, m - 2):
                                    hold(dve, "dve", sa["X"], hv(i, 2 * m - 3))
                                    ln_stats(dve, gv(i, m - 2), 2 + m % 2, lambda t: group_row(X, i, m - 2, t), lnf)
                                if odd and group_exists(i, m - 2):
                                    if int8:
                                        quantise(i, m - 2)
                                    else:
                                        ln_norm(dve, gv(i, m - 2), 2 + m % 2, lambda t: group_row(X, i, m - 2, t),
                                                lambda t: h[2 + m % 2][:, t, :], lnf)
                                if not odd and group_exists(i, m - 4):
                                    if int8:
                                        dequantise(i, m - 4)
                                    elif spectral:
                                        hold(dve, "dve", sf["bias"], gv(i, m - 4))
                                        hold(dve, "dve", sf["ac"], gv(i, m - 4))
                                        nc.vector.tensor_tensor(group_rows(X, i, m - 4), group_rows(X, i, m - 4),
                                                                ac[:, :, :], ALU.add).then_inc(sf["X"], 1)
                            if half_exists(i, n):
                                dve.wait_ge(sa["exp"], v)
                                nc.vector.tensor_reduce(sums[:, :], R, op=ALU.add, axis=AX).then_inc(sa["sum"], 1)
                                dve.wait_ge(sa["sum"], v)
                                nc.vector.reciprocal(rec[q][:, :], sums[:, :]).then_inc(sa["rec"], 1)

                        run_steps(dve, HALVES, step, lag=int(int8 or routed or spectral))

                    @block.scalar
                    def _(act):
                        def step(i, n):
                            m, odd = divmod(n, 2)
                            k = n - 3
                            if half_exists(i, k):
                                act.wait_ge(sa["out"], hv(i, k))
                                if half_exists(i, k - 2):
                                    act.wait_ge(sa["X"], hv(i, k - 2))
                                nc.scalar.activation(ob[k % 2][:, :, :].rearrange("p t c -> p (t c)"), OUT, ACT.Copy
                                                     ).then_inc(sa["ob"], 1)
                            if routed and group_exists(i, m - 4):
                                if not odd:
                                    act.wait_ge(mo["e"], gv(i, m - 4))
                                    nc.scalar.activation(lg[:, :, :].rearrange("p t e -> p (t e)"), LOGITS, ACT.Copy
                                                         ).then_inc(mo["lg"], 1)
                                else:
                                    act.wait_ge(mo["c"], gv(i, m - 4))
                                    nc.scalar.activation(ct[:, :, :, :].rearrange("p a t e -> p (a t e)"), COUNTS, ACT.Copy
                                                         ).then_inc(mo["ct"], 1)
                            k = n - 2
                            if half_exists(i, k):
                                act.wait_ge(sa["ptp"], hv(i, k))
                                nc.scalar.activation(pT[:, :, :, :].rearrange("p t n q -> p (t n q)"), PTP, ACT.Copy
                                                     ).then_inc(sa["pt"], 1)
                            if routed and not odd and group_exists(i, m - 3):
                                act.wait_ge(mo["hTp"], gv(i, m - 3))
                                nc.scalar.activation(hT[2][:, :], PS[:, 4, :], ACT.Copy).then_inc(mo["hT"], 1)
                            if routed and odd and group_exists(i, m - 3):
                                act.wait_ge(mo["lin"], gv(i, m - 3))
                                if group_exists(i, m - 4):
                                    act.wait_ge(mo["lt"], gv(i, m - 4))
                                nc.scalar.activation(ac[:, :, :].rearrange("p t c -> p (t c)"), PS[:, 4, :], ACT.Copy
                                                     ).then_inc(mo["ac"], 1)
                            if spectral and not odd and group_exists(i, m - 3):
                                act.wait_ge(sf["hTp"], gv(i, m - 3))
                                nc.scalar.activation(hT[2][:, :], PS[:, 4, :], ACT.Copy).then_inc(sf["hT"], 1)
                            if spectral and odd and group_exists(i, m - 3):
                                act.wait_ge(sf["out"], gv(i, m - 3))
                                if group_exists(i, m - 4):
                                    act.wait_ge(sf["X"], gv(i, m - 4))
                                nc.scalar.activation(ac[:, :, :].rearrange("p t c -> p (t c)"), PS[:, 4, :], ACT.Copy
                                                     ).then_inc(sf["ac"], 1)
                            k = n + 1
                            if half_exists(i, k):
                                act.wait_ge(sa["vdp"], hv(i, k))
                                l, b = k // 2 % 2, slice(4 * (k % 2), 4 * (k % 2) + 4)
                                for head in range(4):
                                    r = slice(SEQ * (head % 2), SEQ * (head % 2 + 1))
                                    src = VD[r, :].rearrange("p (n q d) -> p n q d", q=4, d=8)[:, :, head, :]
                                    dst = vb[l][r, b, :, :].rearrange("p b t c -> p (b t c)").rearrange(
                                        "p (n q c) -> p n q c", q=2, c=32)[:, :, head // 2, 8 * head:8 * head + 8]
                                    op = nc.scalar.activation(dst, src, ACT.Copy)
                                op.then_inc(sa["vb"], 1)
                            if not odd and group_exists(i, m + 1):
                                l = (m + 1) % 2
                                twice = vT[l][:, :, :, :]
                                v_in = lambda t: t.rearrange("p (b k) -> p b k", b=NB).unsqueeze(2).to_broadcast([P, NB, 2, SEQ])
                                if project:
                                    act.wait_ge(sa["kvp"], gv(i, m + 1))
                                    nc.scalar.activation(kT[l][:, :], KP, ACT.Copy).then_inc(sa["kT"], 1)
                                    nc.scalar.activation(twice, v_in(VP), ACT.Identity, bias=bv).then_inc(sa["vT"], 1)
                                else:
                                    act.wait_ge(*loaded_for(sa_cg, i, m + 1))
                                    act.wait_ge(sa["vdp"], hv(i, n + 1))
                                    nc.scalar.activation(twice, v_in(cg[l][:, :]), ACT.Copy).then_inc(sa["vT"], 1)
                            if odd and group_exists(i, m + 2):
                                act.wait_ge(ln["hTp"], gv(i, m + 2))
                                nc.scalar.activation(hT[m % 2][:, :], HP, ACT.Copy).then_inc(ln["hT"], 1)
                            if odd and project and group_exists(i, m + 1):
                                act.wait_ge(sa["qp"], gv(i, m + 1))
                                nc.scalar.activation(qT[(m + 1) % 2][:, :], QP, ACT.Identity, bias=bq).then_inc(sa["q"], 1)
                            k = n - 2
                            if int8 and not odd and group_exists(i, m - 3):
                                act.wait_ge(i8["qTp"], gv(i, m - 3))
                                nc.scalar.activation(qT8[:, :], bf(I8[:, 0:ROWS // 2]), ACT.Copy).then_inc(i8["qT"], 1)
                            if int8 and odd and group_exists(i, m - 3):
                                act.wait_ge(i8["acc"], gv(i, m - 3))
                                if group_exists(i, m - 4):
                                    act.wait_ge(i8["tmp"], gv(i, m - 4))
                                nc.scalar.activation(ac[:, :, :].rearrange("p t c -> p (t c)"), I8, ACT.Copy
                                                     ).then_inc(i8["ac"], 1)
                            if half_exists(i, k):
                                act.wait_ge(sa["av"], hv(i, k))
                                nc.scalar.activation(oT[k % 2][:, :], O, ACT.Copy).then_inc(sa["o"], 1)
                            if half_exists(i, n):
                                act.wait_ge(sa["sub"], hv(i, n))
                                nc.scalar.activation(pr[n % 2][:, :], pr[n % 2][:, :], ACT.Exp, scale=score_scale
                                                     ).then_inc(sa["exp"], 1)

                            if routed and not odd and group_exists(i, m - 4):
                                act.wait_ge(mo["ls"], gv(i, m - 4))
                                nc.scalar.activation(ex[:, :, :], ls[:, :, :], ACT.Exp).then_inc(mo["ex"], 1)

                        run_steps(act, HALVES, step, lag=int(int8 or routed or spectral))

                    @block.tensor
                    def _(pe):
                        def route(i, n):
                            m, odd = divmod(n, 2)
                            if half_exists(i, n - 1):
                                hold(pe, "pe", sa["sub"], hv(i, n - 1))
                            if not odd:
                                if group_exists(i, m - 5):
                                    pe.wait_ge(mo["ct"], gv(i, m - 5))
                                for t in range(T):
                                    op = nc.tensor.matmul(LOGITS[:, E * t:E * (t + 1)], hT[2][:, t * P:(t + 1) * P],
                                                          we[:, D:D + E], start=True, stop=True)
                                op.then_inc(mo["e"], 1)
                            else:
                                pe.wait_ge(mo["oh"], gv(i, m - 4))
                                flat = oh[:, :, :].rearrange("p t e -> p (t e)")
                                nc.tensor.matmul(COUNTS[:, 0:T * E], tri[:, :], flat, start=True, stop=True)
                                nc.tensor.matmul(COUNTS[:, T * E:2 * T * E], ones[:, :], flat, start=True, stop=True
                                                 ).then_inc(mo["c"], 1)

                        def project_output(i, k):
                            pe.wait_ge(sa["o"], hv(i, k))
                            if half_exists(i, k + 2):
                                hold(pe, "pe", sa["sub"], hv(i, k + 2))
                            for t in range(2):
                                op = nc.tensor.matmul(OUT[:, t * P:(t + 1) * P], oT[k % 2][:, t * P:(t + 1) * P],
                                                      wo[:, :], start=True, stop=True)
                            op.then_inc(sa["out"], 1)

                        def transpose_probabilities(i, k):
                            pe.wait_ge(sa["pn"], hv(i, k))
                            for c in [*range(4, 16), *range(4)]:
                                if c == 0 and routed and group_exists(i, (k + 2) // 2 - 4):
                                    route(i, k + 2)
                                if c == 0 and half_exists(i, k - 1):
                                    project_output(i, k - 1)
                                t, pair = divmod(c, 8)
                                op = nc.tensor.transpose(
                                    PTP[:, c * P:(c + 1) * P],
                                    pr[k % 2][:, :].rearrange("p (r t m c) -> p r t m c", r=Q4, t=2, m=2)[
                                        :, pair // 2, t, pair % 2, :], ident[:, :])
                            op.then_inc(sa["ptp"], 1)

                        def small_products_are_read(i, n):
                            m, odd = divmod(n, 2)
                            if half_exists(i, n + 1):
                                hold(pe, "pe", sa["vb"], hv(i, n + 1))
                            if not odd and project and group_exists(i, m + 1):
                                hold(pe, "pe", sa["vT"], gv(i, m + 1))
                            if odd and group_exists(i, m + 2):
                                hold(pe, "pe", ln["hT"], gv(i, m + 2))
                            if odd and project and group_exists(i, m + 1):
                                hold(pe, "pe", sa["q"], gv(i, m + 1))
                            if int8 and group_exists(i, m - 3):
                                hold(pe, "pe", i8["ac" if odd else "qT"], gv(i, m - 3))

                        def projection_is_read(i, n, r, t):
                            if r == 3 and t == 0 and half_exists(i, n - 3):
                                hold(pe, "pe", sa["ob"], hv(i, n - 3))
                            if routed and r == 3 and t == 0 and group_exists(i, n // 2 - 4):
                                hold(pe, "pe", mo["ct" if n % 2 else "lg"], gv(i, n // 2 - 4))

                        def scores(i, n):
                            m, half = divmod(n, 2)
                            l = m % 2
                            if half == 0:
                                hold(pe, "pe", sa["q"] if project else ln["hT"], gv(i, m))
                                hold(pe, "pe", sa["kb"], gv(i, m))
                                if mask_kind == 1:
                                    hold(pe, "pe", sa["mask"], gv(i, m))
                            if half_exists(i, n - 1):
                                hold(pe, "pe", sa["sub"], hv(i, n - 1))
                            for r in range(Q4):
                                bank = PS[:, r, :].rearrange("p (t n k) -> p t n k", t=2, n=Q4)
                                if mask_kind:
                                    if mask_kind == 1:
                                        mask = nm[l][:, 2 * half:2 * half + 2, :].unsqueeze(2)
                                    else:
                                        mask = nm[:, :].unsqueeze(1).unsqueeze(1)
                                    projection_is_read(i, n, r, 0)
                                    nc.tensor.matmul(bank, ident_bf[:, :], mask.to_broadcast([P, 2, Q4, SEQ]),
                                                     start=True, stop=False, skip_group_check=True)
                            for t in range(2):
                                for r in range(Q4):
                                    bank = PS[:, r, :].rearrange("p (t c) -> p t c", t=2)
                                    if not mask_kind:
                                        projection_is_read(i, n, r, t)
                                    for b in range(2):
                                        seq = 4 * half + 2 * t + b
                                        op = nc.tensor.matmul(
                                            bank[SEQ * b:SEQ * (b + 1), t, :],
                                            qT[l][32 * r:32 * r + 32, SEQ * seq:SEQ * (seq + 1)],
                                            kb[l][32 * r:32 * r + 32, seq, :, :].rearrange("p n k -> p (n k)"),
                                            start=(not mask_kind and t == 0), stop=True, skip_group_check=True)
                            op.then_inc(sa["scores"], 1)

                        def attend(i, k):
                            l = k // 2 % 2
                            hold(pe, "pe", sa["pt"], hv(i, k))
                            for t in range(2):
                                for b in range(2):
                                    seq = 4 * (k % 2) + 2 * t + b
                                    for pair in range(2):
                                        for r in range(Q4):
                                            op = nc.tensor.matmul(
                                                O[32 * r:32 * r + 32, t * P + b * SEQ:t * P + (b + 1) * SEQ],
                                                vb[l][:, seq, 2 * r + pair, :],
                                                pT[:, t, 2 * r + pair, b * SEQ:(b + 1) * SEQ],
                                                start=(pair == 0), stop=(pair == 1))
                            op.then_inc(sa["av"], 1)

                        def step(i, n):
                            m, odd = divmod(n, 2)
                            small_products_are_read(i, n - 1)
                            if half_exists(i, n - 2):
                                transpose_probabilities(i, n - 2)
                            else:
                                if routed and group_exists(i, m - 4):
                                    route(i, n)
                                if half_exists(i, n - 3):
                                    project_output(i, n - 3)
                            if half_exists(i, n):
                                scores(i, n)
                            if half_exists(i, n - 2):
                                hold(pe, "pe", sa["pt"], hv(i, n - 2))
                            if routed and group_exists(i, m - 3):
                                if not odd:
                                    pe.wait_ge(lnf["norm"], gv(i, m - 3))
                                    transposes(PS[:, 4, :], h[2 + (m - 3) % 2]).then_inc(mo["hTp"], 1)
                                else:
                                    for t in range(T):
                                        op = nc.tensor.matmul(PS[:, 4, t * P:(t + 1) * P], hT[2][:, t * P:(t + 1) * P],
                                                              we[:, 0:D], start=True, stop=True)
                                    op.then_inc(mo["lin"], 1)
                            if spectral and group_exists(i, m - 3):
                                if not odd:
                                    pe.wait_ge(lnf["norm"], gv(i, m - 3))
                                    transposes(PS[:, 4, :], h[2 + (m - 3) % 2]).then_inc(sf["hTp"], 1)
                                else:
                                    for t in range(T):
                                        op = nc.tensor.matmul(PS[:, 4, t * P:(t + 1) * P], hT[2][:, t * P:(t + 1) * P],
                                                              M[:, :], start=True, stop=True)
                                    op.then_inc(sf["out"], 1)
                            k = n + 1
                            if half_exists(i, k):
                                hold(pe, "pe", sa["vT"], gv(i, k // 2))
                                for b in range(4):
                                    op = nc.tensor.transpose(
                                        VD[:, b * P:(b + 1) * P],
                                        vT[k // 2 % 2][:, 4 * (k % 2) + b, :, :].rearrange("p a k -> p (a k)"), ident[:, :])
                                op.then_inc(sa["vdp"], 1)
                            if not odd and project and group_exists(i, m + 1):
                                l = (m + 1) % 2
                                pe.wait_ge(*loaded_for(sa_cg, i, m + 1))
                                nc.tensor.matmul(KP, wk[:, :], cg[l][:, :], start=True, stop=True)
                                nc.tensor.matmul(VP, wv[:, :], cg[l][:, :], start=True, stop=True).then_inc(sa["kvp"], 1)
                            if odd and group_exists(i, m + 2):
                                pe.wait_ge(ln["norm"], gv(i, m + 2))
                                transposes(HP, h[m % 2]).then_inc(ln["hTp"], 1)
                            if odd and project and group_exists(i, m + 1):
                                nc.tensor.matmul(QP, wq[:, :], hT[(m + 1) % 2][:, :], start=True, stop=True
                                                 ).then_inc(sa["qp"], 1)
                            if int8 and not odd and group_exists(i, m - 3):
                                pe.wait_ge(i8["q"], gv(i, m - 3))
                                for t in range(T):
                                    op = nc.tensor.transpose(bf(I8[:, 64 * t:64 * t + 64]), qb[:, t, :], ident_bf[:, :])
                                op.then_inc(i8["qTp"], 1)
                            if int8 and odd and group_exists(i, m - 3):
                                for t in range(T):
                                    op = nc.tensor.matmul(I8[:, t * P:(t + 1) * P], qT8[:, t * P:(t + 1) * P], wq8[:, :],
                                                          start=True, stop=True)
                                op.then_inc(i8["acc"], 1)
                            if routed and group_exists(i, m - 3):
                                hold(pe, "pe", mo["ac" if odd else "hT"], gv(i, m - 3))
                            if spectral and group_exists(i, m - 3):
                                hold(pe, "pe", sf["ac" if odd else "hT"], gv(i, m - 3))
                            if half_exists(i, n - 2):
                                attend(i, n - 2)

                        run_steps(pe, HALVES, step, lag=int(int8 or routed or spectral))


        def decoder_layer():
            dl_cg = [sem(f"dl_context{l}") for l in range(WIDE)]
            dl_lane = [sem(f"dl_lane_done{l}") for l in range(WIDE)]
            dl = {n: sem("dl_" + n) for n in (
                "xTp", "xT", "p0", "p1", "pq0", "pq1", "pv0", "pv1", "q0", "q1", "v0", "v1", "k0", "k1", "sc0", "sc1",
                "mx0", "mx1", "sub0", "sub1", "exp0", "exp1", "sum0", "sum1", "rs0", "rs1", "pn0", "pn1", "pTp0", "pTp1",
                "pT0", "pT1", "av0", "av1", "aT0", "aT1", "aTp0", "aTp1", "add0", "add1", "add2", "gm1", "gm2", "gm3",
                "gb1", "gb2", "gb3", "nb", "nTp", "nT", "w1", "f", "hid", "w2", "X")}
            norms = [ln] + [{n: sem(f"dl_{n}{k}") for n in ("bn", "var", "ve", "rstd", "norm")} for k in range(1, 5)]
            lanes = range(WIDE)
            EPS = 0.001
            SCALE = 1.0 / math.sqrt(SEQ)
            with ExitStack() as c:
                def sb(n, shape, dt=F32):
                    return c.enter_context(nc.sbuf_tensor(f"dl_{n}", shape, dt))
                w = {n: constant(f"A3_{n}") for n in ("wq1", "wk1", "wv1", "wq2", "wk2", "wv2", "w1", "w2", "b2", "gamma", "beta")}
                cg = [sb(f"cg{l}", [P, ROWS]) for l in lanes]
                qT = [sb(f"qT{l}", [P, ROWS]) for l in lanes]
                kT = [sb(f"kT{l}", [P, ROWS]) for l in lanes]
                va = [sb(f"va{l}", [P, T, D]) for l in lanes]
                pr = [sb(f"pr{l}", [P, T, SEQ]) for l in lanes]
                pT = [sb(f"pT{l}", [P, 2, P]) for l in lanes]
                aT = [sb(f"aT{l}", [P, T, 2, SEQ]) for l in lanes]
                mx = [sb(f"mx{l}", [P, T]) for l in lanes]
                sm = [sb(f"sm{l}", [P, T]) for l in lanes]
                rs = [sb(f"rs{l}", [P, T]) for l in lanes]
                n1 = [sb(f"n1{l}", [P, T, D]) for l in lanes]
                n2 = [sb(f"n2{l}", [P, T, D]) for l in lanes]
                n2b = [sb(f"n2b{l}", [P, T, D]) for l in lanes]
                n3 = n1
                nT = [sb(f"nT{l}", [P, ROWS]) for l in lanes]
                fT = [sb(f"fT{l}", [P, ROWS]) for l in lanes]
                hd = [sb(f"hd{l}", [P, ROWS]) for l in lanes]
                ORDER = (1, 0, 1, 1, 0, 1, 0, 1, 0, 0, 1, 1, 0, 1, 0, 1, 0, 1)

                def all_tiles(v):
                    return v[:, :].unsqueeze(1).to_broadcast([P, T, D])

                with nc.Block() as block:
                    @block.sync
                    def _(sp):
                        with sp.Fori(0, WIDE_STEPS) as i:
                            for l in lanes:
                                hold(sp, "sp", dl_lane[l], i + 1)
                                sp.dma_start(cg[l][:, :], ctxT[:, bass.ds(WIDE * ROWS * i + ROWS * l, ROWS)]
                                             ).then_inc(dl_cg[l], 16)

                    @block.gpsimd
                    def _(pool):
                        def rstd_of(i, k, groups):
                            for g in groups:
                                ln_rstd(pool, cv(i, g), g % WIDE, EPS if 0 < k < 4 else 1e-5, norms[k])

                        def gamma_beta(i, k, groups, rows):
                            for g in groups:
                                t = rows[g % WIDE]
                                hold(pool, "pool", norms[k]["norm"], cv(i, g))
                                nc.gpsimd.tensor_tensor(t[:, :, :], t[:, :, :], all_tiles(w["gamma"]), ALU.mult
                                                        ).then_inc(dl[f"gm{k}"], 1)
                                hold(pool, "pool", dl[f"gm{k}"], cv(i, g))
                                nc.gpsimd.tensor_tensor(t[:, :, :], t[:, :, :], all_tiles(w["beta"]), ALU.add
                                                        ).then_inc(dl[f"gb{k}"], 1)

                        def first(i, groups, k):
                            if k == 0:
                                rstd_of(i, 0, groups)
                            if k == 6:
                                rstd_of(i, 1, groups)
                            if k == 7:
                                gamma_beta(i, 1, groups, n1)

                        def second(i, groups, k):
                            if k == 3:
                                rstd_of(i, 2, groups)
                            if k == 4:
                                gamma_beta(i, 2, groups, n2)
                            if k == 5:
                                for g in groups:
                                    l = g % WIDE
                                    hold(pool, "pool", dl["gb2"], cv(i, g))
                                    nc.gpsimd.tensor_tensor(n2b[l][:, :, :], n2[l][:, :, :], all_tiles(w["b2"]), ALU.add
                                                            ).then_inc(dl["nb"], 1)
                            if k == 6:
                                rstd_of(i, 3, groups)
                            if k == 7:
                                gamma_beta(i, 3, groups, n3)
                            if k == 8:
                                rstd_of(i, 4, groups)

                        run_halves(pool, ORDER, first, second)

                    @block.vector
                    def _(dve):
                        def tiles(bank):
                            return bank.rearrange("p (t c) -> p t c", t=T)

                        def keys(i, a, groups):
                            for g in groups:
                                l = g % WIDE
                                hold(dve, "dve", dl[f"p{a}"], cv(i, g))
                                nc.vector.tensor_copy(kT[l][:, :], wide_banks(l, 0)).then_inc(dl[f"k{a}"], 1)

                        def scores_less_maxima(i, a, groups):
                            for g in groups:
                                l, v = g % WIDE, cv(i, g)
                                S = wide_banks(l, 0)[:, 0:T * SEQ].rearrange("p (n k) -> p n k", k=SEQ)
                                dve.wait_ge(dl[f"sc{a}"], v)
                                nc.vector.tensor_reduce(mx[l][:, :], S, op=ALU.max, axis=AX).then_inc(dl[f"mx{a}"], 1)
                                dve.wait_ge(dl[f"mx{a}"], v)
                                nc.vector.tensor_tensor(pr[l][:, :, :], S, mx[l][:, :].unsqueeze(2).to_broadcast([P, T, SEQ]),
                                                        ALU.subtract).then_inc(dl[f"sub{a}"], 1)

                        def probabilities(i, a, groups):
                            for g in groups:
                                l, v = g % WIDE, cv(i, g)
                                dve.wait_ge(dl[f"exp{a}"], v)
                                nc.vector.tensor_reduce(sm[l][:, :], pr[l][:, :, :], op=ALU.add, axis=AX
                                                        ).then_inc(dl[f"sum{a}"], 1)
                                dve.wait_ge(dl[f"sum{a}"], v)
                                nc.vector.reciprocal(rs[l][:, :], sm[l][:, :]).then_inc(dl[f"rs{a}"], 1)
                                dve.wait_ge(dl[f"rs{a}"], v)
                                nc.vector.tensor_tensor(pr[l][:, :, :], pr[l][:, :, :],
                                                        rs[l][:, :].unsqueeze(2).to_broadcast([P, T, SEQ]), ALU.mult
                                                        ).then_inc(dl[f"pn{a}"], 1)

                        def stats(i, k, g, rows):
                            ln_stats(dve, cv(i, g), g % WIDE, rows, norms[k])

                        def norm(i, k, groups, rows):
                            for g in groups:
                                t_ = rows[g % WIDE]
                                ln_norm(dve, cv(i, g), g % WIDE, lambda t: t_[:, t, :], lambda t: t_[:, t, :], norms[k])

                        def first(i, groups, k):
                            if k == 0:
                                for g in groups:
                                    hold(dve, "dve", dl_lane[g % WIDE], i + (g // WIDE + 1))
                                    stats(i, 0, g, lambda t: wide_row(X, i, g, t))
                            if k == 1:
                                for g in groups:
                                    ln_norm(dve, cv(i, g), g % WIDE, lambda t: wide_row(X, i, g, t),
                                            lambda t: h[g % WIDE][:, t, :], norms[0])
                            if k == 2:
                                keys(i, 0, groups)
                            if k == 3:
                                scores_less_maxima(i, 0, groups)
                            if k == 4:
                                probabilities(i, 0, groups)
                            if k == 6:
                                for g in groups:
                                    l = g % WIDE
                                    dve.wait_ge(dl["aTp0"], cv(i, g))
                                    nc.vector.tensor_tensor(n1[l][:, :, :], tiles(wide_banks(l, 0)), h[l][:, :, :], ALU.add
                                                            ).then_inc(dl["add0"], 1)
                                    hold(dve, "dve", dl["add0"], cv(i, g))
                                    stats(i, 1, g, lambda t: n1[l][:, t, :])
                            if k == 7:
                                norm(i, 1, groups, n1)

                        def second(i, groups, k):
                            if k == 0:
                                keys(i, 1, groups)
                            if k == 1:
                                scores_less_maxima(i, 1, groups)
                            if k == 2:
                                probabilities(i, 1, groups)
                            if k == 3:
                                for g in groups:
                                    l = g % WIDE
                                    dve.wait_ge(dl["gb1"], cv(i, g))
                                    dve.wait_ge(dl["aTp1"], cv(i, g))
                                    nc.vector.tensor_tensor(n2[l][:, :, :], tiles(wide_banks(l, 0)), n1[l][:, :, :], ALU.add
                                                            ).then_inc(dl["add1"], 1)
                                    hold(dve, "dve", dl["add1"], cv(i, g))
                                    stats(i, 2, g, lambda t: n2[l][:, t, :])
                            if k == 4:
                                norm(i, 2, groups, n2)
                            if k == 5:
                                for g in groups:
                                    l = g % WIDE
                                    dve.wait_ge(dl["f"], cv(i, g))
                                    nc.vector.scalar_tensor_tensor(hd[l][:, :], fT[l][:, :], 0.2, fT[l][:, :], ALU.mult,
                                                                   ALU.max).then_inc(dl["hid"], 1)
                            if k == 6:
                                for g in groups:
                                    l = g % WIDE
                                    dve.wait_ge(dl["nb"], cv(i, g))
                                    dve.wait_ge(dl["w2"], cv(i, g))
                                    nc.vector.tensor_tensor(n3[l][:, :, :], tiles(wide_banks(l, 1)), n2b[l][:, :, :], ALU.add
                                                            ).then_inc(dl["add2"], 1)
                                    hold(dve, "dve", dl["add2"], cv(i, g))
                                    stats(i, 3, g, lambda t: n3[l][:, t, :])
                            if k == 7:
                                norm(i, 3, groups, n3)
                            if k == 8:
                                for g in groups:
                                    l = g % WIDE
                                    hold(dve, "dve", dl["gb3"], cv(i, g))
                                    nc.vector.scalar_tensor_tensor(wide_rows(X, i, g), n3[l][:, :, :], 0.0, wide_rows(X, i, g),
                                                                   ALU.max, ALU.add).then_inc(dl["X"], 1)
                                    hold(dve, "dve", dl["X"], cv(i, g))
                                    stats(i, 4, g, lambda t: wide_row(X, i, g, t))
                            if k == 9:
                                for g in groups:
                                    ln_norm(dve, cv(i, g), g % WIDE, lambda t: wide_row(X, i, g, t),
                                            lambda t: wide_row(Y, i, g, t), norms[4])
                                for g in groups:
                                    hold(dve, "dve", norms[4]["norm"], cv(i, g))
                                    dve.sem_inc(dl_lane[g % WIDE], 1)

                        for lane in dl_lane:
                            dve.sem_inc(lane, 1)
                        run_halves(dve, ORDER, first, second)

                    @block.scalar
                    def _(act):
                        def copy(event, done, i, groups, dst, src):
                            for g in groups:
                                l = g % WIDE
                                act.wait_ge(dl[event], cv(i, g))
                                nc.scalar.activation(dst(l), src(l), ACT.Copy).then_inc(dl[done], 1)

                        def queries(i, a, groups):
                            copy(f"pq{a}", f"q{a}", i, groups, lambda l: qT[l][:, :], lambda l: wide_banks(l, 1))

                        def values_and_exponentials(i, a, groups):
                            copy(f"pv{a}", f"v{a}", i, groups, lambda l: va[l][:, :, :].rearrange("p t c -> p (t c)"),
                                 lambda l: wide_banks(l, 1))
                            for g in groups:
                                l = g % WIDE
                                act.wait_ge(dl[f"sub{a}"], cv(i, g))
                                nc.scalar.activation(pr[l][:, :, :], pr[l][:, :, :], ACT.Exp, scale=SCALE
                                                     ).then_inc(dl[f"exp{a}"], 1)

                        def transposed(i, a, groups):
                            copy(f"pTp{a}", f"pT{a}", i, groups, lambda l: pT[l][:, :, :].rearrange("p u c -> p (u c)"),
                                 lambda l: wide_banks(l, 1)[:, 0:2 * P])

                        def attended(i, a, groups):
                            for g in groups:
                                l = g % WIDE
                                act.wait_ge(dl[f"av{a}"], cv(i, g))
                                for x_ in range(2):
                                    op = nc.scalar.activation(aT[l][:, :, x_, :], wide_banks(l, x_)[:, 0:T * SEQ].rearrange(
                                        "p (t q) -> p t q", t=T), ACT.Copy)
                                op.then_inc(dl[f"aT{a}"], 1)

                        def first(i, groups, k):
                            if k == 1:
                                copy("xTp", "xT", i, groups, lambda l: hT[l][:, :], lambda l: wide_banks(l, 0))
                            if k == 2:
                                queries(i, 0, groups)
                            if k == 3:
                                values_and_exponentials(i, 0, groups)
                            if k == 4:
                                transposed(i, 0, groups)
                            if k == 5:
                                attended(i, 0, groups)

                        def second(i, groups, k):
                            if k == 0:
                                queries(i, 1, groups)
                            if k == 1:
                                values_and_exponentials(i, 1, groups)
                            if k == 2:
                                transposed(i, 1, groups)
                            if k == 3:
                                attended(i, 1, groups)
                            if k == 5:
                                copy("nTp", "nT", i, groups, lambda l: nT[l][:, :], lambda l: wide_banks(l, 1))
                                for g in groups:
                                    l = g % WIDE
                                    act.wait_ge(dl["w1"], cv(i, g))
                                    nc.scalar.activation(fT[l][:, :], wide_banks(l, 0), ACT.Identity, bias=column("A3_b1")
                                                         ).then_inc(dl["f"], 1)

                        run_halves(act, ORDER, first, second)

                    @block.tensor
                    def _(pe):
                        def project(i, a, groups, q_of, kv_of):
                            for g in groups:
                                l = g % WIDE
                                if a == 0:
                                    pe.wait_ge(dl["xT"], cv(i, g))
                                nc.tensor.matmul(wide_banks(l, 1), w[f"wq{a + 1}"][:, :], q_of(l), start=True, stop=True
                                                 ).then_inc(dl[f"pq{a}"], 1)
                                if a == 1:
                                    pe.wait_ge(dl["add0"], cv(i, g))
                                    pe.wait_ge(dl_cg[l], 16 * i + (16 * (g // WIDE) + 16))
                                nc.tensor.matmul(wide_banks(l, 0), w[f"wk{a + 1}"][:, :], kv_of(l), start=True, stop=True
                                                 ).then_inc(dl[f"p{a}"], 1)

                        def values_and_scores(i, a, groups, kv_of):
                            for g in groups:
                                l = g % WIDE
                                pe.wait_ge(dl[f"q{a}"], cv(i, g))
                                for t in range(T):
                                    op = nc.tensor.matmul(wide_banks(l, 1)[:, t * P:(t + 1) * P], kv_of(l)[:, t * P:(t + 1) * P],
                                                          w[f"wv{a + 1}"][:, :], start=True, stop=True)
                                op.then_inc(dl[f"pv{a}"], 1)
                            for g in groups:
                                l = g % WIDE
                                hold(pe, "pe", dl[f"k{a}"], cv(i, g))
                                if a == 0:
                                    nc.tensor.matmul(wide_banks(l, 0)[:, 0:T * SEQ].rearrange("p (n k) -> p n k", k=SEQ),
                                                     ident_bf[:, :], causal_bf[:, :].unsqueeze(1).to_broadcast([P, T, SEQ]),
                                                     start=True, stop=False, skip_group_check=True)
                                for u in range(2):
                                    for b in range(2):
                                        for x_ in range(2):
                                            s = SEQ * (4 * u + 2 * b + x_)
                                            op = nc.tensor.matmul(
                                                wide_banks(l, 0)[SEQ * b:SEQ * (b + 1),
                                                                 SEQ * (2 * u + x_):SEQ * (2 * u + x_ + 1)],
                                                qT[l][:, s:s + SEQ], kT[l][:, s:s + SEQ], start=(a == 1), stop=True,
                                                skip_group_check=True)
                                op.then_inc(dl[f"sc{a}"], 1)

                        def transpose_probabilities(i, a, groups):
                            for g in groups:
                                l = g % WIDE
                                hold(pe, "pe", dl[f"v{a}"], cv(i, g))
                                pe.wait_ge(dl[f"pn{a}"], cv(i, g))
                                for u in range(2):
                                    op = nc.tensor.transpose(wide_banks(l, 1)[:, u * P:(u + 1) * P],
                                                             pr[l][:, 2 * u:2 * u + 2, :].rearrange("p n k -> p (n k)"),
                                                             ident[:, :])
                                op.then_inc(dl[f"pTp{a}"], 1)

                        def attend(i, a, groups):
                            for g in groups:
                                l = g % WIDE
                                hold(pe, "pe", dl[f"pT{a}"], cv(i, g))
                                for t in range(T):
                                    for x_ in range(2):
                                        r = slice(SEQ * x_, SEQ * (x_ + 1))
                                        op = nc.tensor.matmul(wide_banks(l, x_)[:, SEQ * t:SEQ * (t + 1)], va[l][r, t, :],
                                                              pT[l][r, t // 2, SEQ * (t % 2):SEQ * (t % 2 + 1)],
                                                              start=True, stop=True)
                                op.then_inc(dl[f"av{a}"], 1)

                        def transpose_attended(i, a, groups):
                            for g in groups:
                                l = g % WIDE
                                pe.wait_ge(dl[f"aT{a}"], cv(i, g))
                                for t in range(T):
                                    op = nc.tensor.transpose(wide_banks(l, 0)[:, t * P:(t + 1) * P],
                                                             aT[l][:, t, :, :].rearrange("p x q -> p (x q)"), ident[:, :])
                                op.then_inc(dl[f"aTp{a}"], 1)

                        def first(i, groups, k):
                            own = lambda l: hT[l][:, :]
                            if k == 1:
                                for g in groups:
                                    pe.wait_ge(norms[0]["norm"], cv(i, g))
                                    transposes(wide_banks(g % WIDE, 0), h[g % WIDE]).then_inc(dl["xTp"], 1)
                            if k == 2:
                                project(i, 0, groups, own, own)
                            if k == 3:
                                values_and_scores(i, 0, groups, own)
                            if k == 4:
                                transpose_probabilities(i, 0, groups)
                            if k == 5:
                                attend(i, 0, groups)
                                transpose_attended(i, 0, groups)

                        def second(i, groups, k):
                            context = lambda l: cg[l][:, :]
                            if k == 0:
                                project(i, 1, groups, lambda l: aT[l][:, :, :, :].rearrange("p t x q -> p (t x q)"), context)
                            if k == 1:
                                values_and_scores(i, 1, groups, context)
                            if k == 2:
                                transpose_probabilities(i, 1, groups)
                            if k == 3:
                                attend(i, 1, groups)
                                transpose_attended(i, 1, groups)
                            if k == 5:
                                for g in groups:
                                    pe.wait_ge(dl["gb2"], cv(i, g))
                                    transposes(wide_banks(g % WIDE, 1), n2[g % WIDE]).then_inc(dl["nTp"], 1)
                                for g in groups:
                                    l = g % WIDE
                                    pe.wait_ge(dl["nT"], cv(i, g))
                                    nc.tensor.matmul(wide_banks(l, 0), w["w1"][:, :], nT[l][:, :], start=True, stop=True
                                                     ).then_inc(dl["w1"], 1)
                            if k == 6:
                                for g in groups:
                                    l = g % WIDE
                                    pe.wait_ge(dl["hid"], cv(i, g))
                                    for t in range(T):
                                        op = nc.tensor.matmul(wide_banks(l, 1)[:, t * P:(t + 1) * P],
                                                              hd[l][:, t * P:(t + 1) * P], w["w2"][:, :], start=True, stop=True)
                                    op.then_inc(dl["w2"], 1)

                        run_halves(pe, ORDER, first, second)


        NEWTON = 11

        def window_attention(lyr):
            wa = {n: sem("wa_" + n) for n in (
                "tab", "sh", "shr", "shl", "hTp", "hT", "pq", "pk", "pv", "sq", "va", "n2", "abq", "ab", "sum", "nw", "qkn", "qkTp", "qkT", "sc", "mx",
                "sub", "exp", "den", "rden", "pn", "pTp", "pT", "av", "o", "wo", "yT", "yTp", "Y")}
            lanes = range(LANES)
            pre = f"F3_{lyr}_"
            with ExitStack() as c:
                def sb(n, shape, dt=F32):
                    return c.enter_context(nc.sbuf_tensor(f"wa{lyr}_{n}", shape, dt))
                wqkv = sb("wqkv", [P, 3 * INNER])
                wo = sb("wo", [P, 4, D])
                shift = sb("shift", [P, P])
                rope = sb("rope", [P, 4 * HEAD_DIM])
                tab = sb("tab", [P, 4, HEAD_DIM])
                hs = sb("hs", [P, T, D])
                sq = sb("sq", [P, 2 * INNER])
                qk = [sb(f"qk{l}", [P, T, 2 * INNER]) for l in lanes]
                tb = [sb(f"tb{l}", [P, 2 * INNER]) for l in lanes]
                va = [sb(f"va{l}", [P, T, INNER]) for l in lanes]
                ss = [sb(f"ss{l}", [P, T, 2 * HEADS]) for l in lanes]
                y_ = [sb(f"y{l}", [P, T * 2 * HEADS]) for l in lanes]
                t_ = [sb(f"t{l}", [P, T * 2 * HEADS]) for l in lanes]
                qkT = [sb(f"qkT{l}", [P, 8, P]) for l in lanes]
                pr = [sb(f"pr{l}", [P, 8, SEQ]) for l in lanes]
                pT = sb("pT", [P, 4, P])
                mx, den, rden = sb("mx", [P, 8]), sb("den", [P, 8]), sb("rden", [P, 8])
                oT = [sb(f"oT{l}", [P, 4, ROWS]) for l in lanes]
                yT = sb("yT", [P, ROWS])
                with nc.Block() as block:
                    @block.sync
                    def _(sp):
                        load(sp, wqkv[:, :], pre + "wqkv")
                        load(sp, wo[:, :, :].rearrange("p a b -> p (a b)"), pre + "wo")
                        load(sp, shift[:, :], "shift")
                        load(sp, rope[:, :], "rope")
                        load(sp, tab[:, :, :].rearrange("p a b -> p (a b)"), pre + "scales")
                        sp.wait_ge(loaded, loads[0])
                with nc.Block() as block:
                    @block.vector
                    def _(dve):
                        flat = tab[:, :, :].rearrange("p a b -> p (a b)")
                        nc.vector.tensor_tensor(flat, flat, rope[:, :], ALU.mult).then_inc(wa["tab"], 1)
                        dve.wait_ge(wa["tab"], 1)

                UNITS = 2 * T
                AHEAD = 6
                QK = PS[:, 0:2, :].rearrange("p b c -> p (b c)")
                QKT = PS[:, 2:4, :].rearrange("p b c -> p (b c)")
                V, SC, PTP, AV = (PS[:, b, :] for b in range(4, 8))

                def uv(i, k):
                    return UNITS * i + (k + 1)

                def halves(bank0, bank1):
                    return [bank[:, 0:4 * SEQ].rearrange("p (c q) -> p c q", c=4) for bank in (bank0, bank1)]

                outputs = halves(AV, PTP)


                with nc.Block() as block:
                    @block.gpsimd
                    def _(pool):
                        def step(i, n):
                            g = n // T
                            if n % T == T - 1 and group_exists(i, g + 3):
                                if group_exists(i, g + 2):
                                    hold(pool, "pool", wa["hTp"], gv(i, g + 2))
                                nc.gpsimd.tensor_copy(hs[:, :, 0:D // 2], group_rows(Y, i, g + 3)[:, :, 0:D // 2]
                                                      ).then_inc(wa["shl"], 1)
                            k = n + AHEAD - 1
                            if tile_exists(i, k):
                                hold(pool, "pool", wa["ab"], uv(i, k))
                                q = qk[k // T % 2][:, k % T, :]
                                nc.gpsimd.tensor_tensor(q, q, tb[k % 2][:, :], ALU.add).then_inc(wa["sum"], 1)
                            k = n + 2
                            if tile_exists(i, k):
                                m = k // T
                                hold(pool, "pool", wa["nw"], 2 * NEWTON * i + NEWTON * (m + 1))
                                hold(pool, "pool", wa["sum"], uv(i, k))
                                q = qk[m % 2][:, k % T, :].rearrange("p (n d) -> p n d", d=HEAD_DIM)
                                r = y_[m % 2][:, 2 * HEADS * (k % T):2 * HEADS * (k % T + 1)].unsqueeze(2).to_broadcast(
                                    [P, 2 * HEADS, HEAD_DIM])
                                nc.gpsimd.tensor_tensor(q, q, r, ALU.mult).then_inc(wa["qkn"], 1)

                        run_steps(pool, UNITS, step)

                    @block.vector
                    def _(dve):
                        def inverse_root_step(i, m, k):
                            s = ss[m % 2][:, :, :].rearrange("p t n -> p (t n)")
                            y, t = y_[m % 2][:, :], t_[m % 2][:, :]
                            if k:
                                hold(dve, "dve", wa["nw"], 2 * NEWTON * i + (NEWTON * m + k))
                            if k == 0:
                                hold(dve, "dve", wa["n2"], uv(i, T * m + T - 1))
                                op = nc.vector.tensor_scalar(s, s, 1e-24, None, ALU.max)
                            elif k == 1:
                                op = nc.vector.tensor_scalar(y.bitcast(I32), s.bitcast(I32), -0.5, RSQRT_SEED,
                                                             ALU.mult, ALU.add)
                            elif k % 3 == 2:
                                op = nc.vector.scalar_tensor_tensor(t, y, -0.5, y, ALU.mult, ALU.mult)
                            elif k % 3 == 0:
                                op = nc.vector.tensor_tensor(t, t, s, ALU.mult)
                            else:
                                op = nc.vector.scalar_tensor_tensor(y, t, 1.5, y, ALU.add, ALU.mult)
                            op.then_inc(wa["nw"], 1)

                        def step(i, n):
                            g = n // T
                            done = [0]

                            def roots(count):
                                if n % T == 2 and group_exists(i, g + 1):
                                    for k in range(done[0], min(done[0] + count, NEWTON)):
                                        inverse_root_step(i, g + 1, k)
                                    done[0] += count

                            if n % T == T - 1 and group_exists(i, g - 1):
                                hold(dve, "dve", wa["yTp"], gv(i, g - 1))
                                nc.vector.tensor_tensor(group_rows(Y, i, g - 1), V.rearrange("p (t c) -> p t c", t=T),
                                                        group_rows(Y, i, g - 1), ALU.add).then_inc(wa["Y"], 1)
                            if tile_exists(i, n):
                                q = n % 2
                                v = uv(i, n)
                                S = SC.rearrange("p (n k) -> p n k", k=SEQ)
                                dve.wait_ge(wa["sc"], v)
                                nc.vector.tensor_reduce(mx[:, :], S, op=ALU.max, axis=AX).then_inc(wa["mx"], 1)
                                roots(1)
                                dve.wait_ge(wa["mx"], v)
                                nc.vector.tensor_tensor(pr[q][:, :, :], S, mx[:, :].unsqueeze(2).to_broadcast(
                                    [P, 8, SEQ]), ALU.subtract).then_inc(wa["sub"], 1)
                                roots(4)
                                dve.wait_ge(wa["exp"], v)
                                nc.vector.tensor_reduce(den[:, :], pr[q][:, :, :], op=ALU.add, axis=AX
                                                        ).then_inc(wa["den"], 1)
                                roots(1)
                                dve.wait_ge(wa["den"], v)
                                nc.vector.reciprocal(rden[:, :], den[:, :]).then_inc(wa["rden"], 1)
                                roots(1)
                                dve.wait_ge(wa["rden"], v)
                                nc.vector.tensor_tensor(pr[q][:, :, :], pr[q][:, :, :], rden[:, :].unsqueeze(2)
                                                        .to_broadcast([P, 8, SEQ]), ALU.mult).then_inc(wa["pn"], 1)
                            k = n + AHEAD
                            if tile_exists(i, k):
                                lane, t = k // T % 2, k % T
                                hold(dve, "dve", wa["sq"], uv(i, k))
                                roots(1)
                                nc.vector.tensor_reduce(ss[lane][:, t, :], sq[:, :].rearrange("p (n d) -> p n d", d=HEAD_DIM),
                                                        op=ALU.add, axis=AX).then_inc(wa["n2"], 1)
                                roots(1)
                                if tile_exists(i, k - 2):
                                    hold(dve, "dve", wa["sum"], uv(i, k - 2))
                                hd = HEAD_DIM // 2
                                for a, done_with in ((0, "abq"), (1, "ab")):
                                    r = slice(INNER * a, INNER * (a + 1))
                                    own, other, src = (ap[:, r].rearrange("p (h d) -> p h d", d=HEAD_DIM)
                                                       for ap in (qk[lane][:, t, :], tb[k % 2][:, :], QK))
                                    nc.vector.tensor_tensor(own, src, tab[:, a:a + 1, :].to_broadcast([P, HEADS, HEAD_DIM]),
                                                            ALU.mult)
                                    for lo, hi in ((0, hd), (hd, 0)):
                                        op = nc.vector.tensor_tensor(
                                            other[:, :, lo:lo + hd], src[:, :, hi:hi + hd],
                                            tab[:, 2 + a:3 + a, lo:lo + hd].to_broadcast([P, HEADS, hd]), ALU.mult)
                                    op.then_inc(wa[done_with], 1)
                                    roots(1)
                            roots(NEWTON)

                        run_steps(dve, UNITS, step)

                    @block.scalar
                    def _(act):
                        def step(i, n):
                            g = n // T
                            if tile_exists(i, n - 1):
                                act.wait_ge(wa["pTp"], uv(i, n - 1))
                                nc.scalar.activation(pT[:, :, :].rearrange("p c q -> p (c q)"), PTP, ACT.Copy
                                                     ).then_inc(wa["pT"], 1)
                            if tile_exists(i, n):
                                act.wait_ge(wa["sub"], uv(i, n))
                                nc.scalar.activation(pr[n % 2][:, :, :], pr[n % 2][:, :, :], ACT.Exp).then_inc(wa["exp"], 1)
                            k = n + AHEAD
                            if tile_exists(i, k):
                                if tile_exists(i, k - 1):
                                    act.wait_ge(wa["n2"], uv(i, k - 1))
                                act.wait_ge(wa["pq"], uv(i, k))
                                nc.scalar.activation(sq[:, 0:INNER], QK[:, 0:INNER], ACT.Square)
                                act.wait_ge(wa["pk"], uv(i, k))
                                nc.scalar.activation(sq[:, INNER:2 * INNER], QK[:, INNER:2 * INNER], ACT.Square
                                                     ).then_inc(wa["sq"], 1)
                                act.wait_ge(wa["pv"], uv(i, k))
                                nc.scalar.activation(va[k // T % 2][:, k % T, :], V, ACT.Copy).then_inc(wa["va"], 1)
                            if tile_exists(i, n + 1):
                                act.wait_ge(wa["qkTp"], uv(i, n + 1))
                                nc.scalar.activation(qkT[(n + 1) % 2][:, :, :].rearrange("p c q -> p (c q)"), QKT,
                                                     ACT.Copy).then_inc(wa["qkT"], 1)
                            k = n - 1
                            if tile_exists(i, k):
                                act.wait_ge(wa["av"], uv(i, k))
                                for b, o in enumerate(outputs):
                                    s = P * (k % T) + SEQ * b
                                    op = nc.scalar.activation(oT[k // T % 2][:, :, s:s + SEQ], o, ACT.Copy)
                                op.then_inc(wa["o"], 1)
                            if n % T == 0 and group_exists(i, g + 2):
                                act.wait_ge(wa["hTp"], gv(i, g + 2))
                                nc.scalar.activation(hT[g % 2][:, :], V, ACT.Copy).then_inc(wa["hT"], 1)
                            if n % T == 1 and group_exists(i, g - 1):
                                act.wait_ge(wa["wo"], gv(i, g - 1))
                                nc.scalar.activation(yT[:, :], V, ACT.Copy).then_inc(wa["yT"], 1)
                            if n % T == 3 and group_exists(i, g + 3):
                                act.wait_ge(wa["sh"], gv(i, g + 3))
                                nc.scalar.activation(hs[:, :, D // 2:D], V[:, 0:T * D // 2].rearrange("p (t c) -> p t c", t=T),
                                                     ACT.Copy).then_inc(wa["shr"], 1)

                        run_steps(act, UNITS, step)

                    @block.tensor
                    def _(pe):
                        def score(i, n):
                            q = n % 2
                            if tile_exists(i, n - 1):
                                pe.wait_ge(wa["sub"], uv(i, n - 1))
                            pe.wait_ge(wa["qkT"], uv(i, n))
                            nc.tensor.matmul(SC.rearrange("p (n k) -> p n k", k=SEQ), ident_bf[:, :],
                                             causal_bf[:, :].unsqueeze(1).to_broadcast([P, 8, SEQ]),
                                             start=True, stop=False, skip_group_check=True)
                            for k in range(4):
                                for b in range(2):
                                    for hh in range(2):
                                        r = slice(SEQ * hh, SEQ * (hh + 1))
                                        s = slice(SEQ * b, SEQ * (b + 1))
                                        op = nc.tensor.matmul(
                                            SC[r, SEQ * (2 * k + b):SEQ * (2 * k + b + 1)],
                                            qkT[q][r, k, s], qkT[q][r, 4 + k, s], start=False, stop=True,
                                            skip_group_check=True)
                            op.then_inc(wa["sc"], 1)

                        def project_tile(i, n):
                            k = n + AHEAD
                            t = k % T
                            if t == 0:
                                pe.wait_ge(wa["hT"], gv(i, k // T))
                            for j, (read, done_with) in enumerate((("abq", "pq"), ("ab", "pk"), ("va", "pv"))):
                                if tile_exists(i, k - 1):
                                    pe.wait_ge(wa[read], uv(i, k - 1))
                                if j == 2:
                                    g, last_use = divmod(n - 1, T)
                                    name, m = (("hT", g + 2), ("yT", g - 1), ("Y", g - 1), ("shr", g + 3))[last_use]
                                    if group_exists(i, m):
                                        pe.wait_ge(wa[name], gv(i, m))
                                op = nc.tensor.matmul(QK[:, j * INNER:(j + 1) * INNER] if j < 2 else V,
                                                      hT[k // T % 2][:, t * P:(t + 1) * P],
                                                      wqkv[:, j * INNER:(j + 1) * INNER], start=True, stop=True)
                                op.then_inc(wa[done_with], 1)

                        def transpose_probabilities(i, k):
                            pe.wait_ge(wa["pn"], uv(i, k))
                            if tile_exists(i, k - 1):
                                pe.wait_ge(wa["o"], uv(i, k - 1))
                            for c in range(4):
                                op = nc.tensor.transpose(PTP[:, c * P:(c + 1) * P],
                                                         pr[k % 2][:, 2 * c:2 * c + 2, :].rearrange("p n k -> p (n k)"),
                                                         ident[:, :])
                            op.then_inc(wa["pTp"], 1)

                        def transpose_heads(i, k):
                            pe.wait_ge(wa["qkn"], uv(i, k))
                            for c in range(8):
                                op = nc.tensor.transpose(QKT[:, c * P:(c + 1) * P],
                                                         qk[k // T % 2][:, k % T, c * P:(c + 1) * P], ident[:, :])
                            op.then_inc(wa["qkTp"], 1)

                        def attend(i, n):
                            hold(pe, "pe", wa["pT"], uv(i, n))
                            for k in range(4):
                                for b in range(2):
                                    for hh in range(2):
                                        s = slice(SEQ * b, SEQ * (b + 1))
                                        head = 2 * k + hh
                                        op = nc.tensor.matmul(
                                            outputs[b][SEQ * hh:SEQ * (hh + 1), k, :],
                                            va[n // T % 2][s, n % T, HEAD_DIM * head:HEAD_DIM * (head + 1)],
                                            pT[s, k, SEQ * hh:SEQ * (hh + 1)], start=True, stop=True)
                            op.then_inc(wa["av"], 1)

                        def step(i, n):
                            g = n // T
                            if tile_exists(i, n):
                                score(i, n)
                            if tile_exists(i, n - 1):
                                transpose_probabilities(i, n - 1)
                            if tile_exists(i, n + AHEAD):
                                project_tile(i, n)
                            if tile_exists(i, n + 1):
                                transpose_heads(i, n + 1)
                            if tile_exists(i, n - 1):
                                attend(i, n - 1)
                            if tile_exists(i, n + AHEAD):
                                pe.wait_ge(wa["va"], uv(i, n + AHEAD))
                            if n % T == 0 and group_exists(i, g + 2):
                                hold(pe, "pe", wa["shl"], gv(i, g + 2))
                                pe.wait_ge(wa["shr"], gv(i, g + 2))
                                transposes(V, hs).then_inc(wa["hTp"], 1)
                            if n % T == 1 and group_exists(i, g - 1):
                                hold(pe, "pe", wa["o"], uv(i, T * g - 1))
                                for k in range(4):
                                    op = nc.tensor.matmul(V, wo[:, k, :], oT[(g - 1) % 2][:, k, :], start=(k == 0),
                                                          stop=(k == 3))
                                op.then_inc(wa["wo"], 1)
                            if n % T == 2 and group_exists(i, g - 1):
                                pe.wait_ge(wa["yT"], gv(i, g - 1))
                                for t in range(T):
                                    op = nc.tensor.transpose(V[:, t * P:(t + 1) * P], yT[:, t * P:(t + 1) * P], ident[:, :])
                                op.then_inc(wa["yTp"], 1)
                            if n % T == 3 and group_exists(i, g + 3):
                                if group_exists(i, g - 1):
                                    pe.wait_ge(wa["Y"], gv(i, g - 1))
                                nc.tensor.matmul(V[:, 0:T * D // 2].rearrange("p (t c) -> p t c", t=T), shift[:, :],
                                                 group_rows(Y, i, g + 3)[:, :, D // 2:D], start=True, stop=True
                                                 ).then_inc(wa["sh"], 1)

                        run_steps(pe, UNITS, step)

        def gated_ffn(lyr, last):
            stored = [sem(f"stored{l}") for l in range(WIDE)]
            gf_lane = [sem(f"gf_lane_done{l}") for l in range(WIDE)]
            gf = {n: sem("gf_" + n) for n in ["sh", "shr", "shl", "hTp", "hT", "w2", "yT", "yTp", "add"] + [
                f"{n}{k}" for n in ("ag", "gl", "u") for k in range(NHC)]}
            lanes = range(WIDE)
            pre = f"F3_{lyr}_"
            with ExitStack() as c:
                def sb(n, shape, dt=F32):
                    return c.enter_context(nc.sbuf_tensor(f"gf{lyr}_{n}", shape, dt))
                w1 = sb("w1", [P, 2 * HID])
                w2 = sb("w2", [P, NHC, D])
                shift = sb("shift", [P, P])
                hs = [sb(f"hs{l}", [P, T, D]) for l in lanes]
                gl = [[sb(f"gl{l}{k}", [P, ROWS]) for k in range(NHC)] for l in lanes]
                uT = [[sb(f"uT{l}{k}", [P, ROWS]) for k in range(NHC)] for l in lanes]
                yT = [sb(f"yT{l}", [P, ROWS]) for l in lanes]
                xo = [sb(f"xo{l}", [P, T, D]) for l in lanes]
                with nc.Block() as block:
                    @block.sync
                    def _(sp):
                        load(sp, w1[:, :], pre + "w1")
                        load(sp, w2[:, :, :].rearrange("p a b -> p (a b)"), pre + "w2")
                        load(sp, shift[:, :], "shift")
                        sp.wait_ge(loaded, loads[0])

                ORDER = (1, 1, 1, 0, 0, 1, 0, 1)

                with nc.Block() as block:
                    if last:
                        @block.sync
                        def _(sp):
                            for l in lanes:
                                sp.sem_inc(stored[l], 16)
                            with sp.Fori(0, WIDE_STEPS) as i:
                                for l in lanes:
                                    hold(sp, "sp", gf_lane[l], i + 2)
                                    sp.dma_start(out[bass.ds(WIDE * ROWS * i + ROWS * l, ROWS), :].rearrange(
                                        "(t p) c -> p t c", p=P), xo[l][:, :, :]).then_inc(stored[l], 16)
                            for l in lanes:
                                sp.wait_ge(stored[l], 16 * (WIDE_STEPS + 1))

                    @block.gpsimd
                    def _(pool):
                        def first(i, groups, k):
                            if k == 0:
                                for g in groups:
                                    l = g % WIDE
                                    hold(pool, "pool", gf_lane[l], i + (g // WIDE + 1))
                                    nc.gpsimd.tensor_copy(hs[l][:, :, 0:D // 2], wide_rows(Y, i, g)[:, :, 0:D // 2]
                                                          ).then_inc(gf["shl"], 1)
                            if k == 1:
                                for g in groups:
                                    ln_rstd(pool, cv(i, g), g % WIDE, 1e-5)

                        run_halves(pool, ORDER, first, lambda i, groups, k: None)

                    @block.vector
                    def _(dve):
                        def first(i, groups, k):
                            for g in groups:
                                l = g % WIDE
                                if k == 1:
                                    hold(dve, "dve", gf["shl"], cv(i, g))
                                    hold(dve, "dve", gf["shr"], cv(i, g))
                                    ln_stats(dve, cv(i, g), l, lambda t: hs[l][:, t, :])
                                if k == 2:
                                    ln_norm(dve, cv(i, g), l, lambda t: hs[l][:, t, :], lambda t: h[l][:, t, :])

                        def second(i, groups, k):
                            for g in groups:
                                l, v = g % WIDE, cv(i, g)
                                if k < NHC:
                                    m = HID_CHUNKS[k][1]
                                    hold(dve, "dve", gf[f"gl{k}"], v)
                                    nc.vector.scalar_tensor_tensor(uT[l][k][0:m, :], wide_banks(l, 0)[0:m, :],
                                                                   column(pre + "b1", k)[0:m], gl[l][k][0:m, :],
                                                                   ALU.add, ALU.mult).then_inc(gf[f"u{k}"], 1)
                                if k == NHC + 1:
                                    hold(dve, "dve", gf["yTp"], v)
                                    y = wide_banks(l, 1).rearrange("p (t c) -> p t c", t=T)
                                    if not last:
                                        nc.vector.tensor_tensor(wide_rows(Y, i, g), y, wide_rows(Y, i, g), ALU.add
                                                                ).then_inc(gf_lane[l], 1)
                                    else:
                                        hold(dve, "dve", stored[l], 16 * i + 16)
                                        nc.vector.tensor_tensor(xo[l][:, :, :], y, wide_rows(Y, i, g), ALU.add
                                                                ).then_inc(gf["add"], 1)
                                        hold(dve, "dve", gf["add"], v)
                                        nc.vector.tensor_tensor(xo[l][:, :, :], xo[l][:, :, :], wide_rows(X, i, g), ALU.add
                                                                ).then_inc(gf_lane[l], 1)

                        for lane in gf_lane:
                            dve.sem_inc(lane, 1)
                        run_halves(dve, ORDER, first, second)

                    @block.scalar
                    def _(act):
                        def first(i, groups, k):
                            for g in groups:
                                l, v = g % WIDE, cv(i, g)
                                if k == 0:
                                    act.wait_ge(gf["sh"], v)
                                    nc.scalar.activation(hs[l][:, :, D // 2:D],
                                                         wide_banks(l, 0)[:, 0:T * D // 2].rearrange("p (t c) -> p t c", t=T),
                                                         ACT.Copy).then_inc(gf["shr"], 1)
                                if k == 2:
                                    act.wait_ge(gf["hTp"], v)
                                    nc.scalar.activation(hT[l][:, :], wide_banks(l, 1), ACT.Identity,
                                                         scale=column(pre + "lg"), bias=column(pre + "lb")
                                                         ).then_inc(gf["hT"], 1)

                        def second(i, groups, k):
                            for g in groups:
                                l, v = g % WIDE, cv(i, g)
                                if k < NHC:
                                    m = HID_CHUNKS[k][1]
                                    act.wait_ge(gf[f"ag{k}"], v)
                                    nc.scalar.activation(gl[l][k][0:m, :], wide_banks(l, 1)[0:m, :], ACT.Gelu,
                                                         bias=column(pre + "b1", NHC + k)[0:m]).then_inc(gf[f"gl{k}"], 1)
                                if k == NHC:
                                    act.wait_ge(gf["w2"], v)
                                    nc.scalar.activation(yT[l][:, :], wide_banks(l, 0), ACT.Identity,
                                                         bias=column(pre + "b2")).then_inc(gf["yT"], 1)

                        run_halves(act, ORDER, first, second)

                    @block.tensor
                    def _(pe):
                        def first(i, groups, k):
                            for g in groups:
                                l, v = g % WIDE, cv(i, g)
                                if k == 0:
                                    hold(pe, "pe", gf_lane[l], i + (g // WIDE + 1))
                                    nc.tensor.matmul(wide_banks(l, 0)[:, 0:T * D // 2].rearrange("p (t c) -> p t c", t=T),
                                                     shift[:, :], wide_rows(Y, i, g)[:, :, D // 2:D], start=True, stop=True
                                                     ).then_inc(gf["sh"], 1)
                                if k == 2:
                                    pe.wait_ge(ln["norm"], v)
                                    transposes(wide_banks(l, 1), h[l]).then_inc(gf["hTp"], 1)

                        def second(i, groups, k):
                            for g in groups:
                                l, v = g % WIDE, cv(i, g)
                                if k < NHC:
                                    at, m = HID_CHUNKS[k]
                                    if k == 0:
                                        pe.wait_ge(gf["hT"], v)
                                    else:
                                        pe.wait_ge(gf[f"u{k - 1}"], v)
                                    for j in range(2):
                                        op = nc.tensor.matmul(wide_banks(l, j)[0:m, :], w1[:, j * HID + at:j * HID + at + m],
                                                              hT[l][:, :], start=True, stop=True)
                                    op.then_inc(gf[f"ag{k}"], 1)
                                if k == NHC:
                                    pe.wait_ge(gf[f"u{NHC - 1}"], v)
                                    for c_, (at, m) in enumerate(HID_CHUNKS):
                                        op = nc.tensor.matmul(wide_banks(l, 0), w2[0:m, c_, :], uT[l][c_][0:m, :],
                                                              start=(c_ == 0), stop=(c_ == NHC - 1))
                                    op.then_inc(gf["w2"], 1)
                                if k == NHC + 1:
                                    pe.wait_ge(gf["yT"], v)
                                    for t in range(T):
                                        op = nc.tensor.transpose(wide_banks(l, 1)[:, t * P:(t + 1) * P],
                                                                 yT[l][:, t * P:(t + 1) * P], ident[:, :])
                                    op.then_inc(gf["yTp"], 1)

                        run_halves(pe, ORDER, first, second)

        stages = [
            lambda: small_attention("A0", False, False, 1.0 / math.sqrt(SMALL_DIM), 0, int8=True),
            lambda: small_attention("A1", True, False, 1.0 / math.sqrt(D), 1, routed=True),
            lambda: small_attention("A2", True, True, 1.0 / math.sqrt(SMALL_DIM), 2, spectral=True),
            decoder_layer]
        for stage in stages:
            run_stage(stage)
        early_stages.close()
        for lyr in range(DEPTH):
            run_stage(lambda: window_attention(lyr))
            run_stage(lambda: gated_ffn(lyr, lyr == DEPTH - 1))


def host_layout(inputs):
    def rep(v):
        v = np.asarray(v, np.float32)
        return np.broadcast_to(v[None, :], (P, v.shape[0]))

    def block_diagonal(w):
        out = np.zeros((D, D), np.float32)
        for n in range(SMALL_HEADS):
            out[8 * n:8 * n + 8, 8 * n:8 * n + 8] = w
        return out

    p = np.arange(P)
    angle = 2 * np.pi * ((p[:, None] * p[None, :]) % D) / D
    half = np.arange(0, HEAD_DIM, 2, dtype=np.float32)
    inv = (1.0 / 10000.0 ** (half / HEAD_DIM)).astype(np.float32)
    n = (p % SEQ).astype(np.float32)
    freq = (n[:, None] * inv[None, :]).astype(np.float32)
    base = ((half + 0.4 * HEAD_DIM) / (1.4 * HEAD_DIM)).astype(np.float32)
    scale = (base[None, :] ** ((n[:, None] - SEQ // 2) / 32.0).astype(np.float32)).astype(np.float32)
    cos, sin = np.cos(freq), np.sin(freq)
    two = lambda a, b: np.concatenate([a, b], axis=1)
    k = {
        "ident": np.eye(P), "ones": np.ones((P, P)), "tri": p[:, None] <= p[None, :],
        "shift": (p[:, None] + 1 == p[None, :]) & (p[None, :] % SEQ != 0),
        "causal": np.where(np.arange(SEQ)[None, :] > (p % SEQ)[:, None], MASKED, 0.0),
        "head_cols": ((p // 8) % 4)[:, None] == np.arange(4)[None, :],
        "tie": np.broadcast_to((EXPERTS - np.arange(EXPERTS))[None, :], (P, EXPERTS)),
        "dft_cos": np.cos(angle), "dft_sin": np.sin(angle),
        "rope": np.concatenate([two(cos, cos) * two(scale, scale) * 8, two(cos, cos) / two(scale, scale),
                                two(-sin, sin) * two(scale, scale) * 8, two(-sin, sin) / two(scale, scale)], axis=1),
    }
    i = inputs
    w = {
        "A0_wo": i["L0_xattn_w_proj"].T, "A0_bo": rep(i["L0_xattn_b_proj"]), "F0_rhsT": i["L0_ffn_rhs"].T,
        "A1_wq": block_diagonal(i["L1_xattn_Wq"].T), "A1_wk": block_diagonal(i["L1_xattn_Wk"].T),
        "A1_wv": block_diagonal(i["L1_xattn_Wv"].T), "A1_wo": i["L1_xattn_Wo"].T, "A1_bo": rep(i["L1_xattn_bo"]),
        "F1_we": np.concatenate([i["L1_ffn_We"], i["L1_ffn_Wg"]], axis=1), "F1_be": rep(i["L1_ffn_be"]),
        "A2_wq": i["L2_xattn_Wq"], "A2_wk": i["L2_xattn_Wk"], "A2_wv": i["L2_xattn_Wv"], "A2_wo": i["L2_xattn_Wo"],
        "A2_bo": rep(i["L2_xattn_bo"]),
        "F2_wr": i["L2_ffn_w_freq_real"], "F2_wi": i["L2_ffn_w_freq_imag"], "F2_bias": rep(i["L2_ffn_bias"]),
        "A3_b2": rep(i["L3_xattn_b2"]), "A3_gamma": rep(i["L3_xattn_gamma"]),
        "A3_beta": rep(i["L3_xattn_beta"]), "A3_w1": i["L3_xattn_W1"], "A3_w2": i["L3_xattn_W2"],
    }
    for m in ("q1", "k1", "v1", "q2", "k2", "v2"):
        w["A3_w" + m] = i["L3_xattn_W" + m]
    cols = {"A2_bq": i["L2_xattn_bq"], "A2_bk": i["L2_xattn_bk"], "A2_bv": i["L2_xattn_bv"], "A3_b1": i["L3_xattn_b1"]}
    for l in range(2):
        f = f"F3_{l}_"
        qs, ks = i["L3_ffn_q_scale"][l], i["L3_ffn_k_scale"][l]
        hd = HEAD_DIM // 2
        swap = lambda v: np.concatenate([v[hd:], v[:hd]])
        w[f + "wqkv"] = i["L3_ffn_wqkv"][l]
        w[f + "scales"] = rep(np.concatenate([qs, ks, swap(qs), swap(ks)]))
        w[f + "wo"] = i["L3_ffn_wo"][l].reshape(4, P, D).transpose(1, 0, 2).reshape(P, 4 * D)
        cols[f + "lg"], cols[f + "lb"], cols[f + "b2"] = i["L3_ffn_ln_g"][l], i["L3_ffn_ln_b"][l], i["L3_ffn_b2"][l]
        w[f + "w1"] = i["L3_ffn_w1"][l]
        b1, w2 = np.zeros((P, 2 * NHC), np.float32), np.zeros((P, NHC, D), np.float32)
        for c, (at, m) in enumerate(HID_CHUNKS):
            b1[:m, c] = i["L3_ffn_b1"][l][at:at + m]
            b1[:m, NHC + c] = i["L3_ffn_b1"][l][HID + at:HID + at + m]
            w2[:m, c] = i["L3_ffn_w2"][l][at:at + m]
        for c in range(2 * NHC):
            cols[f"{f}b1{c}"] = b1[:, c]
        w[f + "w2"] = w2.reshape(P, NHC * D)
    w["columns"] = np.stack([np.asarray(cols[n], np.float32) for n in COLUMNS], axis=1)
    out = np.zeros((P, WEIGHT_COLS), np.float32)
    for name, n in LAYOUT:
        a = OFFSET[name][0]
        out[:, a:a + n] = w[name] if name in w else k[name]
    return out


def kernel(**inputs):
    from concourse import bacc
    from concourse.bass_utils import run_bass_kernel_spmd

    inputs = {n: np.asarray(v) for n, v in inputs.items()}
    tokens = BATCH * SEQ
    arrays = {
        "x_rows": np.ascontiguousarray(inputs["x"].reshape(tokens, D)),
        "ctx_t": np.ascontiguousarray(inputs["ctx_1024"].reshape(tokens, D).T),
        "mask_batch": np.ascontiguousarray(inputs["mask_Bx1xSxS2_ik1"].reshape(tokens, SEQ)),
        "mask_all": np.ascontiguousarray(inputs["mask_1x1xSxS2_if1"].reshape(SEQ, SEQ)),
        "weights": host_layout(inputs),
    }
    nc = bacc.Bacc("TRN2", target_bir_lowering=False, num_devices=1)
    args = [nc.dram_tensor(n, a.shape, mybir.dt.from_np(a.dtype), kind="ExternalInput").ap() for n, a in arrays.items()]
    out = nc.dram_tensor("y_rows", (tokens, D), F32, kind="ExternalOutput").ap()
    transformer_program(nc, *args, out)
    r = run_bass_kernel_spmd(nc, [arrays], core_ids=[0])
    return r.results[0]["y_rows"].reshape(BATCH, SEQ, D)
```
